# Optimizing a Trainium2 kernel written in Bass

```python
import numpy as np
import jax
import jax.numpy as jnp

def _softmax(x, axis=-1):
    return jax.nn.softmax(x, axis=axis)

def _gelu(x):
    return jax.nn.gelu(x, approximate=True)

def _silu(x):
    return jax.nn.silu(x)

def _sigmoid(x):
    return jax.nn.sigmoid(x)

def _layernorm(x, axis=-1, eps=1e-05):
    m = jnp.mean(x, axis=axis, keepdims=True)
    v = jnp.var(x, axis=axis, keepdims=True)
    return (x - m) / jnp.sqrt(v + eps)

def _scatter_add(tgt, idx, src, axis=0):
    return tgt.at[idx].add(src)

def _segment_sum(src, seg, n):
    return jax.ops.segment_sum(src, seg, n)
kernel_name = 'mk_xattn_seq_d4_seqx_r8_d93389'

def setup_inputs(seed: int=0):
    np.random.seed(seed)
    _w = jnp.asarray

    def _rec_inputs():
        import jax
        import jax.numpy as jnp
        _rk = jax.random.key(seed)
        x = -0.0003929 + 0.9999 * jax.random.normal(jax.random.fold_in(_rk, 1), (32, 64, 256), jnp.float32)
        _lenS = 64 - jax.random.randint(jax.random.fold_in(_rk, 7), (32,), 0, max(1, 64 // 4) + 1, jnp.int32)
        _lenS2 = 64 - jax.random.randint(jax.random.fold_in(_rk, 8), (32,), 0, max(1, 64 // 4) + 1, jnp.int32)
        _ctx_1024P = jax.random.normal(jax.random.fold_in(_rk, 11), (32, 16, 128), jnp.float32)
        _ctx_1024c = jax.random.dirichlet(jax.random.fold_in(_rk, 511), 0.3 * jnp.ones((16,), jnp.float32), (32, 64))
        _ctx_1024t = jnp.einsum('bsk,bkd->bsd', _ctx_1024c, _ctx_1024P)
        _ctx_1024t = _ctx_1024t * jax.lax.rsqrt(jnp.mean(jnp.square(_ctx_1024t)) + 1e-12) * 0.953939
        ctx_1024 = 0.00191187 + 0.999416 * (_ctx_1024t + 0.3 * jax.random.normal(jax.random.fold_in(_rk, 611), (32, 64, 128), jnp.float32))
        pos_1xS = jnp.broadcast_to(jnp.arange(64, dtype=jnp.int32), (1, 64))
        _validS = jnp.arange(64)[None, :] < _lenS[:, None]
        _validS2 = jnp.arange(64)[None, :] < _lenS2[:, None]
        _causal = jnp.tril(jnp.ones((64, 64), dtype=bool))
        mask_BxS2_bk0 = jnp.logical_not(jnp.broadcast_to(_validS2[:, :], (32, 64)))
        mask_BxS_ik0 = jnp.where(jnp.broadcast_to(_validS[:, :], (32, 64)), 0, 1).astype(jnp.int32)
        return (x, ctx_1024, pos_1xS, mask_BxS2_bk0, mask_BxS_ik0)
    x, ctx_1024, pos_1xS, mask_BxS2_bk0, mask_BxS_ik0 = _rec_inputs()

    def _L0_xattn_setup():
        import jax, jax.numpy as jnp
        import numpy as np
        DIM = 256
        DIM_MEDIA = 128
        HEADS = 16
        DIM_HEAD = 64
        INNER = HEADS * DIM_HEAD
        FF_INNER = 4 * DIM
        B, N_TOK, N_LAT = (4, 256, 64)
        EPS = 1e-05

        def layernorm(x, g, b):
            mu = jnp.mean(x, axis=-1, keepdims=True)
            var = jnp.var(x, axis=-1, keepdims=True)
            return (x - mu) * jax.lax.rsqrt(var + EPS) * g + b
        key = jax.random.key(seed)
        ks = jax.random.split(key, 12)
        x = jax.random.normal(ks[0], (B, N_TOK, DIM), dtype=jnp.float32)
        media = jax.random.normal(ks[1], (B, N_LAT, DIM_MEDIA), dtype=jnp.float32)
        media_mask = jax.random.randint(ks[2], (B, N_LAT), 0, 2).astype(bool)
        media_mask = media_mask.at[:, 0].set(True)
        s = lambda d: 1.0 / np.sqrt(d)
        Wq = jax.random.normal(ks[3], (DIM, INNER), dtype=jnp.float32) * s(DIM)
        Wkv = jax.random.normal(ks[4], (DIM_MEDIA, 2 * INNER), dtype=jnp.float32) * s(DIM_MEDIA)
        Wo = jax.random.normal(ks[5], (INNER, DIM), dtype=jnp.float32) * s(INNER)
        W1 = jax.random.normal(ks[6], (DIM, FF_INNER), dtype=jnp.float32) * s(DIM)
        W2 = jax.random.normal(ks[7], (FF_INNER, DIM), dtype=jnp.float32) * s(FF_INNER)
        return {'x': x, 'media': media, 'media_mask': media_mask, 'ln_q_g': jnp.ones((DIM,), jnp.float32), 'ln_q_b': jnp.zeros((DIM,), jnp.float32), 'Wq': Wq, 'Wkv': Wkv, 'Wo': Wo, 'attn_gate': jax.random.normal(ks[8], (1,), jnp.float32) * 0.5, 'ln_ff_g': jnp.ones((DIM,), jnp.float32), 'ln_ff_b': jnp.zeros((DIM,), jnp.float32), 'W1': W1, 'W2': W2, 'ff_gate': jax.random.normal(ks[9], (1,), jnp.float32) * 0.5}
    _L0_xattn_all = _L0_xattn_setup()
    _L0_xattn_in = {k: v for k, v in _L0_xattn_all.items() if k in ('ln_q_g', 'ln_q_b', 'Wq', 'Wkv', 'Wo', 'attn_gate', 'ln_ff_g', 'ln_ff_b', 'W1', 'W2', 'ff_gate')}
    del _L0_xattn_all

    def _L1_xattn_setup():
        import jax, jax.numpy as jnp
        import numpy as np
        EPS = 1e-06

        def _rmsnorm(x, w):
            var = jnp.mean(jnp.square(x), axis=-1, keepdims=True)
            return x * jax.lax.rsqrt(var + EPS) * w
        key = jax.random.key(seed)
        ks = jax.random.split(key, 6)
        B, N, M = (4, 512, 256)
        d_model, memory_dim = (256, 128)
        hidden_states = jax.random.normal(ks[0], (B, N, d_model), dtype=jnp.float32)
        memory = jax.random.normal(ks[1], (B, M, memory_dim), dtype=jnp.float32)
        W_mem = jax.random.normal(ks[2], (d_model, memory_dim), dtype=jnp.float32) / np.sqrt(memory_dim)
        W_gate = jax.random.normal(ks[3], (d_model, 2 * d_model), dtype=jnp.float32) / np.sqrt(2 * d_model)
        b_gate = jax.random.normal(ks[4], (d_model,), dtype=jnp.float32) * 0.01
        norm_w = jnp.ones((d_model,), dtype=jnp.float32)
        return {'hidden_states': hidden_states, 'memory': memory, 'W_mem': W_mem, 'W_gate': W_gate, 'b_gate': b_gate, 'norm_w': norm_w}
    _L1_xattn_all = _L1_xattn_setup()
    _L1_xattn_in = {k: v for k, v in _L1_xattn_all.items() if k in ('W_mem', 'W_gate', 'b_gate', 'norm_w')}
    del _L1_xattn_all

    def _L2_xattn_setup():
        import jax, jax.numpy as jnp
        import numpy as np
        H = 256
        NH = 16
        HD = H // NH
        CH = 128
        CC = 128
        CHD = CC // NH
        I = 688
        B = 2
        L = 256
        LE = 128
        EPS = 1e-06

        def rms_norm(x, w):
            xf = x.astype(jnp.float32)
            var = jnp.mean(xf * xf, axis=-1, keepdims=True)
            return (w * (xf * jax.lax.rsqrt(var + EPS))).astype(x.dtype)

        def expert_mask(tt):
            vm = jnp.zeros(tt.shape, dtype=bool)
            vm = vm.at[:, :-1].set((tt[:, :-1] == 1) & (tt[:, 1:] == 1))
            return vm

        def rotate_half(x):
            d = x.shape[-1] // 2
            return jnp.concatenate([-x[..., d:], x[..., :d]], axis=-1)

        def apply_rotary(q, k, position_ids, seq_len):
            inv = 1.0 / 10000.0 ** (jnp.arange(0, HD, 2, dtype=jnp.float32) / HD)
            t = jnp.arange(seq_len, dtype=jnp.float32)
            freqs = jnp.outer(t, inv)
            emb = jnp.concatenate([freqs, freqs], axis=-1)
            cos = jnp.cos(emb)[position_ids][:, None].astype(q.dtype)
            sin = jnp.sin(emb)[position_ids][:, None].astype(q.dtype)
            return (q * cos + rotate_half(q) * sin, k * cos + rotate_half(k) * sin)

        def sdpa(q, k, v, causal):
            scale = 1.0 / np.sqrt(q.shape[-1])
            scores = jnp.einsum('bhqd,bhkd->bhqk', q * scale, k)
            if causal:
                mask = jnp.tril(jnp.ones((q.shape[-2], k.shape[-2]), dtype=bool))
                scores = jnp.where(mask, scores, jnp.finfo(jnp.float32).min)
            p = jax.nn.softmax(scores.astype(jnp.float32), axis=-1).astype(q.dtype)
            return jnp.einsum('bhqk,bhkd->bhqd', p, v)

        def heads(x, nh, hd):
            b, l, _ = x.shape
            return x.reshape(b, l, nh, hd).transpose(0, 2, 1, 3)
        key = jax.random.key(seed)
        ks = jax.random.split(key, 20)
        s = 0.02
        f32 = jnp.float32
        return {'hidden_states': jax.random.normal(ks[0], (B, L, H), f32), 'encoder_outputs': jax.random.normal(ks[1], (B, LE, CH), f32), 'token_type_ids': jax.random.randint(ks[2], (B, L), 0, 2, jnp.int32), 'position_ids': jnp.arange(L, dtype=jnp.int32)[None, :], 'ln_in_w': jnp.ones((H,), f32), 'ln_post_attn_w': jnp.ones((H,), f32), 'ln_post_cross_w': jnp.ones((H,), f32), 'v_qkv': jax.random.normal(ks[3], (H, 3 * H), f32) * s, 'l_qkv': jax.random.normal(ks[4], (H, 3 * H), f32) * s, 'v_dense': jax.random.normal(ks[5], (H, H), f32) * s, 'l_dense': jax.random.normal(ks[6], (H, H), f32) * s, 'cq_w': jax.random.normal(ks[7], (H, CC), f32) * s, 'ckv_w': jax.random.normal(ks[8], (CH, 2 * CC), f32) * s, 'cdense_w': jax.random.normal(ks[9], (CC, H), f32) * s, 'v_gate': jax.random.normal(ks[10], (H, I), f32) * s, 'v_up': jax.random.normal(ks[11], (H, I), f32) * s, 'v_down': jax.random.normal(ks[12], (I, H), f32) * s, 'l_gate': jax.random.normal(ks[13], (H, I), f32) * s, 'l_up': jax.random.normal(ks[14], (H, I), f32) * s, 'l_down': jax.random.normal(ks[15], (I, H), f32) * s}
    _L2_xattn_all = _L2_xattn_setup()
    _L2_xattn_in = {k: v for k, v in _L2_xattn_all.items() if k in ('ln_in_w', 'ln_post_attn_w', 'ln_post_cross_w', 'v_qkv', 'l_qkv', 'v_dense', 'l_dense', 'cq_w', 'ckv_w', 'cdense_w', 'v_gate', 'v_up', 'v_down', 'l_gate', 'l_up', 'l_down')}
    del _L2_xattn_all

    def _L3_xattn_setup():
        import jax, jax.numpy as jnp
        import numpy as np
        DIM = 256
        DIM_MEDIA = 128
        HEADS = 16
        DIM_HEAD = 64
        INNER = HEADS * DIM_HEAD
        FF_INNER = 4 * DIM
        B, N_TOK, N_LAT = (4, 256, 64)
        EPS = 1e-05

        def layernorm(x, g, b):
            mu = jnp.mean(x, axis=-1, keepdims=True)
            var = jnp.var(x, axis=-1, keepdims=True)
            return (x - mu) * jax.lax.rsqrt(var + EPS) * g + b
        key = jax.random.key(seed)
        ks = jax.random.split(key, 12)
        x = jax.random.normal(ks[0], (B, N_TOK, DIM), dtype=jnp.float32)
        media = jax.random.normal(ks[1], (B, N_LAT, DIM_MEDIA), dtype=jnp.float32)
        media_mask = jax.random.randint(ks[2], (B, N_LAT), 0, 2).astype(bool)
        media_mask = media_mask.at[:, 0].set(True)
        s = lambda d: 1.0 / np.sqrt(d)
        Wq = jax.random.normal(ks[3], (DIM, INNER), dtype=jnp.float32) * s(DIM)
        Wkv = jax.random.normal(ks[4], (DIM_MEDIA, 2 * INNER), dtype=jnp.float32) * s(DIM_MEDIA)
        Wo = jax.random.normal(ks[5], (INNER, DIM), dtype=jnp.float32) * s(INNER)
        W1 = jax.random.normal(ks[6], (DIM, FF_INNER), dtype=jnp.float32) * s(DIM)
        W2 = jax.random.normal(ks[7], (FF_INNER, DIM), dtype=jnp.float32) * s(FF_INNER)
        return {'x': x, 'media': media, 'media_mask': media_mask, 'ln_q_g': jnp.ones((DIM,), jnp.float32), 'ln_q_b': jnp.zeros((DIM,), jnp.float32), 'Wq': Wq, 'Wkv': Wkv, 'Wo': Wo, 'attn_gate': jax.random.normal(ks[8], (1,), jnp.float32) * 0.5, 'ln_ff_g': jnp.ones((DIM,), jnp.float32), 'ln_ff_b': jnp.zeros((DIM,), jnp.float32), 'W1': W1, 'W2': W2, 'ff_gate': jax.random.normal(ks[9], (1,), jnp.float32) * 0.5}
    _L3_xattn_all = _L3_xattn_setup()
    _L3_xattn_in = {k: v for k, v in _L3_xattn_all.items() if k in ('ln_q_g', 'ln_q_b', 'Wq', 'Wkv', 'Wo', 'attn_gate', 'ln_ff_g', 'ln_ff_b', 'W1', 'W2', 'ff_gate')}
    del _L3_xattn_all
    return {'x': x, 'ctx_1024': ctx_1024, 'pos_1xS': pos_1xS, 'mask_BxS2_bk0': mask_BxS2_bk0, 'mask_BxS_ik0': mask_BxS_ik0, 'L0_xattn_ln_q_g': _L0_xattn_in['ln_q_g'], 'L0_xattn_ln_q_b': _L0_xattn_in['ln_q_b'], 'L0_xattn_Wq': _L0_xattn_in['Wq'], 'L0_xattn_Wkv': _L0_xattn_in['Wkv'], 'L0_xattn_Wo': _L0_xattn_in['Wo'], 'L0_xattn_attn_gate': _L0_xattn_in['attn_gate'], 'L0_xattn_ln_ff_g': _L0_xattn_in['ln_ff_g'], 'L0_xattn_ln_ff_b': _L0_xattn_in['ln_ff_b'], 'L0_xattn_W1': _L0_xattn_in['W1'], 'L0_xattn_W2': _L0_xattn_in['W2'], 'L0_xattn_ff_gate': _L0_xattn_in['ff_gate'], 'L1_xattn_W_mem': _L1_xattn_in['W_mem'], 'L1_xattn_W_gate': _L1_xattn_in['W_gate'], 'L1_xattn_b_gate': _L1_xattn_in['b_gate'], 'L1_xattn_norm_w': _L1_xattn_in['norm_w'], 'L2_xattn_ln_in_w': _L2_xattn_in['ln_in_w'], 'L2_xattn_ln_post_attn_w': _L2_xattn_in['ln_post_attn_w'], 'L2_xattn_ln_post_cross_w': _L2_xattn_in['ln_post_cross_w'], 'L2_xattn_v_qkv': _L2_xattn_in['v_qkv'], 'L2_xattn_l_qkv': _L2_xattn_in['l_qkv'], 'L2_xattn_v_dense': _L2_xattn_in['v_dense'], 'L2_xattn_l_dense': _L2_xattn_in['l_dense'], 'L2_xattn_cq_w': _L2_xattn_in['cq_w'], 'L2_xattn_ckv_w': _L2_xattn_in['ckv_w'], 'L2_xattn_cdense_w': _L2_xattn_in['cdense_w'], 'L2_xattn_v_gate': _L2_xattn_in['v_gate'], 'L2_xattn_v_up': _L2_xattn_in['v_up'], 'L2_xattn_v_down': _L2_xattn_in['v_down'], 'L2_xattn_l_gate': _L2_xattn_in['l_gate'], 'L2_xattn_l_up': _L2_xattn_in['l_up'], 'L2_xattn_l_down': _L2_xattn_in['l_down'], 'L3_xattn_ln_q_g': _L3_xattn_in['ln_q_g'], 'L3_xattn_ln_q_b': _L3_xattn_in['ln_q_b'], 'L3_xattn_Wq': _L3_xattn_in['Wq'], 'L3_xattn_Wkv': _L3_xattn_in['Wkv'], 'L3_xattn_Wo': _L3_xattn_in['Wo'], 'L3_xattn_attn_gate': _L3_xattn_in['attn_gate'], 'L3_xattn_ln_ff_g': _L3_xattn_in['ln_ff_g'], 'L3_xattn_ln_ff_b': _L3_xattn_in['ln_ff_b'], 'L3_xattn_W1': _L3_xattn_in['W1'], 'L3_xattn_W2': _L3_xattn_in['W2'], 'L3_xattn_ff_gate': _L3_xattn_in['ff_gate']}

def reference(x, ctx_1024, pos_1xS, mask_BxS2_bk0, mask_BxS_ik0, L0_xattn_ln_q_g, L0_xattn_ln_q_b, L0_xattn_Wq, L0_xattn_Wkv, L0_xattn_Wo, L0_xattn_attn_gate, L0_xattn_ln_ff_g, L0_xattn_ln_ff_b, L0_xattn_W1, L0_xattn_W2, L0_xattn_ff_gate, L1_xattn_W_mem, L1_xattn_W_gate, L1_xattn_b_gate, L1_xattn_norm_w, L2_xattn_ln_in_w, L2_xattn_ln_post_attn_w, L2_xattn_ln_post_cross_w, L2_xattn_v_qkv, L2_xattn_l_qkv, L2_xattn_v_dense, L2_xattn_l_dense, L2_xattn_cq_w, L2_xattn_ckv_w, L2_xattn_cdense_w, L2_xattn_v_gate, L2_xattn_v_up, L2_xattn_v_down, L2_xattn_l_gate, L2_xattn_l_up, L2_xattn_l_down, L3_xattn_ln_q_g, L3_xattn_ln_q_b, L3_xattn_Wq, L3_xattn_Wkv, L3_xattn_Wo, L3_xattn_attn_gate, L3_xattn_ln_ff_g, L3_xattn_ln_ff_b, L3_xattn_W1, L3_xattn_W2, L3_xattn_ff_gate):
    import jax
    import jax.numpy as jnp

    def _L0_xattn_ref(x, media, media_mask, ln_q_g, ln_q_b, Wq, Wkv, Wo, attn_gate, ln_ff_g, ln_ff_b, W1, W2, ff_gate):
        import jax, jax.numpy as jnp
        import numpy as np
        DIM = 256
        DIM_MEDIA = 128
        HEADS = 16
        DIM_HEAD = 64
        INNER = HEADS * DIM_HEAD
        FF_INNER = 4 * DIM
        B, N_TOK, N_LAT = (4, 256, 64)
        EPS = 1e-05

        def layernorm(x, g, b):
            mu = jnp.mean(x, axis=-1, keepdims=True)
            var = jnp.var(x, axis=-1, keepdims=True)
            return (x - mu) * jax.lax.rsqrt(var + EPS) * g + b
        scale = DIM_HEAD ** (-0.5)
        qn = layernorm(x, ln_q_g, ln_q_b)
        q = qn @ Wq * scale
        kv = media @ Wkv
        k, v = jnp.split(kv, 2, axis=-1)
        split_heads = lambda t: t.reshape(t.shape[0], t.shape[1], HEADS, DIM_HEAD).transpose(0, 2, 1, 3)
        q, k, v = (split_heads(q), split_heads(k), split_heads(v))
        sim = jnp.einsum('bhid,bhjd->bhij', q, k)
        neg_inf = jnp.finfo(sim.dtype).min
        sim = jnp.where(media_mask[:, None, None, :], sim, neg_inf)
        attn = jax.nn.softmax(sim, axis=-1)
        out = jnp.einsum('bhij,bhjd->bhid', attn, v)
        out = out.transpose(0, 2, 1, 3).reshape(x.shape[0], x.shape[1], INNER)
        attn_out = out @ Wo
        x = x + jnp.tanh(attn_gate) * attn_out
        h = layernorm(x, ln_ff_g, ln_ff_b)
        h = jax.nn.gelu(h @ W1, approximate=False) @ W2
        x = x + jnp.tanh(ff_gate) * h
        return x

    def _L1_xattn_ref(hidden_states, memory, W_mem, W_gate, b_gate, norm_w):
        import jax, jax.numpy as jnp
        import numpy as np
        EPS = 1e-06

        def _rmsnorm(x, w):
            var = jnp.mean(jnp.square(x), axis=-1, keepdims=True)
            return x * jax.lax.rsqrt(var + EPS) * w
        D = hidden_states.shape[-1]
        memory_proj = jnp.einsum('bme,de->bmd', memory, W_mem)
        scores = jnp.einsum('bnd,bmd->bnm', hidden_states, memory_proj) / jnp.sqrt(jnp.float32(D))
        attn = jax.nn.softmax(scores, axis=-1)
        memory_context = jnp.einsum('bnm,bmd->bnd', attn, memory_proj)
        gate_input = jnp.concatenate([hidden_states, memory_context], axis=-1)
        gate = jax.nn.sigmoid(jnp.einsum('bnf,df->bnd', gate_input, W_gate) + b_gate)
        fused = hidden_states + gate * memory_context
        return _rmsnorm(fused, norm_w)

    def _L2_xattn_ref(hidden_states, encoder_outputs, token_type_ids, position_ids, ln_in_w, ln_post_attn_w, ln_post_cross_w, v_qkv, l_qkv, v_dense, l_dense, cq_w, ckv_w, cdense_w, v_gate, v_up, v_down, l_gate, l_up, l_down):
        import jax, jax.numpy as jnp
        import numpy as np
        H = 256
        NH = 16
        HD = H // NH
        CH = 128
        CC = 128
        CHD = CC // NH
        I = 688
        B = 2
        L = 256
        LE = 128
        EPS = 1e-06

        def rms_norm(x, w):
            xf = x.astype(jnp.float32)
            var = jnp.mean(xf * xf, axis=-1, keepdims=True)
            return (w * (xf * jax.lax.rsqrt(var + EPS))).astype(x.dtype)

        def expert_mask(tt):
            vm = jnp.zeros(tt.shape, dtype=bool)
            vm = vm.at[:, :-1].set((tt[:, :-1] == 1) & (tt[:, 1:] == 1))
            return vm

        def rotate_half(x):
            d = x.shape[-1] // 2
            return jnp.concatenate([-x[..., d:], x[..., :d]], axis=-1)

        def apply_rotary(q, k, position_ids, seq_len):
            inv = 1.0 / 10000.0 ** (jnp.arange(0, HD, 2, dtype=jnp.float32) / HD)
            t = jnp.arange(seq_len, dtype=jnp.float32)
            freqs = jnp.outer(t, inv)
            emb = jnp.concatenate([freqs, freqs], axis=-1)
            cos = jnp.cos(emb)[position_ids][:, None].astype(q.dtype)
            sin = jnp.sin(emb)[position_ids][:, None].astype(q.dtype)
            return (q * cos + rotate_half(q) * sin, k * cos + rotate_half(k) * sin)

        def sdpa(q, k, v, causal):
            scale = 1.0 / np.sqrt(q.shape[-1])
            scores = jnp.einsum('bhqd,bhkd->bhqk', q * scale, k)
            if causal:
                mask = jnp.tril(jnp.ones((q.shape[-2], k.shape[-2]), dtype=bool))
                scores = jnp.where(mask, scores, jnp.finfo(jnp.float32).min)
            p = jax.nn.softmax(scores.astype(jnp.float32), axis=-1).astype(q.dtype)
            return jnp.einsum('bhqk,bhkd->bhqd', p, v)

        def heads(x, nh, hd):
            b, l, _ = x.shape
            return x.reshape(b, l, nh, hd).transpose(0, 2, 1, 3)
        b, l, _ = hidden_states.shape
        vm = expert_mask(token_type_ids)[..., None]
        residual = hidden_states
        x = rms_norm(hidden_states, ln_in_w)
        mixed = jnp.where(vm, x @ v_qkv, x @ l_qkv)
        q, k, v = jnp.split(mixed, 3, axis=-1)
        q, k, v = (heads(q, NH, HD), heads(k, NH, HD), heads(v, NH, HD))
        q, k = apply_rotary(q, k, position_ids, l)
        ctx = sdpa(q, k, v, causal=True)
        ctx = ctx.transpose(0, 2, 1, 3).reshape(b, l, H)
        attn_out = jnp.where(vm, ctx @ v_dense, ctx @ l_dense)
        hidden_states = residual + attn_out
        ci = rms_norm(hidden_states, ln_post_cross_w)
        cq = heads(ci @ cq_w, NH, CHD)
        ckv = encoder_outputs @ ckv_w
        ck, cv = jnp.split(ckv, 2, axis=-1)
        ck, cv = (heads(ck, NH, CHD), heads(cv, NH, CHD))
        cctx = sdpa(cq, ck, cv, causal=False)
        cctx = cctx.transpose(0, 2, 1, 3).reshape(b, l, CC)
        hidden_states = hidden_states + cctx @ cdense_w
        mi = rms_norm(hidden_states, ln_post_attn_w)
        v_out = jax.nn.silu(mi @ v_gate) * (mi @ v_up) @ v_down
        l_out = jax.nn.silu(mi @ l_gate) * (mi @ l_up) @ l_down
        hidden_states = hidden_states + jnp.where(vm, v_out, l_out)
        return hidden_states

    def _L3_xattn_ref(x, media, media_mask, ln_q_g, ln_q_b, Wq, Wkv, Wo, attn_gate, ln_ff_g, ln_ff_b, W1, W2, ff_gate):
        import jax, jax.numpy as jnp
        import numpy as np
        DIM = 256
        DIM_MEDIA = 128
        HEADS = 16
        DIM_HEAD = 64
        INNER = HEADS * DIM_HEAD
        FF_INNER = 4 * DIM
        B, N_TOK, N_LAT = (4, 256, 64)
        EPS = 1e-05

        def layernorm(x, g, b):
            mu = jnp.mean(x, axis=-1, keepdims=True)
            var = jnp.var(x, axis=-1, keepdims=True)
            return (x - mu) * jax.lax.rsqrt(var + EPS) * g + b
        scale = DIM_HEAD ** (-0.5)
        qn = layernorm(x, ln_q_g, ln_q_b)
        q = qn @ Wq * scale
        kv = media @ Wkv
        k, v = jnp.split(kv, 2, axis=-1)
        split_heads = lambda t: t.reshape(t.shape[0], t.shape[1], HEADS, DIM_HEAD).transpose(0, 2, 1, 3)
        q, k, v = (split_heads(q), split_heads(k), split_heads(v))
        sim = jnp.einsum('bhid,bhjd->bhij', q, k)
        neg_inf = jnp.finfo(sim.dtype).min
        sim = jnp.where(media_mask[:, None, None, :], sim, neg_inf)
        attn = jax.nn.softmax(sim, axis=-1)
        out = jnp.einsum('bhij,bhjd->bhid', attn, v)
        out = out.transpose(0, 2, 1, 3).reshape(x.shape[0], x.shape[1], INNER)
        attn_out = out @ Wo
        x = x + jnp.tanh(attn_gate) * attn_out
        h = layernorm(x, ln_ff_g, ln_ff_b)
        h = jax.nn.gelu(h @ W1, approximate=False) @ W2
        x = x + jnp.tanh(ff_gate) * h
        return x
    x = _L0_xattn_ref(x, ctx_1024, mask_BxS2_bk0, L0_xattn_ln_q_g, L0_xattn_ln_q_b, L0_xattn_Wq, L0_xattn_Wkv, L0_xattn_Wo, L0_xattn_attn_gate, L0_xattn_ln_ff_g, L0_xattn_ln_ff_b, L0_xattn_W1, L0_xattn_W2, L0_xattn_ff_gate)
    x = _L1_xattn_ref(x, ctx_1024, L1_xattn_W_mem, L1_xattn_W_gate, L1_xattn_b_gate, L1_xattn_norm_w)
    x = _L2_xattn_ref(x, ctx_1024, mask_BxS_ik0, pos_1xS, L2_xattn_ln_in_w, L2_xattn_ln_post_attn_w, L2_xattn_ln_post_cross_w, L2_xattn_v_qkv, L2_xattn_l_qkv, L2_xattn_v_dense, L2_xattn_l_dense, L2_xattn_cq_w, L2_xattn_ckv_w, L2_xattn_cdense_w, L2_xattn_v_gate, L2_xattn_v_up, L2_xattn_v_down, L2_xattn_l_gate, L2_xattn_l_up, L2_xattn_l_down)
    x = _L3_xattn_ref(x, ctx_1024, mask_BxS2_bk0, L3_xattn_ln_q_g, L3_xattn_ln_q_b, L3_xattn_Wq, L3_xattn_Wkv, L3_xattn_Wo, L3_xattn_attn_gate, L3_xattn_ln_ff_g, L3_xattn_ln_ff_b, L3_xattn_W1, L3_xattn_W2, L3_xattn_ff_gate)
    return x

_drawn_inputs = setup_inputs


def setup_inputs(seed=0):
    import zlib

    import numpy as np

    out = dict(_drawn_inputs(seed))
    spreads = {'L0_xattn_ln_q_g': (1.0, 0.6),
     'L0_xattn_ln_q_b': (0.0, 0.8),
     'L0_xattn_ln_ff_g': (1.0, 0.6),
     'L0_xattn_ln_ff_b': (0.0, 0.8),
     'L1_xattn_norm_w': (1.0, 0.2),
     'L2_xattn_ln_in_w': (1.0, 0.6),
     'L2_xattn_ln_post_attn_w': (1.0, 0.6),
     'L2_xattn_ln_post_cross_w': (1.0, 0.6),
     'L3_xattn_ln_q_g': (1.0, 0.6),
     'L3_xattn_ln_q_b': (0.0, 2.0),
     'L3_xattn_ln_ff_g': (1.0, 0.6),
     'L3_xattn_ln_ff_b': (0.0, 2.0)}
    factors = {'L0_xattn_W1': 2.775,
     'L1_xattn_b_gate': 8.0,
     'L2_xattn_v_qkv': 8.0,
     'L2_xattn_v_dense': 5.469,
     'L2_xattn_cq_w': 64.0,
     'L2_xattn_v_gate': 5.836,
     'L2_xattn_v_up': 5.784,
     'L2_xattn_v_down': 5.832,
     'L3_xattn_W1': 9.814,
     'L2_xattn_l_dense': 4.751,
     'L2_xattn_ckv_w': 6.327,
     'L2_xattn_cdense_w': 6.393,
     'L2_xattn_l_gate': 5.514,
     'L2_xattn_l_up': 5.397,
     'L2_xattn_l_down': 5.433,
     'L3_xattn_Wq': 2.7,
     'L3_xattn_W2': 2.842}
    for name, (base, spread) in spreads.items():
        noise = np.random.default_rng([zlib.crc32(name.encode()), seed]).standard_normal(out[name].shape)
        drawn = base * np.exp(spread * noise) if base else spread * noise
        out[name] = jnp.asarray(drawn.astype(out[name].dtype))
    for name, factor in factors.items():
        out[name] = (out[name] * factor).astype(out[name].dtype)
    return out
```

```python
from contextlib import ExitStack

import numpy as np

import concourse.bass as bass
from concourse import mybir

ALU = mybir.AluOpType
ACT = mybir.ActivationFunctionType
AX = mybir.AxisListType
F32 = mybir.dt.float32
F32R = mybir.dt.float32r
BF16 = mybir.dt.bfloat16
I32 = mybir.dt.int32
U8 = mybir.dt.uint8

P = 128
BATCH = 32
SEQ = 64
TOK = BATCH * SEQ
D = 256
DC = D // P
CTX = 128
TILES = TOK // P
BT = 2
BLK = BT * P
NB = TOK // BLK
BB = BLK // SEQ
HEADS = 16
PAIRS = HEADS // 2
INNER = 1024
FF = 1024
MOE_FF = 688
F_SIZES = [116, 116, 114, 114, 114, 114]
F_OFF = [sum(F_SIZES[:i]) for i in range(len(F_SIZES))]
MASKED = -(2.0 ** 127)
KB = 1024

W_ATT = {"wk": INNER, "wv": INNER, "wq": DC * INNER, "wo": PAIRS * D}
W_FFN = {"w1": DC * FF, "w2": (FF // P) * D}
W_MEM = {"wm": D, "wg": 4 * D}
W_SELF = {"qkv": 4 * 3 * D, "dense": DC * 2 * D}
W_CROSS = {"cq": DC * P, "ckv": 2 * P, "cd": D}
W_MOE = {"gu": 4 * 2 * MOE_FF, "dn": len(F_SIZES) * 2 * D}
WEIGHTS = [W_ATT, W_FFN, W_MEM, W_SELF, W_CROSS, W_MOE, W_ATT, W_FFN]
WCOLS = [sum(w.values()) for w in WEIGHTS]
CHUNK = [c // NB for c in WCOLS]

COLS = {}


def _col(name, n):
    COLS[name] = (sum(w for _, w in COLS.values()), n)


for _n in ("g0", "b0", "g1", "b1", "g6", "b6", "g7", "b7", "g3", "g4", "g5"):
    _col(_n, DC)
_col("gate0", 1), _col("gate1", 1), _col("gate6", 1), _col("gate7", 1)
_col("hm8", 8), _col("hm16", 16), _col("tcol", 1)
_col("eps5", BT), _col("eps6", BT), _col("minus_half", BT)
_col("bgate", D), _col("normw", D), _col("ident", P)
_col("cossin", 32), _col("causal", SEQ), _col("batch_sel", P)
NCOLS = sum(w for _, w in COLS.values())


class Ring:

    def __init__(self, core, name, banks, jobs):
        self.banks = banks
        self.full = [core.sem(f"{name}_full{b}") for b in banks]
        self.empty = [core.sem(f"{name}_empty{b}") for b in banks]
        self.at, fills, drains = {}, [0] * len(banks), [0] * len(banks)
        for n, (job, d) in enumerate(jobs):
            b = n % len(banks)
            self.at[job] = (b, fills[b], drains[b], d)
            fills[b] += 1
            drains[b] += d
        self.fills, self.drains = fills, drains

    def bank(self, job):
        return self.banks[self.at[job][0]]

    def full_of(self, job):
        return self.full[self.at[job][0]]

    def empty_of(self, job):
        return self.empty[self.at[job][0]]

    def filled(self, job, t):
        b, fills, _, _ = self.at[job]
        return t * self.fills[b] + fills + 1

    def free(self, job, t):
        b, _, drains, _ = self.at[job]
        return t * self.drains[b] + drains

    def drained(self, job, t):
        b, _, drains, d = self.at[job]
        return t * self.drains[b] + drains + d


def first(t):
    return isinstance(t, int) and t == 0


def sweep(eng, head, step, tail):
    head()
    with eng.Fori(1, NB) as u:
        step(u)
    tail()


def f32(part):
    return part.bitcast(F32)


def wide(ap, axis, n):
    shape = list(ap.shape)
    return ap.unsqueeze(axis).broadcast_to(shape[:axis] + [n] + shape[axis:])


class Core:

    def __init__(self, nc, ctx, dram, out):
        self.nc, self.ctx, self.dram, self.out = nc, ctx, dram, out

        def sb(name, shape, dt=F32):
            return ctx.enter_context(nc.sbuf_tensor(name, shape, dt))

        self.x = sb("x", [P, TILES + BT, D])
        self.ctx_h = sb("ctx_h", [P, TOK], F32R)
        self.ctx_l = sb("ctx_l", [P, TOK], F32R)
        self.cols = sb("cols", [P, NCOLS])
        self.ident_b = sb("ident_b", [P, P], BF16)
        self.causal = sb("causal", [P, SEQ], BF16)
        self.batch_sel = sb("batch_sel", [2, P], BF16)
        self.mask_row = sb("mask_row", [2, TILES, SEQ], BF16)
        self.gates = sb("gates", [P, 4])
        self.vm = sb("vm", [P, TILES + BT])
        self.not_vm = sb("not_vm", [P, TILES + BT])
        self.rope = sb("rope", [P, 32])
        self.w_raw = sb("w_raw", [P, max(CHUNK)])
        self.bn = sb("bn", [P, BT, 6])
        self.mv = sb("mv", [P, BT, 2])
        self.ve = sb("ve", [P, 3, BT])
        self.rstd = sb("rstd", [P, BT])
        self.spare = sb("spare", [P, 3])
        self.phase_sems = []
        self.begun = nc.alloc_semaphore(name="begun")
        self.low = -(-nc.sbuf_base // 64) * 64
        self.high = nc.sbuf_top // 64 * 64
        self.psum = ctx.enter_context(nc.psum_tensor("psum", [P, 8, 512], F32))
        self.weights, self.low_end, self.high_start = [], [], []
        for n, c in enumerate(WCOLS):
            size = 2 * 4 * c
            at = self.low if n % 2 == 0 else self.high - size
            h = nc.alloc_sbuf_tensor_at(f"w{n}_h", [P, c], F32R, offset=at)
            l = nc.alloc_sbuf_tensor_at(f"w{n}_l", [P, c], F32R, offset=at + size // 2)
            self.weights.append((h, l))
        for n in range(len(WCOLS)):
            live = [m for m in (n, n + 1) if m < len(WCOLS)]
            self.low_end.append(self.low + max([8 * WCOLS[m] for m in live if m % 2 == 0], default=0))
            self.high_start.append(self.high - max([8 * WCOLS[m] for m in live if m % 2], default=0))

    def sem(self, name):
        self.phase_sems.append(self.nc.alloc_semaphore(name=name))
        return self.phase_sems[-1]

    def end_phase(self):
        self.nc.clear_and_free_semaphores(self.phase_sems)
        self.nc.all_engine_barrier()
        self.phase_sems = []

    def col(self, name, rows=P):
        a, n = COLS[name]
        return self.cols[0:rows, a:a + n]

    def weight(self, n, name):
        a = 0
        for k, w in WEIGHTS[n].items():
            if k == name:
                return tuple(part[:, a:a + w] for part in self.weights[n])
            a += w

    def placer(self, n):
        at = [self.low_end[n]]

        def place(name, shape, dt=F32):
            size = int(np.prod(shape[1:])) * (2 if dt == BF16 else 4)
            size = -(-size // 64) * 64
            t = self.nc.alloc_sbuf_tensor_at(f"p{n}_{name}", shape, dt, offset=at[0])
            at[0] += size
            assert at[0] <= self.high_start[n], (n, name, at[0], self.high_start[n])
            return t

        return place


def block_tokens(t):
    return bass.ds(t * BLK, BLK)


def block_tiles(t):
    return bass.ds(t * BT, BT)


class NextWeights:

    def __init__(self, core, n):
        self.core, self.n = core, n
        if n < len(WEIGHTS):
            self.landed = core.sem(f"w{n}_landed")
            self.high_done = core.sem(f"w{n}_high_done")
            self.low_done = core.sem(f"w{n}_low_done")

    def load(self, sp, t):
        if self.n >= len(WEIGHTS):
            return
        c = CHUNK[self.n]
        if not first(t):
            sp.wait_ge(self.low_done, t)
        sp.dma_start(self.core.w_raw[:, 0:c], self.core.dram[f"w{self.n}"][:, bass.ds(t * c, c)]).then_inc(self.landed, 16)

    def split(self, pool, t, ready):
        if self.n >= len(WEIGHTS):
            return
        c = CHUNK[self.n]
        h, l = self.core.weights[self.n]
        at = bass.ds(t * c, c)
        raw = self.core.w_raw[:, 0:c]
        pool.wait_ge(self.landed, 16 * t + 16)
        pool.wait_ge(ready, 1)
        pool.tensor_copy(h[:, at], raw).then_inc(self.high_done, 1)
        pool.wait_ge(self.high_done, t + 1)
        pool.tensor_tensor(l[:, at], raw, f32(h[:, at]), ALU.subtract).then_inc(self.low_done, 1)


class Norm:

    def __init__(self, core, n, kind, eps, xn, ring, last_job, ready=None):
        self.core, self.kind, self.eps, self.xn, self.ring, self.last = core, kind, eps, xn, ring, last_job
        self.stats_done = core.sem(f"n{n}_stats")
        self.mean_done = core.sem(f"n{n}_mean")
        self.var_done = core.sem(f"n{n}_var")
        self.rstd_done = core.sem(f"n{n}_rstd")
        self.xn_done = core.sem(f"n{n}_xn")
        self.steps = 1 if kind == "layer" else 3
        self.outs = 2 * BT if kind == "experts" else BT

    def stats(self, dve, t, src=None):
        c = self.core
        for k in range(BT):
            row = c.x[:, bass.ds(t * BT + k, 1), :].squeeze(1) if src is None else src[:, k, :]
            dve.bn_stats(c.bn[:, k, :], row).then_inc(self.stats_done, 1)
        dve.wait_ge(self.stats_done, BT * t + BT)
        dve.tensor_copy(c.spare[:, 1:2], c.spare[:, 0:1])
        for k in range(BT):
            dve.bn_aggr(c.mv[:, k, :], c.bn[:, k, :]).then_inc(self.mean_done, 1)

    def invert(self, pool, t):
        c = self.core
        mean, var = c.mv[:, :, 0], c.mv[:, :, 1]
        eps, half = c.col(self.eps), c.col("minus_half")
        n = self.steps
        pool.wait_ge(self.mean_done, BT * t + BT)
        if self.kind == "layer":
            pool.tensor_tensor(c.ve[:, 2, :], var, eps, ALU.add).then_inc(self.var_done, 1)
        else:
            pool.tensor_tensor(c.ve[:, 0, :], mean, mean, ALU.mult).then_inc(self.var_done, 1)
            pool.wait_ge(self.var_done, n * t + 1)
            pool.tensor_tensor(c.ve[:, 1, :], c.ve[:, 0, :], var, ALU.add).then_inc(self.var_done, 1)
            pool.wait_ge(self.var_done, n * t + 2)
            pool.tensor_tensor(c.ve[:, 2, :], c.ve[:, 1, :], eps, ALU.add).then_inc(self.var_done, 1)
        pool.wait_ge(self.var_done, n * t + n)
        pool.tensor_tensor(c.rstd[:, :], c.ve[:, 2, :], half, ALU.pow).then_inc(self.rstd_done, 1)

    def normalise(self, dve, t):
        c = self.core
        if not first(t):
            dve.wait_ge(self.ring.full_of(self.last), self.ring.filled(self.last, t - 1))
        dve.wait_ge(self.rstd_done, t + 1)
        for k in range(BT):
            row = c.x[:, bass.ds(t * BT + k, 1), :].squeeze(1)
            r = c.rstd[:, k:k + 1]
            if self.kind == "layer":
                dve.tensor_scalar(self.xn[:, k, 0, :], row, c.mv[:, k, 0:1], r, ALU.subtract, ALU.mult).then_inc(self.xn_done, 1)
            elif self.kind == "rms":
                dve.tensor_scalar(self.xn[:, k, 0, :], row, r, None, ALU.mult).then_inc(self.xn_done, 1)
            else:
                at = bass.ds(t * BT + k, 1)
                dve.tensor_scalar(self.xn[:, k, 0, :], row, r, c.vm[:, at], ALU.mult, ALU.mult).then_inc(self.xn_done, 1)
                dve.tensor_scalar(self.xn[:, k, 1, :], row, r, c.not_vm[:, at], ALU.mult, ALU.mult).then_inc(self.xn_done, 1)


class Turned:

    def __init__(self, core, n, norm, ring, jobs, y, xh, xl, gain, shift):
        self.core, self.norm, self.ring, self.jobs = core, norm, ring, jobs
        self.y, self.xh, self.xl, self.gain, self.shift = y, xh, xl, gain, shift
        self.high_done = core.sem(f"t{n}_high")
        self.split_done = core.sem(f"t{n}_split")

    def transpose(self, pe, t):
        c = self.core
        pe.wait_ge(self.norm.xn_done, self.norm.outs * (t + 1))
        for j, job in enumerate(self.jobs):
            if not (first(t) and self.ring.free(job, 0) == 0):
                pe.wait_ge(self.ring.empty_of(job), self.ring.free(job, t))
            bank = self.ring.bank(job)
            for ch in range(DC):
                for k in range(BT):
                    done = pe.transpose(c.psum[:, bank, (ch * BT + k) * P:(ch * BT + k + 1) * P],
                                        self.norm.xn[:, k, j, ch * P:(ch + 1) * P], c.col("ident"))
            done.then_inc(self.ring.full_of(job), 1)

    def scale(self, act, t):
        c, n = self.core, len(self.jobs)
        for j, job in enumerate(self.jobs):
            act.wait_ge(self.ring.full_of(job), self.ring.filled(job, t))
            if not first(t):
                act.wait_ge(self.split_done, n * t - n + j + 1)
            for ch in range(DC):
                gain = c.col(self.gain)[:, ch:ch + 1]
                bias = c.col(self.shift)[:, ch:ch + 1] if self.shift else 0.0
                done = act.activation(self.y[:, j * DC + ch, :], c.psum[:, self.ring.bank(job), ch * BLK:(ch + 1) * BLK],
                                      ACT.Identity, bias=bias, scale=gain)
            done.then_inc(self.ring.empty_of(job), 1)

    def split(self, dve, t):
        n = len(self.jobs)
        for j, job in enumerate(self.jobs):
            part = slice(j * DC, (j + 1) * DC)
            dve.wait_ge(self.ring.empty_of(job), self.ring.drained(job, t))
            dve.tensor_copy(self.xh[:, part, :], self.y[:, part, :]).then_inc(self.high_done, 1)
            dve.wait_ge(self.high_done, n * t + j + 1)
            dve.tensor_tensor(self.xl[:, part, :], self.y[:, part, :], f32(self.xh[:, part, :]), ALU.subtract)\
               .then_inc(self.split_done, 1)


def three(pe, out, stationary, moving, start, stop):
    (sh, sl), (mh, ml) = stationary, moving
    pe.matmul(out, sh, mh, start=start, stop=False)
    pe.matmul(out, sh, ml, start=False, stop=False)
    return pe.matmul(out, sl, mh, start=False, stop=stop)


def pe_wait_free(pe, ring, job, t):
    if not (first(t) and ring.free(job, 0) == 0):
        pe.wait_ge(ring.empty_of(job), ring.free(job, t))


class Softmax:

    def __init__(self, core, n, place, ring, read_job):
        self.core, self.ring, self.read_job = core, ring, read_job
        self.e = place("e", [P, BT, HEADS, SEQ])
        self.top = place("top", [P, BT, HEADS])
        self.total = place("total", [P, BT, HEADS])
        self.inverse = place("inverse", [P, BT, HEADS])
        self.scored = core.sem(f"s{n}_scored")
        self.top_done = core.sem(f"s{n}_top")
        self.less_done = core.sem(f"s{n}_less")
        self.exp_done = core.sem(f"s{n}_exp")
        self.total_done = core.sem(f"s{n}_total")
        self.inverse_done = core.sem(f"s{n}_inverse")
        self.ready = core.sem(f"s{n}_ready")

    def scores(self, k):
        return self.core.psum[:, 2 * k:2 * k + 2, :].rearrange("p b (h j) -> p (b h) j", j=SEQ)

    def less_top(self, dve, t, k):
        dve.wait_ge(self.scored, BT * t + k + 1)
        dve.tensor_reduce(self.top[:, k, :], self.scores(k), AX.X, ALU.max).then_inc(self.top_done, 1)
        dve.wait_ge(self.top_done, BT * t + k + 1)
        if not first(t):
            job = self.read_job[k]
            dve.wait_ge(self.ring.full_of(job), self.ring.filled(job, t - 1))
        dve.tensor_tensor(self.e[:, k], self.scores(k), wide(self.top[:, k, :], 2, SEQ), ALU.subtract)\
           .then_inc(self.less_done, 1)

    def exp(self, act, t, k):
        act.wait_ge(self.less_done, BT * t + k + 1)
        act.activation(self.e[:, k], self.e[:, k], ACT.Exp).then_inc(self.exp_done, 1)

    def sums(self, dve, t, k):
        dve.wait_ge(self.exp_done, BT * t + k + 1)
        dve.tensor_reduce(self.total[:, k, :], self.e[:, k], AX.X, ALU.add).then_inc(self.total_done, 1)
        dve.wait_ge(self.total_done, BT * t + k + 1)
        dve.reciprocal(self.inverse[:, k, :], self.total[:, k, :]).then_inc(self.inverse_done, 1)

    def divide(self, pool, t, k):
        pool.wait_ge(self.inverse_done, BT * t + k + 1)
        pool.tensor_tensor(self.e[:, k], self.e[:, k], wide(self.inverse[:, k, :], 2, SEQ), ALU.mult)\
            .then_inc(self.ready, 1)


def turn_probabilities(pe, core, soft, ring, t, k):
    pe.wait_ge(soft.ready, BT * t + k + 1)
    for i in range(2):
        job = f"pt{k}{i}"
        pe_wait_free(pe, ring, job, t)
        for q in range(4):
            pair = 4 * i + q
            done = pe.transpose(core.psum[:, ring.bank(job), q * P:(q + 1) * P],
                                soft.e[:, k, 2 * pair:2 * pair + 2, :], core.col("ident"))
        done.then_inc(ring.full_of(job), 1)


def keep_probabilities(act, core, ring, pt, t, k):
    for i in range(2):
        job = f"pt{k}{i}"
        act.wait_ge(ring.full_of(job), ring.filled(job, t))
        act.activation(pt[:, k, 4 * i:4 * i + 4, :], core.psum[:, ring.bank(job), :], ACT.Copy)\
           .then_inc(ring.empty_of(job), 1)


def output_high(act, core, ring, job, dst, src, done, t):
    act.wait_ge(ring.full_of(job), ring.filled(job, t))
    act.activation(dst, src, ACT.Copy).then_inc(done, 1)


def output_low(dve, core, ring, job, dst, src, high, done, count, t):
    dve.wait_ge(done, count)
    dve.tensor_tensor(dst, src, f32(high), ALU.subtract).then_inc(ring.empty_of(job), 1)


def copy_context(dve, core, ring, after, buf, sem, t):
    if not first(t):
        dve.wait_ge(ring.full_of(after), ring.filled(after, t - 1))
    for dst, src in zip(buf, (core.ctx_h, core.ctx_l)):
        dve.tensor_scalar(dst[:, :], f32(src[:, block_tokens(t)]), 1.0, None, ALU.mult).then_inc(sem, 1)


def setup(core):
    nc, dram = core.nc, core.dram
    place = core.placer(0)
    raw_w = place("raw_w", [P, WCOLS[0]])
    raw_ctx = place("raw_ctx", [P, TILES, CTX])
    mask8 = place("mask8", [2, TILES, SEQ // 4], I32)
    maskf = place("maskf", [2, TILES, SEQ])
    types = place("types", [P, 2, TILES], I32)
    typef = place("typef", [P, 2, TILES])
    pos = place("pos", [SEQ, P], I32)
    posf = place("posf", [SEQ, 3, P])
    onehot = place("onehot", [SEQ, P])
    loaded, tables, landed = core.sem("loaded"), core.sem("tables"), [core.sem(f"w0_landed{c}") for c in range(6)]
    x_landed = core.sem("x_landed")
    turned, kept = core.sem("ctx_turned"), core.sem("ctx_kept")
    w_high, ctx_high, steps, rope_done = core.sem("w0_high"), core.sem("ctx_high"), core.sem("setup_steps"), core.sem("rope_done")
    tanh_done, zeroed, sel_done = core.sem("tanh_done"), core.sem("pad_zeroed"), core.sem("sel_done")
    n_chunks = 6
    wc = WCOLS[0] // n_chunks
    GROUPS = 4
    per = TILES // GROUPS
    h, l = core.weights[0]

    with nc.Block() as block:
        @block.sync
        def _(sp):
            sp.dma_start(raw_ctx[:, :, :], dram["ctx"].rearrange("(t p) e -> p t e", p=P)).then_inc(loaded, 16)
            sp.dma_start(core.cols[:, :], dram["cols"]).then_inc(tables, 16)
            sp.dma_start(core.x[:, 0:TILES, :], dram["x"].rearrange("(t p) d -> p t d", p=P)).then_inc(x_landed, 16)
            for c in range(n_chunks):
                sp.dma_start(raw_w[:, c * wc:(c + 1) * wc], dram["w0"][:, c * wc:(c + 1) * wc]).then_inc(landed[c], 16)
            sp.wait_ge(x_landed, 16)

        @block.gpsimd
        def _(pool):
            pool.memset(core.x[:, TILES:TILES + BT, :], 0.0).then_inc(core.begun, 1)
            pool.memset(core.spare[:, :], 0.0).then_inc(zeroed, 1)
            pool.memset(core.vm[:, TILES:TILES + BT], 0.0).then_inc(zeroed, 1)
            pool.memset(core.not_vm[:, TILES:TILES + BT], 0.0).then_inc(zeroed, 1)
            pool.wait_ge(tables, 16 * 4)
            pool.tensor_copy(core.ident_b[:, :], core.col("ident")).then_inc(zeroed, 1)
            pool.tensor_copy(core.causal[:, :], core.col("causal")).then_inc(zeroed, 1)
            pool.tensor_copy(core.batch_sel[:, :], core.col("batch_sel", 2)).then_inc(zeroed, 1)

        @block.tensor
        def _(pe):
            pe.wait_ge(loaded, 16)
            pe.wait_ge(tables, 16 * 4)
            for g in range(GROUPS):
                for i in range(per):
                    done = pe.transpose(core.psum[:, g, i * P:(i + 1) * P], raw_ctx[:, g * per + i, :], core.col("ident"))
                done.then_inc(turned, 1)
            pe.wait_ge(rope_done, 1)
            pe.matmul(core.psum[:, 4, 0:32], onehot[:, :], core.col("cossin", SEQ), start=True, stop=True).then_inc(turned, 1)

        @block.scalar
        def _(act):
            act.dma_start(mask8[:, :, :], dram["ctx_mask"]).then_inc(tables, 16)
            act.dma_start(types[:, :, :], dram["types"]).then_inc(tables, 16)
            act.dma_start(pos[:, :], dram["pos"]).then_inc(tables, 16)
            act.wait_ge(tables, 16 * 4)
            a = COLS["gate0"][0]
            act.activation(core.gates[:, :], core.cols[:, a:a + 4], ACT.Tanh).then_inc(tanh_done, 1)
            for g in range(GROUPS):
                act.wait_ge(turned, g + 1)
                act.activation(core.ctx_h[:, g * per * P:(g + 1) * per * P], core.psum[:, g, :], ACT.Copy).then_inc(ctx_high, 1)
            for c in range(n_chunks):
                act.wait_ge(landed[c], 16)
                act.activation(h[:, c * wc:(c + 1) * wc], raw_w[:, c * wc:(c + 1) * wc], ACT.Copy).then_inc(w_high, 1)

        @block.vector
        def _(dve):
            n = 0

            def chained(ins):
                nonlocal n
                n += 1
                ins.then_inc(steps, 1)
                dve.wait_ge(steps, n)

            dve.wait_ge(tables, 16 * 4)
            chained(dve.tensor_copy(posf[:, 0, :], pos[:, :]))
            chained(dve.tensor_scalar(posf[:, 1, :], posf[:, 0, :], 0.0, float(SEQ), ALU.is_lt, ALU.mult))
            chained(dve.tensor_tensor(posf[:, 2, :], posf[:, 1, :], posf[:, 0, :], ALU.add))
            chained(dve.tensor_scalar(posf[:, 0, :], posf[:, 2, :], 0.0, float(SEQ - 1), ALU.max, ALU.min))
            dve.tensor_scalar(onehot[:, :], posf[:, 0, :], core.col("tcol", SEQ), None, ALU.is_equal).then_inc(rope_done, 1)
            chained(dve.tensor_copy(maskf[:, :, :], mask8[:, :, :].bitcast(U8)))
            dve.tensor_scalar(core.mask_row[:, :, :], maskf[:, :, :], -1.0, -MASKED, ALU.add, ALU.mult).then_inc(sel_done, 1)
            chained(dve.tensor_copy(typef[:, :, :], types[:, :, :]))
            chained(dve.tensor_scalar(typef[:, :, :], typef[:, :, :], 1.0, None, ALU.is_equal))
            chained(dve.tensor_tensor(core.vm[:, 0:TILES], typef[:, 0, :], typef[:, 1, :], ALU.mult))
            dve.tensor_scalar(core.not_vm[:, 0:TILES], core.vm[:, 0:TILES], -1.0, 1.0, ALU.mult, ALU.add).then_inc(sel_done, 1)
            for g in range(GROUPS):
                part = slice(g * per * P, (g + 1) * per * P)
                dve.wait_ge(ctx_high, g + 1)
                dve.tensor_tensor(core.ctx_l[:, part], core.psum[:, g, :], f32(core.ctx_h[:, part]), ALU.subtract).then_inc(kept, 1)
            dve.wait_ge(turned, GROUPS + 1)
            dve.tensor_copy(core.rope[:, :], core.psum[:, 4, 0:32]).then_inc(kept, 1)
            for c in range(n_chunks):
                part = slice(c * wc, (c + 1) * wc)
                dve.wait_ge(w_high, c + 1)
                dve.tensor_tensor(l[:, part], raw_w[:, part], f32(h[:, part]), ALU.subtract).then_inc(kept, 1)


def gated_attention(core, n, gate):
    nc, psum = core.nc, core.psum
    place = core.placer(n)
    xn = place("xn", [P, BT, 1, D])
    y = place("y", [P, DC, BLK])
    xh = place("xh", [P, DC, BLK], F32R)
    xl = place("xl", [P, DC, BLK], F32R)
    ch_b = place("ctx_block_h", [P, BLK], F32R)
    cl_b = place("ctx_block_l", [P, BLK], F32R)
    q = place("q", [P, PAIRS, BLK])
    keys = place("keys", [P, PAIRS, BB, 2, SEQ])
    vals = place("vals", [P, PAIRS, BB, 2, SEQ])
    pt = place("pt", [P, BT, PAIRS, P])
    oh = place("oh", [P, PAIRS, BLK], F32R)
    ol = place("ol", [P, PAIRS, BLK], F32R)
    ring1 = Ring(core, f"a{n}", (4, 5),
                 [("xt", 1)] + [(f"k{i}", 2) for i in range(4)] + [(f"q{i}", 1) for i in range(4)]
                 + [(f"v{k}{i}", 2) for k in range(BT) for i in range(2)])
    ring2 = Ring(core, f"o{n}", (6, 7),
                 [(f"{w}{k}{i}", 1) for k in range(BT) for w in ("pt", "av") for i in range(2)] + [("wo", 1)])
    wk, wv, wq, wo = (core.weight(n, w) for w in ("wk", "wv", "wq", "wo"))
    wq = [w.rearrange("p (c m) -> p c m", c=DC) for w in wq]
    wo = [w.rearrange("p (c m) -> p c m", c=PAIRS) for w in wo]
    norm = Norm(core, n, "layer", "eps5", xn, ring1, "xt")
    turned = Turned(core, n, norm, ring1, ["xt"], y, xh, xl, f"g{n}", f"b{n}")
    soft = Softmax(core, n, place, ring2, ["pt01", "pt11"])
    following = NextWeights(core, n + 1)
    copied, out_high, cleared, stored = (core.sem(f"{s}{n}") for s in ("copied", "out_high", "cleared", "residual"))

    with nc.Block() as block:
        @block.sync
        def _(sp):
            sweep(sp, lambda: following.load(sp, 0), lambda u: following.load(sp, u), lambda: None)

        @block.gpsimd
        def _(pool):
            pool.memset(keys[:, :, :, :, :], 0.0).then_inc(cleared, 1)

            def late(t):
                soft.divide(pool, t, 0)
                soft.divide(pool, t, 1)
                following.split(pool, t, cleared)

            def head():
                norm.invert(pool, 0)
                norm.invert(pool, 1)
                late(0)

            def step(u):
                norm.invert(pool, u + 1)
                late(u)

            sweep(pool, head, step, lambda: None)

        @block.tensor
        def _(pe):
            def project_keys(t):
                for i in range(4):
                    job = f"k{i}"
                    pe_wait_free(pe, ring1, job, t)
                    for s in range(2):
                        m = slice((2 * i + s) * P, (2 * i + s + 1) * P)
                        done = three(pe, psum[:, ring1.bank(job), s * BLK:(s + 1) * BLK], [w[:, m] for w in wk],
                                     [core.ctx_h[:, block_tokens(t)], core.ctx_l[:, block_tokens(t)]], True, True)
                    done.then_inc(ring1.full_of(job), 1)

            def project_queries(t):
                pe.wait_ge(turned.split_done, t + 1)
                for i in range(4):
                    job = f"q{i}"
                    pe_wait_free(pe, ring1, job, t)
                    for s in range(2):
                        m = slice((2 * i + s) * P, (2 * i + s + 1) * P)
                        for c in range(DC):
                            done = three(pe, psum[:, ring1.bank(job), s * BLK:(s + 1) * BLK], [w[:, c, m] for w in wq],
                                         [xh[:, c, :], xl[:, c, :]], c == 0, c == DC - 1)
                    done.then_inc(ring1.full_of(job), 1)

            def project_values(t):
                pe.wait_ge(copied, 2 * t + 2)
                for k in range(BT):
                    for i in range(2):
                        job = f"v{k}{i}"
                        pe_wait_free(pe, ring1, job, t)
                        three(pe, psum[:, ring1.bank(job), :], [b[:, k * P:(k + 1) * P] for b in (ch_b, cl_b)],
                              [w[:, i * 512:(i + 1) * 512] for w in wv], True, True).then_inc(ring1.full_of(job), 1)

            def score(t):
                for job in ("q2", "q3", "k3"):
                    pe.wait_ge(ring1.empty_of(job), ring1.drained(job, t))
                for k in range(BT):
                    for half in range(2):
                        bank = 2 * k + half
                        if not first(t):
                            pe.wait_ge(core.begun, 1)
                            pe.wait_ge(soft.less_done, BT * t - BT + k + 1)
                        pe.matmul(psum[:, bank, :], core.batch_sel[:, :],
                                  wide(core.mask_row[:, bass.ds(BT * t + k, 1), :].squeeze(1), 1, 8),
                                  start=True, stop=False, skip_group_check=True)
                        for pair in range(4):
                            pr = 4 * half + pair
                            for b in range(2):
                                done = pe.matmul(psum[64 * b:64 * b + 64, bank, pair * P:(pair + 1) * P],
                                                 q[:, pr, (2 * k + b) * SEQ:(2 * k + b + 1) * SEQ],
                                                 keys[:, pr, 2 * k + b, :, :], start=False, stop=True, skip_group_check=True)
                    done.then_inc(soft.scored, 1)

            def weigh(t, k):
                pe.wait_ge(ring1.empty_of("v11"), ring1.drained("v11", t))
                pe.wait_ge(ring1.empty_of("v10"), ring1.drained("v10", t))
                for i in range(2):
                    job = f"av{k}{i}"
                    for w in (f"pt{k}{i}",):
                        pe.wait_ge(ring2.empty_of(w), ring2.drained(w, t))
                    pe_wait_free(pe, ring2, job, t)
                    for s in range(4):
                        pair = 4 * i + s
                        for b in range(2):
                            done = pe.matmul(psum[:, ring2.bank(job), s * P + b * SEQ:s * P + (b + 1) * SEQ],
                                             vals[:, pair, 2 * k + b, :, :], pt[:, k, pair, b * SEQ:(b + 1) * SEQ],
                                             start=True, stop=True)
                    done.then_inc(ring2.full_of(job), 1)

            def project_out(t):
                for job in ("av10", "av11"):
                    pe.wait_ge(ring2.empty_of(job), ring2.drained(job, t))
                pe_wait_free(pe, ring2, "wo", t)
                for k in range(BT):
                    for c in range(PAIRS):
                        done = three(pe, psum[:, ring2.bank("wo"), k * D:(k + 1) * D],
                                     [o[:, c, k * P:(k + 1) * P] for o in (oh, ol)], [w[:, c, :] for w in wo],
                                     c == 0, c == PAIRS - 1)
                done.then_inc(ring2.full_of("wo"), 1)

            def front(t):
                turned.transpose(pe, t)
                project_keys(t)
                project_queries(t)
                score(t)

            def middle(t):
                for k in range(BT):
                    turn_probabilities(pe, core, soft, ring2, t, k)
                    weigh(t, k)

            def head():
                pe.wait_ge(cleared, 2)
                front(0)
                project_values(0)

            def step(u):
                front(u)
                middle(u - 1)
                project_values(u)
                project_out(u - 1)

            def tail():
                middle(NB - 1)
                project_out(NB - 1)

            sweep(pe, head, step, tail)

        def keep_keys(eng_copy, s, t):
            for i in range(4):
                job = f"k{i}"
                eng_copy(job, ring1.filled(job, t),
                         keys[64 * s:64 * s + 64, 2 * i:2 * i + 2, :, s, :],
                         psum[64 * s:64 * s + 64, ring1.bank(job), :].rearrange("p (a b j) -> p a b j", a=2, b=BB))

        def keep_values(eng_copy, b, t):
            for k in range(BT):
                for i in range(2):
                    job = f"v{k}{i}"
                    src = psum[64 * b:64 * b + 64, ring1.bank(job), :].rearrange("p (a s d) -> p a s d", a=4, s=2)
                    for s in range(2):
                        eng_copy(job, ring1.filled(job, t) if s == 0 else None,
                                 vals[64 * s:64 * s + 64, 4 * i:4 * i + 4, 2 * k + b, s, :], src[:, :, s, :], s == 1)

        @block.scalar
        def _(act):
            def copy(job, full, dst, src, last=True):
                if full is not None:
                    act.wait_ge(ring1.full_of(job), full)
                done = act.activation(dst, src, ACT.Copy)
                if last:
                    done.then_inc(ring1.empty_of(job), 1)

            def front(t):
                turned.scale(act, t)
                keep_keys(copy, 0, t)
                for i in range(4):
                    job = f"q{i}"
                    act.wait_ge(ring1.full_of(job), ring1.filled(job, t))
                    act.activation(q[:, 2 * i:2 * i + 2, :], psum[:, ring1.bank(job), :], ACT.Copy, scale=0.125)\
                       .then_inc(ring1.empty_of(job), 1)

            def outputs(t, k):
                keep_probabilities(act, core, ring2, pt, t, k)
                for i in range(2):
                    job = f"av{k}{i}"
                    output_high(act, core, ring2, job, oh[:, 4 * i:4 * i + 4, k * P:(k + 1) * P],
                                psum[:, ring2.bank(job), :].rearrange("p (a t) -> p a t", a=4), out_high, t)

            def head():
                act.wait_ge(cleared, 2)
                front(0)
                soft.exp(act, 0, 0)
                soft.exp(act, 0, 1)
                keep_values(copy, 0, 0)

            def step(u):
                front(u)
                for k in range(BT):
                    outputs(u - 1, k)
                    soft.exp(act, u, k)
                keep_values(copy, 0, u)

            def tail():
                for k in range(BT):
                    outputs(NB - 1, k)

            sweep(act, head, step, tail)

        @block.vector
        def _(dve):
            def copy(job, full, dst, src, last=True):
                if full is not None:
                    dve.wait_ge(ring1.full_of(job), full)
                done = dve.tensor_copy(dst, src)
                if last:
                    done.then_inc(ring1.empty_of(job), 1)

            def outputs(t, k):
                for i in range(2):
                    job = f"av{k}{i}"
                    high = oh[:, 4 * i:4 * i + 4, k * P:(k + 1) * P]
                    output_low(dve, core, ring2, job, ol[:, 4 * i:4 * i + 4, k * P:(k + 1) * P],
                               psum[:, ring2.bank(job), :].rearrange("p (a t) -> p a t", a=4), high, out_high,
                               4 * t + 2 * k + i + 1, t)

            def residual(t):
                dve.wait_ge(ring2.full_of("wo"), ring2.filled("wo", t))
                rows = core.x[:, block_tiles(t), :]
                dve.scalar_tensor_tensor(rows, psum[:, ring2.bank("wo"), :].rearrange("p (k d) -> p k d", k=BT), gate,
                                         rows, ALU.mult, ALU.add).then_inc(ring2.empty_of("wo"), 1)

            def front(t):
                turned.split(dve, t)
                norm.stats(dve, t + 1)
                copy_context(dve, core, ring1, "v11", (ch_b, cl_b), copied, t)
                keep_keys(copy, 1, t)

            def head():
                dve.memset(vals[:, :, :, :, :], 0.0).then_inc(cleared, 1)
                norm.stats(dve, 0)
                norm.normalise(dve, 0)
                dve.wait_ge(cleared, 2)
                front(0)
                for k in range(BT):
                    soft.less_top(dve, 0, k)
                for k in range(BT):
                    soft.sums(dve, 0, k)
                keep_values(copy, 1, 0)
                norm.normalise(dve, 1)

            def step(u):
                front(u)
                soft.less_top(dve, u, 0)
                outputs(u - 1, 0)
                soft.less_top(dve, u, 1)
                soft.sums(dve, u, 0)
                outputs(u - 1, 1)
                soft.sums(dve, u, 1)
                keep_values(copy, 1, u)
                residual(u - 1)
                norm.normalise(dve, u + 1)

            def tail():
                for k in range(BT):
                    outputs(NB - 1, k)
                residual(NB - 1)

            sweep(dve, head, step, tail)


def feed_forward(core, n, gate, last):
    nc, psum = core.nc, core.psum
    place = core.placer(n)
    xn = place("xn", [P, BT, 1, D])
    y = place("y", [P, DC, BLK])
    xh = place("xh", [P, DC, BLK], F32R)
    xl = place("xl", [P, DC, BLK], F32R)
    FT = FF // P
    hid = place("hid", [P, FT, BLK])
    hh = place("hid_h", [P, FT, BLK], F32R)
    hl = place("hid_l", [P, FT, BLK], F32R)
    ring = Ring(core, f"f{n}", tuple(range(6)), [("xt", 1)] + [(f"h{i}", 1) for i in range(4)] + [("w2", 1)])
    w1 = [w.rearrange("p (c m) -> p c m", c=DC) for w in core.weight(n, "w1")]
    w2 = [w.rearrange("p (c m) -> p c m", c=FT) for w in core.weight(n, "w2")]
    norm = Norm(core, n, "layer", "eps5", xn, ring, "xt")
    turned = Turned(core, n, norm, ring, ["xt"], y, xh, xl, f"g{n}", f"b{n}")
    following = NextWeights(core, n + 1)
    hid_high, hid_low, started, stored = (core.sem(f"{s}{n}") for s in ("hid_high", "hid_low", "started", "stored"))
    out = core.out.rearrange("(t p) d -> p t d", p=P)

    with nc.Block() as block:
        @block.sync
        def _(sp):
            def store(t):
                if last:
                    sp.wait_ge(ring.empty_of("w2"), ring.drained("w2", t))
                    sp.dma_start(out[:, block_tiles(t), :], core.x[:, block_tiles(t), :]).then_inc(stored, 16)

            def step(u):
                following.load(sp, u)
                store(u - 1)

            sweep(sp, lambda: following.load(sp, 0), step, lambda: store(NB - 1))
            if last:
                sp.wait_ge(stored, 16 * NB)

        @block.gpsimd
        def _(pool):
            pool.memset(core.ve[:, 0, :], 0.0).then_inc(started, 1)

            def head():
                norm.invert(pool, 0)
                norm.invert(pool, 1)
                following.split(pool, 0, started)

            def step(u):
                norm.invert(pool, u + 1)
                following.split(pool, u, started)

            sweep(pool, head, step, lambda: None)

        @block.tensor
        def _(pe):
            def up(t):
                pe.wait_ge(turned.split_done, t + 1)
                for i in range(4):
                    job = f"h{i}"
                    pe_wait_free(pe, ring, job, t)
                    for s in range(2):
                        m = slice((2 * i + s) * P, (2 * i + s + 1) * P)
                        for c in range(DC):
                            done = three(pe, psum[:, ring.bank(job), s * BLK:(s + 1) * BLK], [w[:, c, m] for w in w1],
                                         [xh[:, c, :], xl[:, c, :]], c == 0, c == DC - 1)
                    done.then_inc(ring.full_of(job), 1)

            def down(t):
                pe_wait_free(pe, ring, "w2", t)
                for k in range(BT):
                    for c in range(FT):
                        if k == 0 and c % 2 == 0:
                            pe.wait_ge(hid_low, 4 * t + c // 2 + 1)
                        done = three(pe, psum[:, ring.bank("w2"), k * D:(k + 1) * D],
                                     [g[:, c, k * P:(k + 1) * P] for g in (hh, hl)], [w[:, c, :] for w in w2],
                                     c == 0, c == FT - 1)
                done.then_inc(ring.full_of("w2"), 1)

            def head():
                turned.transpose(pe, 0)
                up(0)

            def step(u):
                turned.transpose(pe, u)
                down(u - 1)
                up(u)

            sweep(pe, head, step, lambda: down(NB - 1))

        @block.scalar
        def _(act):
            def step(t):
                turned.scale(act, t)
                for i in range(4):
                    job = f"h{i}"
                    act.wait_ge(ring.full_of(job), ring.filled(job, t))
                    if not first(t):
                        act.wait_ge(hid_low, 4 * t - 4 + i + 1)
                    act.activation(hid[:, 2 * i:2 * i + 2, :], psum[:, ring.bank(job), :], ACT.Gelu).then_inc(ring.empty_of(job), 1)

            sweep(act, lambda: step(0), step, lambda: None)

        @block.vector
        def _(dve):
            def split_hidden(t):
                for i in range(4):
                    job, part = f"h{i}", slice(2 * i, 2 * i + 2)
                    dve.wait_ge(ring.empty_of(job), ring.drained(job, t))
                    dve.tensor_copy(hh[:, part, :], hid[:, part, :]).then_inc(hid_high, 1)
                    dve.wait_ge(hid_high, 4 * t + i + 1)
                    dve.tensor_tensor(hl[:, part, :], hid[:, part, :], f32(hh[:, part, :]), ALU.subtract).then_inc(hid_low, 1)

            def residual(t):
                dve.wait_ge(ring.full_of("w2"), ring.filled("w2", t))
                rows = core.x[:, block_tiles(t), :]
                dve.scalar_tensor_tensor(rows, psum[:, ring.bank("w2"), :].rearrange("p (k d) -> p k d", k=BT), gate,
                                         rows, ALU.mult, ALU.add).then_inc(ring.empty_of("w2"), 1)

            def head():
                norm.stats(dve, 0)
                norm.normalise(dve, 0)
                turned.split(dve, 0)
                norm.stats(dve, 1)
                norm.normalise(dve, 1)
                split_hidden(0)

            def step(u):
                turned.split(dve, u)
                norm.stats(dve, u + 1)
                residual(u - 1)
                norm.normalise(dve, u + 1)
                split_hidden(u)

            sweep(dve, head, step, lambda: residual(NB - 1))


def memory_gate(core, n):
    nc, psum = core.nc, core.psum
    place = core.placer(n)
    rows = place("rows", [P, BT, D])
    y = place("y", [P, DC, BLK])
    xh, xl = (place(s, [P, DC, BLK], F32R) for s in ("xh", "xl"))
    ch_b, cl_b = (place(s, [P, BLK], F32R) for s in ("ctx_block_h", "ctx_block_l"))
    mem_t = place("mem_t", [P, DC, BLK])
    mem = place("mem", [P, BT, D])
    e = place("e", [P, BT, SEQ])
    top, total, inverse = (place(s, [P, BT]) for s in ("top", "total", "inverse"))
    prob = place("prob", [P, BT, 2, SEQ])
    pt = place("pt", [P, BT, P])
    ct_h, ct_l = (place(s, [P, DC, BLK], F32R) for s in ("ct_h", "ct_l"))
    z, ez, ez1, g, gc, fused = (place(s, [P, BT, D]) for s in ("z", "ez", "ez1", "g", "gc", "fused"))
    ring1 = Ring(core, "m1_", (0, 1, 2, 3), [("xt", 1), ("mt", 1), ("mp", 1), ("sc", 1)])
    ring2 = Ring(core, "m2_", (4, 5, 6, 7), [("pt", 1), ("ct", 1), ("cx", 1), ("gt", 1)])
    wm = core.weight(n, "wm")
    wg = [w.rearrange("p (c m) -> p c m", c=4) for w in core.weight(n, "wg")]
    norm = Norm(core, n, "rms", "eps6", None, ring1, "xt")
    following = NextWeights(core, n + 1)
    sems = ("copied", "rows_ready", "x_high", "x_split", "top_done", "exp_done", "total_done", "inverse_done", "prob_ready",
            "ct_high", "exp_gate", "gate_steps", "fused_done", "zeroed")
    (copied, rows_ready, x_high, x_split, top_done, exp_done, total_done, inverse_done, prob_ready,
     ct_high, exp_gate, gate_steps, fused_done, zeroed) = (core.sem(f"m_{s}") for s in sems)
    tile = lambda k: slice(k * P, (k + 1) * P)
    banked = lambda ring, job, k=BT: psum[:, ring.bank(job), :].rearrange("p (k d) -> p k d", k=k)

    with nc.Block() as block:
        @block.sync
        def _(sp):
            sweep(sp, lambda: following.load(sp, 0), lambda u: following.load(sp, u), lambda: None)

        @block.gpsimd
        def _(pool):
            pool.memset(prob[:, :, :, :], 0.0).then_inc(zeroed, 1)

            def step(u):
                norm.invert(pool, u - 1)
                following.split(pool, u, zeroed)

            sweep(pool, lambda: following.split(pool, 0, zeroed), step, lambda: norm.invert(pool, NB - 1))

        @block.tensor
        def _(pe):
            def turn_rows(t):
                pe.wait_ge(rows_ready, t + 1)
                pe_wait_free(pe, ring1, "xt", t)
                for c in range(DC):
                    for k in range(BT):
                        done = pe.transpose(psum[:, ring1.bank("xt"), (c * BT + k) * P:(c * BT + k + 1) * P],
                                            rows[:, k, c * P:(c + 1) * P], core.col("ident"))
                done.then_inc(ring1.full_of("xt"), 1)

            def memory_turned(t):
                pe_wait_free(pe, ring1, "mt", t)
                for c in range(DC):
                    done = three(pe, psum[:, ring1.bank("mt"), c * BLK:(c + 1) * BLK], [w[:, tile(c)] for w in wm],
                                 [core.ctx_h[:, block_tokens(t)], core.ctx_l[:, block_tokens(t)]], True, True)
                done.then_inc(ring1.full_of("mt"), 1)

            def memory(t):
                pe.wait_ge(copied, 2 * t + 2)
                pe_wait_free(pe, ring1, "mp", t)
                for k in range(BT):
                    done = three(pe, psum[:, ring1.bank("mp"), k * D:(k + 1) * D], [b[:, tile(k)] for b in (ch_b, cl_b)], wm, True, True)
                done.then_inc(ring1.full_of("mp"), 1)

            def score(t):
                for job in ("xt", "mt"):
                    pe.wait_ge(ring1.empty_of(job), ring1.drained(job, t))
                pe_wait_free(pe, ring1, "sc", t)
                for k in range(BT):
                    for c in range(DC):
                        for b in range(2):
                            at = slice((2 * k + b) * SEQ, (2 * k + b + 1) * SEQ)
                            done = pe.matmul(psum[64 * b:64 * b + 64, ring1.bank("sc"), k * SEQ:(k + 1) * SEQ],
                                             y[:, c, at], mem_t[:, c, at], start=c == 0, stop=c == DC - 1)
                done.then_inc(ring1.full_of("sc"), 1)

            def turn_prob(t):
                pe.wait_ge(prob_ready, 2 * t + 2)
                pe_wait_free(pe, ring2, "pt", t)
                for k in range(BT):
                    done = pe.transpose(psum[:, ring2.bank("pt"), tile(k)], prob[:, k, :, :], core.col("ident"))
                done.then_inc(ring2.full_of("pt"), 1)

            def weigh(t):
                pe.wait_ge(ring2.empty_of("pt"), ring2.drained("pt", t))
                pe.wait_ge(ring1.empty_of("mp"), ring1.drained("mp", t))
                pe_wait_free(pe, ring2, "ct", t)
                for c in range(DC):
                    for k in range(BT):
                        done = pe.matmul(psum[:, ring2.bank("ct"), c * BLK + k * P:c * BLK + (k + 1) * P],
                                         mem[:, k, tile(c)], pt[:, k, :], start=True, stop=True)
                done.then_inc(ring2.full_of("ct"), 1)
                pe_wait_free(pe, ring2, "cx", t)
                for k in range(BT):
                    done = pe.matmul(psum[:, ring2.bank("cx"), k * D:(k + 1) * D], pt[:, k, :], mem[:, k, :], start=True, stop=True)
                done.then_inc(ring2.full_of("cx"), 1)

            def gate(t):
                pe.wait_ge(x_split, t + 1)
                pe_wait_free(pe, ring2, "gt", t)
                pe.wait_ge(ring2.empty_of("ct"), ring2.drained("ct", t))
                for k in range(BT):
                    for c in range(4):
                        parts = (xh, xl) if c < DC else (ct_h, ct_l)
                        done = three(pe, psum[:, ring2.bank("gt"), k * D:(k + 1) * D], [p[:, c % DC, tile(k)] for p in parts],
                                     [w[:, c, :] for w in wg], c == 0, c == 3)
                done.then_inc(ring2.full_of("gt"), 1)

            def head():
                pe.wait_ge(zeroed, 1)
                turn_rows(0)
                memory_turned(0)
                memory(0)
                score(0)

            def step(u):
                turn_prob(u - 1)
                turn_rows(u)
                memory_turned(u)
                weigh(u - 1)
                memory(u)
                gate(u - 1)
                score(u)

            def tail():
                turn_prob(NB - 1)
                weigh(NB - 1)
                gate(NB - 1)

            sweep(pe, head, step, tail)

        @block.scalar
        def _(act):
            def keep(ring, job, dst, src, t, done=None):
                act.wait_ge(ring.full_of(job), ring.filled(job, t))
                act.activation(dst, src, ACT.Copy).then_inc(ring.empty_of(job) if done is None else done, 1)

            def keep_y(t):
                if not first(t):
                    act.wait_ge(x_split, t)
                keep(ring1, "xt", y[:, :, :], banked(ring1, "xt"), t)

            def soft(t):
                act.wait_ge(ring1.empty_of("sc"), ring1.drained("sc", t))
                act.activation(e[:, :, :], e[:, :, :], ACT.Exp, scale=1.0 / 16).then_inc(exp_done, 1)

            def gate(t):
                act.wait_ge(ring2.empty_of("gt"), ring2.drained("gt", t))
                act.activation(ez[:, :, :], z[:, :, :], ACT.Exp, scale=-1.0).then_inc(exp_gate, 1)

            def head():
                keep_y(0)
                keep(ring1, "mt", mem_t[:, :, :], banked(ring1, "mt"), 0)
                keep(ring1, "mp", mem[:, :, :], banked(ring1, "mp"), 0)
                soft(0)

            def step(u):
                keep(ring2, "pt", pt[:, :, :], psum[:, ring2.bank("pt"), 0:BLK].rearrange("p (k t) -> p k t", k=BT), u - 1)
                keep_y(u)
                keep(ring1, "mt", mem_t[:, :, :], banked(ring1, "mt"), u)
                keep(ring2, "ct", ct_h[:, :, :], banked(ring2, "ct"), u - 1, ct_high)
                keep(ring1, "mp", mem[:, :, :], banked(ring1, "mp"), u)
                soft(u)
                gate(u - 1)

            def tail():
                keep(ring2, "pt", pt[:, :, :], psum[:, ring2.bank("pt"), 0:BLK].rearrange("p (k t) -> p k t", k=BT), NB - 1)
                keep(ring2, "ct", ct_h[:, :, :], banked(ring2, "ct"), NB - 1, ct_high)
                gate(NB - 1)

            sweep(act, head, step, tail)

        @block.vector
        def _(dve):
            def bring_rows(t):
                if not first(t):
                    dve.wait_ge(ring1.full_of("xt"), ring1.filled("xt", t - 1))
                dve.tensor_scalar(rows[:, :, :], core.x[:, block_tiles(t), :], 1.0, None, ALU.mult).then_inc(rows_ready, 1)

            def split_rows(t):
                dve.wait_ge(ring1.empty_of("xt"), ring1.drained("xt", t))
                if not first(t):
                    dve.wait_ge(ring2.full_of("gt"), ring2.filled("gt", t - 1))
                dve.tensor_copy(xh[:, :, :], y[:, :, :]).then_inc(x_high, 1)
                dve.wait_ge(x_high, t + 1)
                dve.tensor_tensor(xl[:, :, :], y[:, :, :], f32(xh[:, :, :]), ALU.subtract).then_inc(x_split, 1)

            def split_weighted(t):
                dve.wait_ge(ct_high, t + 1)
                dve.tensor_tensor(ct_l[:, :, :], banked(ring2, "ct"), f32(ct_h[:, :, :]), ALU.subtract).then_inc(ring2.empty_of("ct"), 1)

            def soft(t):
                scores = psum[:, ring1.bank("sc"), 0:BT * SEQ].rearrange("p (k j) -> p k j", k=BT)
                dve.wait_ge(ring1.full_of("sc"), ring1.filled("sc", t))
                dve.tensor_reduce(top[:, :], scores, AX.X, ALU.max).then_inc(top_done, 1)
                dve.wait_ge(top_done, t + 1)
                dve.tensor_tensor(e[:, :, :], scores, wide(top[:, :], 2, SEQ), ALU.subtract).then_inc(ring1.empty_of("sc"), 1)
                dve.wait_ge(exp_done, t + 1)
                dve.tensor_reduce(total[:, :], e[:, :, :], AX.X, ALU.add).then_inc(total_done, 1)
                dve.wait_ge(total_done, t + 1)
                dve.reciprocal(inverse[:, :], total[:, :]).then_inc(inverse_done, 1)
                dve.wait_ge(inverse_done, t + 1)
                for b in range(2):
                    half = slice(64 * b, 64 * b + 64)
                    dve.tensor_tensor(prob[half, :, b, :], e[half, :, :], wide(inverse[half, :], 2, SEQ), ALU.mult).then_inc(prob_ready, 1)

            def fuse(t):
                dve.wait_ge(ring2.full_of("gt"), ring2.filled("gt", t))
                dve.tensor_tensor(z[:, :, :], banked(ring2, "gt"), wide(core.col("bgate"), 1, BT), ALU.add).then_inc(ring2.empty_of("gt"), 1)
                dve.wait_ge(exp_gate, t + 1)
                dve.tensor_scalar(ez1[:, :, :], ez[:, :, :], 1.0, None, ALU.add).then_inc(gate_steps, 1)
                dve.wait_ge(gate_steps, 3 * t + 1)
                dve.reciprocal(g[:, :, :], ez1[:, :, :]).then_inc(gate_steps, 1)
                dve.wait_ge(gate_steps, 3 * t + 2)
                dve.wait_ge(ring2.full_of("cx"), ring2.filled("cx", t))
                dve.tensor_tensor(gc[:, :, :], banked(ring2, "cx"), g[:, :, :], ALU.mult).then_inc(ring2.empty_of("cx"), 1)
                dve.wait_ge(ring2.empty_of("cx"), ring2.drained("cx", t))
                dve.tensor_tensor(fused[:, :, :], gc[:, :, :], core.x[:, block_tiles(t), :], ALU.add).then_inc(gate_steps, 1)
                dve.wait_ge(gate_steps, 3 * t + 3)
                norm.stats(dve, t, fused)
                dve.wait_ge(norm.rstd_done, t + 1)
                for k in range(BT):
                    dve.scalar_tensor_tensor(core.x[:, bass.ds(BT * t + k, 1), :].squeeze(1), fused[:, k, :], core.rstd[:, k:k + 1],
                                             core.col("normw"), ALU.mult, ALU.mult).then_inc(fused_done, 1)

            def head():
                bring_rows(0)
                copy_context(dve, core, ring1, "mp", (ch_b, cl_b), copied, 0)
                split_rows(0)
                dve.wait_ge(zeroed, 1)
                soft(0)
                bring_rows(1)

            def step(u):
                copy_context(dve, core, ring1, "mp", (ch_b, cl_b), copied, u)
                split_weighted(u - 1)
                split_rows(u)
                soft(u)
                fuse(u - 1)
                bring_rows(u + 1)

            def tail():
                split_weighted(NB - 1)
                fuse(NB - 1)

            sweep(dve, head, step, tail)


def add_experts(dve, core, ring, jobs, mixed, t):
    for k, job in enumerate(jobs):
        row = core.x[:, bass.ds(BT * t + k, 1), :].squeeze(1)
        dve.wait_ge(ring.full_of(job), ring.filled(job, t))
        dve.scalar_tensor_tensor(row, psum_half(core, ring, job, 1), core.not_vm[:, bass.ds(BT * t + k, 1)], row,
                                 ALU.mult, ALU.add).then_inc(mixed, 1)
    for k, job in enumerate(jobs):
        row = core.x[:, bass.ds(BT * t + k, 1), :].squeeze(1)
        dve.wait_ge(mixed, BT * t + k + 1)
        dve.scalar_tensor_tensor(row, psum_half(core, ring, job, 0), core.vm[:, bass.ds(BT * t + k, 1)], row,
                                 ALU.mult, ALU.add).then_inc(ring.empty_of(job), 1)


def psum_half(core, ring, job, i):
    return core.psum[:, ring.bank(job), i * D:(i + 1) * D]


def self_attention(core, n):
    nc, psum = core.nc, core.psum
    place = core.placer(n)
    XC = 2 * DC
    HD = D // HEADS
    xn = place("xn", [P, BT, 2, D])
    y = place("y", [P, XC, BLK])
    xh, xl = (place(s, [P, XC, BLK], F32R) for s in ("xh", "xl"))
    by_cos, by_sin, turned_qk = (place(s, [P, BT, 2 * D]) for s in ("by_cos", "by_sin", "turned_qk"))
    q = place("q", [P, DC, BLK])
    keys = place("keys", [P, BB, DC, 8, SEQ])
    vals = place("vals", [P, BB, PAIRS, 2, HD])
    pt = place("pt", [P, BT, PAIRS, P])
    oh, ol = (place(s, [P, DC, BLK], F32R) for s in ("oh", "ol"))
    ring1 = Ring(core, "s1_", (4, 5), [("xv", 1), ("xo", 1), ("qk0", 1), ("qk1", 1), ("rt0", 2), ("rt1", 2), ("v", 2)])
    ring2 = Ring(core, "s2_", (6, 7),
                 [("pt00", 1), ("pt01", 1), ("av0", 1), ("pt10", 1), ("pt11", 1), ("av1", 1), ("d0", 1), ("d1", 1)])
    qkv = [w.rearrange("p (c m) -> p c m", c=XC) for w in core.weight(n, "qkv")]
    dense = [w.rearrange("p (c m) -> p c m", c=DC) for w in core.weight(n, "dense")]
    norm = Norm(core, n, "experts", "eps6", xn, ring1, "xo")
    turned = Turned(core, n, norm, ring1, ["xv", "xo"], y, xh, xl, f"g{n}", None)
    soft = Softmax(core, n, place, ring2, ["pt01", "pt11"])
    following = NextWeights(core, n + 1)
    rotated, out_high, cleared, mixed = (core.sem(f"{s}{n}") for s in ("rotated", "out_high", "cleared", "mixed"))
    tile = lambda k: slice(k * P, (k + 1) * P)

    with nc.Block() as block:
        @block.sync
        def _(sp):
            sweep(sp, lambda: following.load(sp, 0), lambda u: following.load(sp, u), lambda: None)

        @block.gpsimd
        def _(pool):
            pool.memset(vals[:, :, :, :, :], 0.0).then_inc(cleared, 1)

            def rotate(t):
                for k in range(BT):
                    pool.wait_ge(ring1.empty_of(f"qk{k}"), ring1.drained(f"qk{k}", t))
                    pool.tensor_tensor(turned_qk[:, k, :], by_cos[:, k, :], by_sin[:, k, :], ALU.add).then_inc(rotated, 1)

            def late(t):
                norm.invert(pool, t + 1)
                rotate(t)
                soft.divide(pool, t, 0)
                soft.divide(pool, t, 1)
                following.split(pool, t, cleared)

            def head():
                norm.invert(pool, 0)
                late(0)

            sweep(pool, head, late, lambda: None)

        @block.tensor
        def _(pe):
            def project_qk(t):
                pe.wait_ge(turned.split_done, 2 * t + 2)
                for k in range(BT):
                    job = f"qk{k}"
                    pe_wait_free(pe, ring1, job, t)
                    for c in range(XC):
                        done = three(pe, psum[:, ring1.bank(job), :], [p[:, c, tile(k)] for p in (xh, xl)],
                                     [w[:, c, 0:2 * D] for w in qkv], c == 0, c == XC - 1)
                    done.then_inc(ring1.full_of(job), 1)

            def project_values(t):
                pe_wait_free(pe, ring1, "v", t)
                for k in range(BT):
                    for c in range(XC):
                        done = three(pe, psum[:, ring1.bank("v"), k * D:(k + 1) * D], [p[:, c, tile(k)] for p in (xh, xl)],
                                     [w[:, c, 2 * D:3 * D] for w in qkv], c == 0, c == XC - 1)
                done.then_inc(ring1.full_of("v"), 1)

            def turn_qk(t):
                for k in range(BT):
                    job = f"rt{k}"
                    pe.wait_ge(rotated, BT * t + k + 1)
                    pe_wait_free(pe, ring1, job, t)
                    for i in range(4):
                        done = pe.transpose(psum[:, ring1.bank(job), tile(i)], turned_qk[:, k, tile(i)], core.col("ident"))
                    done.then_inc(ring1.full_of(job), 1)

            def score(t):
                for k in range(BT):
                    pe.wait_ge(ring1.empty_of(f"rt{k}"), ring1.drained(f"rt{k}", t))
                    if not first(t):
                        pe.wait_ge(soft.less_done, BT * t - BT + k + 1)
                    for c in range(DC):
                        bank = 2 * k + c
                        pe.matmul(psum[:, bank, :], core.ident_b[:, :], wide(core.causal[:, :], 1, 8), start=True, stop=False,
                                  skip_group_check=True)
                        for b in range(2):
                            done = pe.matmul(psum[64 * b:64 * b + 64, bank, :], q[:, c, (2 * k + b) * SEQ:(2 * k + b + 1) * SEQ],
                                             keys[:, 2 * k + b, c, :, :], start=False, stop=True, skip_group_check=True)
                    done.then_inc(soft.scored, 1)

            def weigh(t, k):
                job = f"av{k}"
                for i in range(2):
                    pe.wait_ge(ring2.empty_of(f"pt{k}{i}"), ring2.drained(f"pt{k}{i}", t))
                pe.wait_ge(ring1.empty_of("v"), ring1.drained("v", t))
                pe_wait_free(pe, ring2, job, t)
                pe.wait_ge(core.begun, 1)
                for c in range(DC):
                    for b in range(2):
                        for s in range(4):
                            done = pe.matmul(psum[32 * s:32 * s + 32, ring2.bank(job), c * P + b * SEQ:c * P + (b + 1) * SEQ],
                                             vals[:, 2 * k + b, 4 * c + s, :, :], pt[:, k, 4 * c + s, b * SEQ:(b + 1) * SEQ],
                                             start=True, stop=True)
                done.then_inc(ring2.full_of(job), 1)

            def project_out(t):
                for k in range(BT):
                    job = f"d{k}"
                    pe.wait_ge(ring2.empty_of(f"av{k}"), ring2.drained(f"av{k}", t))
                    pe_wait_free(pe, ring2, job, t)
                    for c in range(DC):
                        done = three(pe, psum[:, ring2.bank(job), :], [o[:, c, tile(k)] for o in (oh, ol)],
                                     [w[:, c, :] for w in dense], c == 0, c == DC - 1)
                    done.then_inc(ring2.full_of(job), 1)

            def front(t):
                turned.transpose(pe, t)
                project_qk(t)
                turn_qk(t)
                score(t)

            def middle(t):
                for k in range(BT):
                    turn_probabilities(pe, core, soft, ring2, t, k)
                    weigh(t, k)

            def head():
                pe.wait_ge(cleared, 1)
                front(0)
                project_values(0)

            def step(u):
                front(u)
                middle(u - 1)
                project_values(u)
                project_out(u - 1)

            def tail():
                middle(NB - 1)
                project_out(NB - 1)

            sweep(pe, head, step, tail)

        def keep_values(copy, b, t):
            for k in range(BT):
                src = psum[64 * b:64 * b + 64, ring1.bank("v"), k * D:(k + 1) * D].rearrange("p (a s d) -> p a s d", a=PAIRS, s=2)
                for s in range(2):
                    copy("v", ring1.filled("v", t) if k == 0 and s == 0 else None, vals[64 * s:64 * s + 64, 2 * k + b, :, s, :],
                         src[:, :, s, :], k == 1 and s == 1)

        @block.scalar
        def _(act):
            def copy(job, full, dst, src, last=True):
                if full is not None:
                    act.wait_ge(ring1.full_of(job), full)
                done = act.activation(dst, src, ACT.Copy)
                if last:
                    done.then_inc(ring1.empty_of(job), 1)

            def front(t):
                turned.scale(act, t)
                for k in range(BT):
                    job = f"rt{k}"
                    act.wait_ge(ring1.full_of(job), ring1.filled(job, t))
                    act.activation(q[:, :, tile(k)], psum[:, ring1.bank(job), 0:D].rearrange("p (c t) -> p c t", c=DC), ACT.Copy,
                                   scale=0.25).then_inc(ring1.empty_of(job), 1)

            def outputs(t, k):
                keep_probabilities(act, core, ring2, pt, t, k)
                output_high(act, core, ring2, f"av{k}", oh[:, :, tile(k)],
                            psum[:, ring2.bank(f"av{k}"), 0:D].rearrange("p (c t) -> p c t", c=DC), out_high, t)

            def head():
                act.wait_ge(cleared, 1)
                front(0)
                soft.exp(act, 0, 0)
                soft.exp(act, 0, 1)
                keep_values(copy, 0, 0)

            def step(u):
                front(u)
                for k in range(BT):
                    outputs(u - 1, k)
                    soft.exp(act, u, k)
                keep_values(copy, 0, u)

            def tail():
                for k in range(BT):
                    outputs(NB - 1, k)

            sweep(act, head, step, tail)

        @block.vector
        def _(dve):
            def copy(job, full, dst, src, last=True):
                if full is not None:
                    dve.wait_ge(ring1.full_of(job), full)
                done = dve.tensor_copy(dst, src)
                if last:
                    done.then_inc(ring1.empty_of(job), 1)

            def rotate(t):
                heads, half = 2 * HEADS, HD // 2
                for k in range(BT):
                    job = f"qk{k}"
                    src = psum[:, ring1.bank(job), :].rearrange("p (h d) -> p h d", h=heads)
                    sin = by_sin[:, k, :].rearrange("p (h d) -> p h d", h=heads)
                    dve.wait_ge(ring1.full_of(job), ring1.filled(job, t))
                    if not first(t):
                        dve.wait_ge(rotated, BT * t - BT + k + 1)
                    dve.tensor_tensor(by_cos[:, k, :].rearrange("p (h d) -> p h d", h=heads), src,
                                      wide(core.rope[:, 0:HD], 1, heads), ALU.mult)
                    dve.tensor_tensor(sin[:, :, 0:half], src[:, :, half:HD], wide(core.rope[:, HD:HD + half], 1, heads), ALU.mult)
                    dve.tensor_tensor(sin[:, :, half:HD], src[:, :, 0:half], wide(core.rope[:, HD + half:2 * HD], 1, heads), ALU.mult)\
                       .then_inc(ring1.empty_of(job), 1)

            def spread_keys(t):
                for k in range(BT):
                    job = f"rt{k}"
                    dve.wait_ge(ring1.empty_of(job), ring1.drained(job, t) - 1)
                    for c in range(DC):
                        src = psum[:, ring1.bank(job), (DC + c) * P:(DC + c + 1) * P].rearrange("p (b j) -> p b j", b=2)
                        done = dve.tensor_tensor(keys[:, 2 * k:2 * k + 2, c, :, :], wide(src, 2, 8),
                                                 wide(wide(core.col("hm8"), 2, SEQ), 1, 2), ALU.mult)
                    done.then_inc(ring1.empty_of(job), 1)

            def outputs(t, k):
                output_low(dve, core, ring2, f"av{k}", ol[:, :, tile(k)],
                           psum[:, ring2.bank(f"av{k}"), 0:D].rearrange("p (c t) -> p c t", c=DC), oh[:, :, tile(k)], out_high,
                           BT * t + k + 1, t)

            def front(t):
                turned.split(dve, t)
                norm.stats(dve, t + 1)
                rotate(t)
                spread_keys(t)

            def head():
                norm.stats(dve, 0)
                norm.normalise(dve, 0)
                front(0)
                for k in range(BT):
                    soft.less_top(dve, 0, k)
                for k in range(BT):
                    soft.sums(dve, 0, k)
                dve.wait_ge(cleared, 1)
                keep_values(copy, 1, 0)
                norm.normalise(dve, 1)

            def step(u):
                front(u)
                soft.less_top(dve, u, 0)
                outputs(u - 1, 0)
                soft.less_top(dve, u, 1)
                soft.sums(dve, u, 0)
                outputs(u - 1, 1)
                soft.sums(dve, u, 1)
                keep_values(copy, 1, u)
                add_experts(dve, core, ring2, ("d0", "d1"), mixed, u - 1)
                norm.normalise(dve, u + 1)

            def tail():
                for k in range(BT):
                    outputs(NB - 1, k)
                add_experts(dve, core, ring2, ("d0", "d1"), mixed, NB - 1)

            sweep(dve, head, step, tail)


def cross_attention(core, n):
    nc, psum = core.nc, core.psum
    place = core.placer(n)
    HD = P // HEADS
    xn = place("xn", [P, BT, 1, D])
    y = place("y", [P, DC, BLK])
    xh, xl = (place(s, [P, DC, BLK], F32R) for s in ("xh", "xl"))
    ch_b, cl_b = (place(s, [P, BLK], F32R) for s in ("ctx_block_h", "ctx_block_l"))
    q = place("q", [P, BLK])
    keys = place("keys", [P, BB, HEADS, SEQ])
    vals = place("vals", [P, BB, 4, 96])
    pt = place("pt", [P, BT, PAIRS, P])
    oh, ol = (place(s, [P, BLK], F32R) for s in ("oh", "ol"))
    ring1 = Ring(core, "c1_", (4, 5), [("xt", 1), ("qk", 2), ("v", 2)])
    ring2 = Ring(core, "c2_", (6, 7),
                 [("pt00", 1), ("pt01", 1), ("av0", 1), ("pt10", 1), ("pt11", 1), ("av1", 1), ("cd", 1)])
    cq = [w.rearrange("p (c m) -> p c m", c=DC) for w in core.weight(n, "cq")]
    ckv, cd = core.weight(n, "ckv"), core.weight(n, "cd")
    norm = Norm(core, n, "rms", "eps6", xn, ring1, "xt")
    turned = Turned(core, n, norm, ring1, ["xt"], y, xh, xl, f"g{n}", None)
    soft = Softmax(core, n, place, ring2, ["pt01", "pt11"])
    following = NextWeights(core, n + 1)
    copied, out_high, cleared = (core.sem(f"{s}{n}") for s in ("copied", "out_high", "cleared"))
    tile = lambda k: slice(k * P, (k + 1) * P)

    with nc.Block() as block:
        @block.sync
        def _(sp):
            sweep(sp, lambda: following.load(sp, 0), lambda u: following.load(sp, u), lambda: None)

        @block.gpsimd
        def _(pool):
            pool.memset(vals[:, :, :, :], 0.0).then_inc(cleared, 1)

            def late(t):
                norm.invert(pool, t + 1)
                soft.divide(pool, t, 0)
                soft.divide(pool, t, 1)
                following.split(pool, t, cleared)

            def head():
                norm.invert(pool, 0)
                late(0)

            sweep(pool, head, late, lambda: None)

        @block.tensor
        def _(pe):
            def project_qk(t):
                job = "qk"
                pe_wait_free(pe, ring1, job, t)
                three(pe, psum[:, ring1.bank(job), BLK:2 * BLK], [w[:, 0:P] for w in ckv],
                      [core.ctx_h[:, block_tokens(t)], core.ctx_l[:, block_tokens(t)]], True, True)
                pe.wait_ge(turned.split_done, t + 1)
                for c in range(DC):
                    done = three(pe, psum[:, ring1.bank(job), 0:BLK], [w[:, c, :] for w in cq], [xh[:, c, :], xl[:, c, :]],
                                 c == 0, c == DC - 1)
                done.then_inc(ring1.full_of(job), 1)

            def project_values(t):
                pe.wait_ge(copied, 2 * t + 2)
                pe_wait_free(pe, ring1, "v", t)
                for k in range(BT):
                    done = three(pe, psum[:, ring1.bank("v"), tile(k)], [b[:, tile(k)] for b in (ch_b, cl_b)],
                                 [w[:, P:2 * P] for w in ckv], True, True)
                done.then_inc(ring1.full_of("v"), 1)

            def score(t):
                pe.wait_ge(ring1.empty_of("qk"), ring1.drained("qk", t))
                for k in range(BT):
                    if not first(t):
                        pe.wait_ge(soft.less_done, BT * t - BT + k + 1)
                    for half in range(2):
                        for b in range(2):
                            done = pe.matmul(psum[64 * b:64 * b + 64, 2 * k + half, :], q[:, (2 * k + b) * SEQ:(2 * k + b + 1) * SEQ],
                                             keys[:, 2 * k + b, 8 * half:8 * half + 8, :], start=True, stop=True)
                    done.then_inc(soft.scored, 1)

            def weigh(t, k):
                job = f"av{k}"
                for i in range(2):
                    pe.wait_ge(ring2.empty_of(f"pt{k}{i}"), ring2.drained(f"pt{k}{i}", t))
                pe.wait_ge(ring1.empty_of("v"), ring1.drained("v", t))
                pe_wait_free(pe, ring2, job, t)
                for b in range(2):
                    for e in range(2):
                        for s in range(4):
                            done = pe.matmul(psum[32 * s:32 * s + 32, ring2.bank(job), b * SEQ:(b + 1) * SEQ],
                                             vals[:, 2 * k + b, s, 32 * e:32 * e + 32], pt[:, k, 2 * s + e, b * SEQ:(b + 1) * SEQ],
                                             start=e == 0, stop=e == 1)
                done.then_inc(ring2.full_of(job), 1)

            def project_out(t):
                for k in range(BT):
                    pe.wait_ge(ring2.empty_of(f"av{k}"), ring2.drained(f"av{k}", t))
                pe_wait_free(pe, ring2, "cd", t)
                for k in range(BT):
                    done = three(pe, psum[:, ring2.bank("cd"), k * D:(k + 1) * D], [o[:, tile(k)] for o in (oh, ol)], cd, True, True)
                done.then_inc(ring2.full_of("cd"), 1)

            def front(t):
                turned.transpose(pe, t)
                project_qk(t)
                score(t)

            def middle(t):
                for k in range(BT):
                    turn_probabilities(pe, core, soft, ring2, t, k)
                    weigh(t, k)

            def head():
                pe.wait_ge(cleared, 1)
                front(0)
                project_values(0)

            def step(u):
                front(u)
                middle(u - 1)
                project_values(u)
                project_out(u - 1)

            def tail():
                middle(NB - 1)
                project_out(NB - 1)

            sweep(pe, head, step, tail)

        def keep_values(copy, b, t):
            for k in range(BT):
                src = psum[64 * b:64 * b + 64, ring1.bank("v"), tile(k)].rearrange("p (a e s d) -> p a e s d", a=4, e=2, s=2)
                for s in range(2):
                    dst = vals[64 * s:64 * s + 64, 2 * k + b, :, :].rearrange("p a (e w) -> p a e w", e=2)
                    copy("v", ring1.filled("v", t) if k == 0 and s == 0 else None, dst[:, :, :, s * HD:(s + 1) * HD],
                         src[:, :, :, s, :], k == 1 and s == 1)

        @block.scalar
        def _(act):
            def copy(job, full, dst, src, last=True):
                if full is not None:
                    act.wait_ge(ring1.full_of(job), full)
                done = act.activation(dst, src, ACT.Copy)
                if last:
                    done.then_inc(ring1.empty_of(job), 1)

            def front(t):
                turned.scale(act, t)
                act.wait_ge(ring1.full_of("qk"), ring1.filled("qk", t))
                act.activation(q[:, :], psum[:, ring1.bank("qk"), 0:BLK], ACT.Copy, scale=float(1 / np.sqrt(HD)))\
                   .then_inc(ring1.empty_of("qk"), 1)

            def outputs(t, k):
                keep_probabilities(act, core, ring2, pt, t, k)
                output_high(act, core, ring2, f"av{k}", oh[:, tile(k)], psum[:, ring2.bank(f"av{k}"), 0:P], out_high, t)

            def head():
                act.wait_ge(cleared, 1)
                front(0)
                soft.exp(act, 0, 0)
                soft.exp(act, 0, 1)
                keep_values(copy, 0, 0)

            def step(u):
                front(u)
                for k in range(BT):
                    outputs(u - 1, k)
                    soft.exp(act, u, k)
                keep_values(copy, 0, u)

            def tail():
                for k in range(BT):
                    outputs(NB - 1, k)

            sweep(act, head, step, tail)

        @block.vector
        def _(dve):
            def copy(job, full, dst, src, last=True):
                if full is not None:
                    dve.wait_ge(ring1.full_of(job), full)
                done = dve.tensor_copy(dst, src)
                if last:
                    done.then_inc(ring1.empty_of(job), 1)

            def spread_keys(t):
                dve.wait_ge(ring1.empty_of("qk"), ring1.drained("qk", t) - 1)
                for k in range(BT):
                    src = psum[:, ring1.bank("qk"), BLK + k * P:BLK + (k + 1) * P].rearrange("p (b j) -> p b j", b=2)
                    done = dve.tensor_tensor(keys[:, 2 * k:2 * k + 2, :, :], wide(src, 2, HEADS),
                                             wide(wide(core.col("hm16"), 2, SEQ), 1, 2), ALU.mult)
                done.then_inc(ring1.empty_of("qk"), 1)

            def outputs(t, k):
                output_low(dve, core, ring2, f"av{k}", ol[:, tile(k)], psum[:, ring2.bank(f"av{k}"), 0:P], oh[:, tile(k)], out_high,
                           BT * t + k + 1, t)

            def residual(t):
                rows = core.x[:, block_tiles(t), :]
                dve.wait_ge(ring2.full_of("cd"), ring2.filled("cd", t))
                dve.tensor_tensor(rows, psum[:, ring2.bank("cd"), :].rearrange("p (k d) -> p k d", k=BT), rows, ALU.add)\
                   .then_inc(ring2.empty_of("cd"), 1)

            def front(t):
                turned.split(dve, t)
                norm.stats(dve, t + 1)
                copy_context(dve, core, ring1, "v", (ch_b, cl_b), copied, t)
                spread_keys(t)

            def head():
                norm.stats(dve, 0)
                norm.normalise(dve, 0)
                front(0)
                for k in range(BT):
                    soft.less_top(dve, 0, k)
                for k in range(BT):
                    soft.sums(dve, 0, k)
                dve.wait_ge(cleared, 1)
                keep_values(copy, 1, 0)
                norm.normalise(dve, 1)

            def step(u):
                front(u)
                soft.less_top(dve, u, 0)
                outputs(u - 1, 0)
                soft.less_top(dve, u, 1)
                soft.sums(dve, u, 0)
                outputs(u - 1, 1)
                soft.sums(dve, u, 1)
                keep_values(copy, 1, u)
                residual(u - 1)
                norm.normalise(dve, u + 1)

            def tail():
                for k in range(BT):
                    outputs(NB - 1, k)
                residual(NB - 1)

            sweep(dve, head, step, tail)


def experts(core, n):
    nc, psum = core.nc, core.psum
    place = core.placer(n)
    XC, NF = 2 * DC, len(F_SIZES)
    xn = place("xn", [P, BT, 2, D])
    y = place("y", [P, XC, BLK])
    xh, xl = (place(s, [P, XC, BLK], F32R) for s in ("xh", "xl"))
    silu = place("silu", [P, 2, BLK])
    hid = place("hid", [P, NF, BLK])
    hh, hl = (place(s, [P, NF, BLK], F32R) for s in ("hid_h", "hid_l"))
    ring_x = Ring(core, "ex_", (0, 1), [("xv", 1), ("xo", 1)])
    ring_g = Ring(core, "eg_", (2, 3, 4, 5), [(f"g{f}", 1) for f in range(NF)])
    ring_d = Ring(core, "ed_", (6, 7), [("d0", 1), ("d1", 1)])
    gu = [w.rearrange("p (c m) -> p c m", c=XC) for w in core.weight(n, "gu")]
    dn = [w.rearrange("p (c m) -> p c m", c=NF) for w in core.weight(n, "dn")]
    norm = Norm(core, n, "experts", "eps6", xn, ring_x, "xo")
    turned = Turned(core, n, norm, ring_x, ["xv", "xo"], y, xh, xl, f"g{n}", None)
    following = NextWeights(core, n + 1)
    silu_done, hid_high, hid_low, mixed, started = (core.sem(f"e_{s}") for s in ("silu", "hid_high", "hid_low", "mixed", "started"))
    tile = lambda k: slice(k * P, (k + 1) * P)

    with nc.Block() as block:
        @block.sync
        def _(sp):
            sweep(sp, lambda: following.load(sp, 0), lambda u: following.load(sp, u), lambda: None)

        @block.gpsimd
        def _(pool):
            pool.memset(core.spare[:, 2:3], 0.0).then_inc(started, 1)

            def late(t):
                norm.invert(pool, t + 1)
                for f, size in enumerate(F_SIZES):
                    pool.wait_ge(hid_high, NF * t + f + 1)
                    pool.tensor_tensor(hl[0:size, f, :], hid[0:size, f, :], f32(hh[0:size, f, :]), ALU.subtract).then_inc(hid_low, 1)
                following.split(pool, t, started)

            def head():
                norm.invert(pool, 0)
                late(0)

            sweep(pool, head, late, lambda: None)

        @block.tensor
        def _(pe):
            def up(t):
                pe.wait_ge(turned.split_done, 2 * t + 2)
                for f, (off, size) in enumerate(zip(F_OFF, F_SIZES)):
                    job = f"g{f}"
                    pe_wait_free(pe, ring_g, job, t)
                    for i in range(2):
                        m = slice(i * MOE_FF + off, i * MOE_FF + off + size)
                        for c in range(XC):
                            done = three(pe, psum[0:size, ring_g.bank(job), i * BLK:(i + 1) * BLK], [w[:, c, m] for w in gu],
                                         [xh[:, c, :], xl[:, c, :]], c == 0, c == XC - 1)
                    done.then_inc(ring_g.full_of(job), 1)

            def down(t):
                for k in range(BT):
                    job = f"d{k}"
                    pe_wait_free(pe, ring_d, job, t)
                    for f, size in enumerate(F_SIZES):
                        if k == 0:
                            pe.wait_ge(hid_low, NF * t + f + 1)
                        done = three(pe, psum[:, ring_d.bank(job), :], [g[0:size, f, tile(k)] for g in (hh, hl)],
                                     [w[0:size, f, :] for w in dn], f == 0, f == NF - 1)
                    done.then_inc(ring_d.full_of(job), 1)

            def head():
                turned.transpose(pe, 0)
                up(0)

            def step(u):
                turned.transpose(pe, u)
                down(u - 1)
                up(u)

            sweep(pe, head, step, lambda: down(NB - 1))

        @block.scalar
        def _(act):
            def step(t):
                turned.scale(act, t)
                for f, size in enumerate(F_SIZES):
                    job = f"g{f}"
                    act.wait_ge(ring_g.full_of(job), ring_g.filled(job, t))
                    if f >= 2:
                        act.wait_ge(ring_g.empty_of(f"g{f - 2}"), ring_g.drained(f"g{f - 2}", t))
                    elif not first(t):
                        act.wait_ge(ring_g.empty_of(f"g{NF - 2 + f}"), ring_g.drained(f"g{NF - 2 + f}", t - 1))
                    act.activation(silu[0:size, f % 2, :], psum[0:size, ring_g.bank(job), 0:BLK], ACT.Silu).then_inc(silu_done, 1)

            sweep(act, lambda: step(0), step, lambda: None)

        @block.vector
        def _(dve):
            def hidden(t):
                for f, size in enumerate(F_SIZES):
                    job = f"g{f}"
                    dve.wait_ge(silu_done, NF * t + f + 1)
                    if not first(t):
                        dve.wait_ge(hid_low, NF * t - NF + f + 1)
                    dve.tensor_tensor(hid[0:size, f, :], psum[0:size, ring_g.bank(job), BLK:2 * BLK], silu[0:size, f % 2, :], ALU.mult)\
                       .then_inc(ring_g.empty_of(job), 1)
                    dve.wait_ge(ring_g.empty_of(job), ring_g.drained(job, t))
                    dve.tensor_copy(hh[0:size, f, :], hid[0:size, f, :]).then_inc(hid_high, 1)

            def head():
                norm.stats(dve, 0)
                norm.normalise(dve, 0)
                turned.split(dve, 0)
                norm.stats(dve, 1)
                norm.normalise(dve, 1)
                hidden(0)

            def step(u):
                turned.split(dve, u)
                norm.stats(dve, u + 1)
                add_experts(dve, core, ring_d, ("d0", "d1"), mixed, u - 1)
                norm.normalise(dve, u + 1)
                hidden(u)

            sweep(dve, head, step, lambda: add_experts(dve, core, ring_d, ("d0", "d1"), mixed, NB - 1))


def build_program(nc, dram, out, phases=tuple(range(8))):
    with ExitStack() as ctx:
        core = Core(nc, ctx, dram, out)
        setup(core)
        steps = [
            lambda: gated_attention(core, 0, core.gates[:, 0:1]),
            lambda: feed_forward(core, 1, core.gates[:, 1:2], False),
            lambda: memory_gate(core, 2),
            lambda: self_attention(core, 3),
            lambda: cross_attention(core, 4),
            lambda: experts(core, 5),
            lambda: gated_attention(core, 6, core.gates[:, 2:3]),
            lambda: feed_forward(core, 7, core.gates[:, 3:4], True),
        ]
        core.end_phase()
        for n in phases:
            steps[n]()
            if n != phases[-1]:
                core.end_phase()


def _chunks(w, k):
    return w.reshape(k, P, -1).transpose(1, 0, 2).reshape(P, -1)


def _pack(a):
    cat = np.concatenate

    def att(p):
        wkv = a[f"{p}_Wkv"]
        return cat([wkv[:, :INNER], wkv[:, INNER:], _chunks(a[f"{p}_Wq"], DC), _chunks(a[f"{p}_Wo"], PAIRS)], 1)

    def ffn(p):
        return cat([_chunks(a[f"{p}_W1"], DC), _chunks(a[f"{p}_W2"], FF // P)], 1)

    m, e = "L1_xattn_", "L2_xattn_"
    qkv = cat([_chunks(a[e + "v_qkv"], DC), _chunks(a[e + "l_qkv"], DC)], 1)
    dense = _chunks(cat([a[e + "v_dense"], a[e + "l_dense"]], 1), DC)
    gu = cat([_chunks(cat([a[e + v + "gate"], a[e + v + "up"]], 1), DC) for v in ("v_", "l_")], 1)
    down = cat([a[e + "v_down"], a[e + "l_down"]], 1)
    dn = np.zeros((P, len(F_SIZES), 2 * D), np.float32)
    for f, (o, s) in enumerate(zip(F_OFF, F_SIZES)):
        dn[:s, f] = down[o:o + s]
    packed = [
        att("L0_xattn"), ffn("L0_xattn"),
        cat([a[m + "W_mem"].T, _chunks(a[m + "W_gate"].T, 4)], 1),
        cat([qkv, dense], 1),
        cat([_chunks(a[e + "cq_w"], DC), a[e + "ckv_w"], a[e + "cdense_w"]], 1),
        cat([gu, dn.reshape(P, -1)], 1),
        att("L3_xattn"), ffn("L3_xattn"),
    ]
    got = {f"w{n}": np.ascontiguousarray(w) for n, w in enumerate(packed)}

    cols = np.zeros((P, NCOLS), np.float32)

    def put(name, v):
        at, n = COLS[name]
        cols[:, at:at + n] = v

    for name, key in (("g0", "L0_xattn_ln_q_g"), ("b0", "L0_xattn_ln_q_b"), ("g1", "L0_xattn_ln_ff_g"), ("b1", "L0_xattn_ln_ff_b"),
                      ("g6", "L3_xattn_ln_q_g"), ("b6", "L3_xattn_ln_q_b"), ("g7", "L3_xattn_ln_ff_g"), ("b7", "L3_xattn_ln_ff_b"),
                      ("g3", e + "ln_in_w"), ("g4", e + "ln_post_cross_w"), ("g5", e + "ln_post_attn_w")):
        put(name, a[key].reshape(DC, P).T)
    for name, key in (("gate0", "L0_xattn_attn_gate"), ("gate1", "L0_xattn_ff_gate"),
                      ("gate6", "L3_xattn_attn_gate"), ("gate7", "L3_xattn_ff_gate")):
        put(name, a[key][None, :])
    part = np.arange(P)
    put("hm8", part[:, None] // 16 == np.arange(8)[None, :])
    put("hm16", part[:, None] // 8 == np.arange(16)[None, :])
    put("tcol", part[:, None])
    put("eps5", 1e-5), put("eps6", 1e-6), put("minus_half", -0.5)
    put("bgate", a[m + "b_gate"][None, :]), put("normw", a[m + "norm_w"][None, :])
    put("ident", np.eye(P))
    inv = (1.0 / 10000.0 ** (np.arange(0, 16, 2, dtype=np.float32) / 16)).astype(np.float32)
    ang = np.outer(np.arange(SEQ, dtype=np.float32), inv).astype(np.float32)
    at, _ = COLS["cossin"]
    cols[:SEQ, at:at + 32] = np.concatenate([np.cos(ang), np.cos(ang), -np.sin(ang), np.sin(ang)], 1)
    put("causal", np.where(np.arange(SEQ)[None, :] <= part[:, None] % SEQ, 0.0, MASKED))
    put("batch_sel", part[:, None] == part[None, :] // SEQ)
    got["cols"] = cols

    keep = a["mask_BxS2_bk0"].view(np.int32).reshape(TILES, 2, SEQ // 4)
    got["ctx_mask"] = np.ascontiguousarray(keep.transpose(1, 0, 2))
    types = a["mask_BxS_ik0"]
    after = np.concatenate([types[:, 1:], np.zeros((BATCH, 1), types.dtype)], 1)
    got["types"] = np.ascontiguousarray(np.stack([types.reshape(TILES, P).T, after.reshape(TILES, P).T], 1))
    got["pos"] = np.ascontiguousarray(np.broadcast_to(np.tile(a["pos_1xS"], (1, 2)), (SEQ, P)))
    got["x"] = a["x"].reshape(TOK, D)
    got["ctx"] = a["ctx_1024"].reshape(TOK, CTX)
    return got


def kernel(**inputs):
    import concourse.bacc as bacc
    from concourse.bass_utils import run_bass_kernel_spmd

    packed = _pack({k: np.asarray(v) for k, v in inputs.items()})
    nc = bacc.Bacc("TRN2", target_bir_lowering=False, num_devices=1)
    dram = {k: nc.dram_tensor(f"in_{k}", v.shape, mybir.dt.from_np(v.dtype), kind="ExternalInput").ap() for k, v in packed.items()}
    out = nc.dram_tensor("out", (TOK, D), F32, kind="ExternalOutput").ap()
    build_program(nc, dram, out)
    r = run_bass_kernel_spmd(nc, [{f"in_{k}": v for k, v in packed.items()}], core_ids=[0])
    return r.results[0]["out"].reshape(BATCH, SEQ, D)
```

```python
from contextlib import ExitStack

import numpy as np

import concourse.bass as bass
from concourse import mybir

ALU = mybir.AluOpType
ACT = mybir.ActivationFunctionType
AX = mybir.AxisListType
F32 = mybir.dt.float32
F32R = mybir.dt.float32r
BF16 = mybir.dt.bfloat16
I32 = mybir.dt.int32
U8 = mybir.dt.uint8

P = 128
BATCH = 32
SEQ = 64
TOK = BATCH * SEQ
D = 256
DC = D // P
CTX = 128
TILES = TOK // P
BT = 2
BLK = BT * P
NB = TOK // BLK
BB = BLK // SEQ
HEADS = 16
PAIRS = HEADS // 2
INNER = 1024
FF = 1024
MOE_FF = 688
F_SIZES = [116, 116, 114, 114, 114, 114]
F_OFF = [sum(F_SIZES[:i]) for i in range(len(F_SIZES))]
MASKED = -(2.0 ** 127)
KB = 1024

W_ATT = {"wk": INNER, "wv": INNER, "wq": DC * INNER, "wo": PAIRS * D}
W_FFN = {"w1": DC * FF, "w2": (FF // P) * D}
W_MEM = {"wm": D, "wg": 4 * D}
W_SELF = {"qkv": 4 * 3 * D, "dense": DC * 2 * D}
W_CROSS = {"cq": DC * P, "ckv": 2 * P, "cd": D}
W_MOE = {"gu": 4 * 2 * MOE_FF, "dn": len(F_SIZES) * 2 * D}
WEIGHTS = [W_ATT, W_FFN, W_MEM, W_SELF, W_CROSS, W_MOE, W_ATT, W_FFN]
WCOLS = [sum(w.values()) for w in WEIGHTS]
CHUNK = [c // NB for c in WCOLS]

COLS = {}


def _col(name, n):
    COLS[name] = (sum(w for _, w in COLS.values()), n)


for _n in ("g0", "b0", "g1", "b1", "g6", "b6", "g7", "b7", "g3", "g4", "g5"):
    _col(_n, DC)
_col("gate0", 1), _col("gate1", 1), _col("gate6", 1), _col("gate7", 1)
_col("hm8", 8), _col("hm16", 16)
_col("eps5", BT), _col("eps6", BT), _col("minus_half", BT)
_col("bgate", D), _col("normw", D), _col("ident", P)
KEPT = sum(w for _, w in COLS.values())
_col("tcol", 1), _col("cossin", 32), _col("causal", SEQ), _col("batch_sel", P)
NCOLS = sum(w for _, w in COLS.values())


class Ring:

    def __init__(self, core, name, banks, jobs):
        self.banks = banks
        self.full = [core.sem(f"{name}_full{b}") for b in banks]
        self.empty = [core.sem(f"{name}_empty{b}") for b in banks]
        self.at, fills, drains = {}, [0] * len(banks), [0] * len(banks)
        for n, (job, d) in enumerate(jobs):
            b = n % len(banks)
            self.at[job] = (b, fills[b], drains[b], d)
            fills[b] += 1
            drains[b] += d
        self.fills, self.drains = fills, drains

    def bank(self, job):
        return self.banks[self.at[job][0]]

    def full_of(self, job):
        return self.full[self.at[job][0]]

    def empty_of(self, job):
        return self.empty[self.at[job][0]]

    def filled(self, job, t):
        b, fills, _, _ = self.at[job]
        return t * self.fills[b] + fills + 1

    def free(self, job, t):
        b, _, drains, _ = self.at[job]
        return t * self.drains[b] + drains

    def drained(self, job, t):
        b, _, drains, d = self.at[job]
        return t * self.drains[b] + drains + d


def first(t):
    return isinstance(t, int) and t == 0


def sweep(eng, head, step, tail):
    head()
    with eng.Fori(1, NB) as u:
        step(u)
    tail()


def f32(part):
    return part.bitcast(F32)


def wide(ap, axis, n):
    shape = list(ap.shape)
    return ap.unsqueeze(axis).broadcast_to(shape[:axis] + [n] + shape[axis:])


class Core:

    def __init__(self, nc, ctx, dram, out):
        self.nc, self.ctx, self.dram, self.out = nc, ctx, dram, out

        def sb(name, shape, dt=F32):
            return ctx.enter_context(nc.sbuf_tensor(name, shape, dt))

        self.x = sb("x", [P, TILES + BT, D])
        ctx_t = sb("ctx_t", [P, 2 * TOK + BLK], F32R)
        self.ctx_pad = ctx_t[:, 2 * TOK:2 * TOK + BLK]
        self.ctx_h, self.ctx_l = ctx_t[:, 0:TOK + BLK], ctx_t[:, TOK:2 * TOK + BLK]
        self.cols = sb("cols", [P, KEPT])
        self.ident_b = sb("ident_b", [P, P], BF16)
        self.causal = sb("causal", [P, SEQ], BF16)
        self.batch_sel = sb("batch_sel", [2, P], BF16)
        self.mask_row = sb("mask_row", [2, TILES, SEQ], BF16)
        self.gates = sb("gates", [P, 4])
        self.vm = sb("vm", [P, TILES + BT])
        self.not_vm = sb("not_vm", [P, TILES + BT])
        self.rope = sb("rope", [P, 32])
        self.w_raw = sb("w_raw", [P, max(CHUNK)])
        self.bn = sb("bn", [P, BT, 6])
        self.mv = sb("mv", [P, BT, 2])
        self.ve = sb("ve", [P, 3, BT])
        self.rstd = sb("rstd", [P, BT])
        self.spare = sb("spare", [P, 3])
        self.phase_sems = []
        self.begun = nc.alloc_semaphore(name="begun")
        self.x_rest = nc.alloc_semaphore(name="x_rest")
        self.wo_landed = nc.alloc_semaphore(name="wo_landed")
        self.low = -(-nc.sbuf_base // 64) * 64
        self.high = nc.sbuf_top // 64 * 64
        self.psum = ctx.enter_context(nc.psum_tensor("psum", [P, 8, 512], F32))
        self.weights, self.low_end, self.high_start = [], [], []
        for n, c in enumerate(WCOLS):
            size = 2 * 4 * c
            at = self.low if n % 2 == 0 else self.high - size
            h = nc.alloc_sbuf_tensor_at(f"w{n}_h", [P, c], F32R, offset=at)
            l = nc.alloc_sbuf_tensor_at(f"w{n}_l", [P, c], F32R, offset=at + size // 2)
            self.weights.append((h, l))
        for n in range(len(WCOLS)):
            live = [m for m in (n, n + 1) if m < len(WCOLS)]
            self.low_end.append(self.low + max([8 * WCOLS[m] for m in live if m % 2 == 0], default=0))
            self.high_start.append(self.high - max([8 * WCOLS[m] for m in live if m % 2], default=0))

        self.raw_w0 = nc.alloc_sbuf_tensor_at("raw_w0", [P, WCOLS[0]], F32, offset=self.high - 4 * WCOLS[0])

    def sem(self, name):
        self.phase_sems.append(self.nc.alloc_semaphore(name=name))
        return self.phase_sems[-1]

    def end_phase(self):
        self.nc.clear_and_free_semaphores(self.phase_sems)
        self.nc.all_engine_barrier()
        self.phase_sems = []

    def col(self, name, rows=P):
        a, n = COLS[name]
        return self.cols[0:rows, a:a + n]

    def weight(self, n, name):
        a = 0
        for k, w in WEIGHTS[n].items():
            if k == name:
                return tuple(part[:, a:a + w] for part in self.weights[n])
            a += w

    def placer(self, n):
        at = [self.low_end[n]]

        def place(name, shape, dt=F32):
            size = int(np.prod(shape[1:])) * (2 if dt == BF16 else 4)
            size = -(-size // 64) * 64
            t = self.nc.alloc_sbuf_tensor_at(f"p{n}_{name}", shape, dt, offset=at[0])
            at[0] += size
            assert at[0] <= self.high_start[n], (n, name, at[0], self.high_start[n])
            return t

        return place


def block_tokens(t):
    return bass.ds(t * BLK, BLK)


def block_tiles(t):
    return bass.ds(t * BT, BT)


class NextWeights:

    def __init__(self, core, n):
        self.core, self.n = core, n
        if n < len(WEIGHTS):
            self.landed = core.sem(f"w{n}_landed")
            self.high_done = core.sem(f"w{n}_high_done")
            self.low_done = core.sem(f"w{n}_low_done")

    def load(self, sp, t):
        if self.n >= len(WEIGHTS):
            return
        c = CHUNK[self.n]
        if not first(t):
            sp.wait_ge(self.low_done, t)
        sp.dma_start(self.core.w_raw[:, 0:c], self.core.dram[f"w{self.n}"][:, bass.ds(t * c, c)]).then_inc(self.landed, 16)

    def split(self, pool, t, ready):
        if self.n >= len(WEIGHTS):
            return
        c = CHUNK[self.n]
        h, l = self.core.weights[self.n]
        at = bass.ds(t * c, c)
        raw = self.core.w_raw[:, 0:c]
        pool.wait_ge(self.landed, 16 * t + 16)
        pool.wait_ge(ready, 1)
        pool.tensor_copy(h[:, at], raw).then_inc(self.high_done, 1)
        pool.wait_ge(self.high_done, t + 1)
        pool.tensor_tensor(l[:, at], raw, f32(h[:, at]), ALU.subtract).then_inc(self.low_done, 1)


class Norm:

    def __init__(self, core, n, kind, eps, xn, ring, last_job, ready=None):
        self.core, self.kind, self.eps, self.xn, self.ring, self.last = core, kind, eps, xn, ring, last_job
        self.stats_done = core.sem(f"n{n}_stats")
        self.mean_done = core.sem(f"n{n}_mean")
        self.var_done = core.sem(f"n{n}_var")
        self.rstd_done = core.sem(f"n{n}_rstd")
        self.xn_done = core.sem(f"n{n}_xn")
        self.steps = 1 if kind == "layer" else 3
        self.outs = 2 * BT if kind == "experts" else BT

    def stats(self, dve, t, src=None):
        c = self.core
        for k in range(BT):
            row = c.x[:, bass.ds(t * BT + k, 1), :].squeeze(1) if src is None else src[:, k, :]
            dve.bn_stats(c.bn[:, k, :], row).then_inc(self.stats_done, 1)
        dve.wait_ge(self.stats_done, BT * t + BT)
        dve.tensor_copy(c.spare[:, 1:2], c.spare[:, 0:1])
        for k in range(BT):
            dve.bn_aggr(c.mv[:, k, :], c.bn[:, k, :]).then_inc(self.mean_done, 1)

    def invert(self, pool, t):
        c = self.core
        mean, var = c.mv[:, :, 0], c.mv[:, :, 1]
        eps, half = c.col(self.eps), c.col("minus_half")
        n = self.steps
        pool.wait_ge(self.mean_done, BT * t + BT)
        if self.kind == "layer":
            pool.tensor_tensor(c.ve[:, 2, :], var, eps, ALU.add).then_inc(self.var_done, 1)
        else:
            pool.tensor_tensor(c.ve[:, 0, :], mean, mean, ALU.mult).then_inc(self.var_done, 1)
            pool.wait_ge(self.var_done, n * t + 1)
            pool.tensor_tensor(c.ve[:, 1, :], c.ve[:, 0, :], var, ALU.add).then_inc(self.var_done, 1)
            pool.wait_ge(self.var_done, n * t + 2)
            pool.tensor_tensor(c.ve[:, 2, :], c.ve[:, 1, :], eps, ALU.add).then_inc(self.var_done, 1)
        pool.wait_ge(self.var_done, n * t + n)
        pool.tensor_tensor(c.rstd[:, :], c.ve[:, 2, :], half, ALU.pow).then_inc(self.rstd_done, 1)

    def normalise(self, dve, t):
        c = self.core
        if not first(t):
            dve.wait_ge(self.ring.full_of(self.last), self.ring.filled(self.last, t - 1))
        dve.wait_ge(self.rstd_done, t + 1)
        for k in range(BT):
            row = c.x[:, bass.ds(t * BT + k, 1), :].squeeze(1)
            r = c.rstd[:, k:k + 1]
            if self.kind == "layer":
                dve.tensor_scalar(self.xn[:, k, 0, :], row, c.mv[:, k, 0:1], r, ALU.subtract, ALU.mult).then_inc(self.xn_done, 1)
            elif self.kind == "rms":
                dve.tensor_scalar(self.xn[:, k, 0, :], row, r, None, ALU.mult).then_inc(self.xn_done, 1)
            else:
                at = bass.ds(t * BT + k, 1)
                dve.tensor_scalar(self.xn[:, k, 0, :], row, r, c.vm[:, at], ALU.mult, ALU.mult).then_inc(self.xn_done, 1)
                dve.tensor_scalar(self.xn[:, k, 1, :], row, r, c.not_vm[:, at], ALU.mult, ALU.mult).then_inc(self.xn_done, 1)


class Turned:

    def __init__(self, core, n, norm, ring, jobs, y, xh, xl, gain, shift):
        self.core, self.norm, self.ring, self.jobs = core, norm, ring, jobs
        self.y, self.xh, self.xl, self.gain, self.shift = y, xh, xl, gain, shift
        self.high_done = core.sem(f"t{n}_high")
        self.split_done = core.sem(f"t{n}_split")

    def transpose(self, pe, t):
        c = self.core
        pe.wait_ge(self.norm.xn_done, self.norm.outs * (t + 1))
        for j, job in enumerate(self.jobs):
            if not (first(t) and self.ring.free(job, 0) == 0):
                pe.wait_ge(self.ring.empty_of(job), self.ring.free(job, t))
            bank = self.ring.bank(job)
            for ch in range(DC):
                for k in range(BT):
                    done = pe.transpose(c.psum[:, bank, (ch * BT + k) * P:(ch * BT + k + 1) * P],
                                        self.norm.xn[:, k, j, ch * P:(ch + 1) * P], c.col("ident"))
            done.then_inc(self.ring.full_of(job), 1)

    def scale(self, act, t):
        c, n = self.core, len(self.jobs)
        for j, job in enumerate(self.jobs):
            act.wait_ge(self.ring.full_of(job), self.ring.filled(job, t))
            if not first(t):
                act.wait_ge(self.split_done, n * t - n + j + 1)
            for ch in range(DC):
                gain = c.col(self.gain)[:, ch:ch + 1]
                bias = c.col(self.shift)[:, ch:ch + 1] if self.shift else 0.0
                done = act.activation(self.y[:, j * DC + ch, :], c.psum[:, self.ring.bank(job), ch * BLK:(ch + 1) * BLK],
                                      ACT.Identity, bias=bias, scale=gain)
            done.then_inc(self.ring.empty_of(job), 1)

    def split(self, dve, t):
        n = len(self.jobs)
        for j, job in enumerate(self.jobs):
            part = slice(j * DC, (j + 1) * DC)
            dve.wait_ge(self.ring.empty_of(job), self.ring.drained(job, t))
            dve.tensor_copy(self.xh[:, part, :], self.y[:, part, :]).then_inc(self.high_done, 1)
            dve.wait_ge(self.high_done, n * t + j + 1)
            dve.tensor_tensor(self.xl[:, part, :], self.y[:, part, :], f32(self.xh[:, part, :]), ALU.subtract)\
               .then_inc(self.split_done, 1)


def three(pe, out, stationary, moving, start, stop):
    (sh, sl), (mh, ml) = stationary, moving
    pe.matmul(out, sh, mh, start=start, stop=False)
    pe.matmul(out, sh, ml, start=False, stop=False)
    return pe.matmul(out, sl, mh, start=False, stop=stop)


def pe_wait_free(pe, ring, job, t):
    if not (first(t) and ring.free(job, 0) == 0):
        pe.wait_ge(ring.empty_of(job), ring.free(job, t))


class Softmax:

    def __init__(self, core, n, place, ring, read_job):
        self.core, self.ring, self.read_job = core, ring, read_job
        self.e = place("e", [P, BT, HEADS, SEQ])
        self.top = place("top", [P, BT, HEADS])
        self.total = place("total", [P, BT, HEADS])
        self.inverse = place("inverse", [P, BT, HEADS])
        self.scored = core.sem(f"s{n}_scored")
        self.top_done = core.sem(f"s{n}_top")
        self.less_done = core.sem(f"s{n}_less")
        self.exp_done = core.sem(f"s{n}_exp")
        self.total_done = core.sem(f"s{n}_total")
        self.inverse_done = core.sem(f"s{n}_inverse")
        self.ready = core.sem(f"s{n}_ready")

    def scores(self, k):
        return self.core.psum[:, 2 * k:2 * k + 2, :].rearrange("p b (h j) -> p (b h) j", j=SEQ)

    def less_top(self, dve, t, k):
        dve.wait_ge(self.scored, BT * t + k + 1)
        dve.tensor_reduce(self.top[:, k, :], self.scores(k), AX.X, ALU.max).then_inc(self.top_done, 1)
        dve.wait_ge(self.top_done, BT * t + k + 1)
        if not first(t):
            job = self.read_job[k]
            dve.wait_ge(self.ring.full_of(job), self.ring.filled(job, t - 1))
        dve.tensor_tensor(self.e[:, k], self.scores(k), wide(self.top[:, k, :], 2, SEQ), ALU.subtract)\
           .then_inc(self.less_done, 1)

    def exp(self, act, t, k):
        act.wait_ge(self.less_done, BT * t + k + 1)
        act.activation(self.e[:, k], self.e[:, k], ACT.Exp).then_inc(self.exp_done, 1)

    def sums(self, dve, t, k):
        dve.wait_ge(self.exp_done, BT * t + k + 1)
        dve.tensor_reduce(self.total[:, k, :], self.e[:, k], AX.X, ALU.add).then_inc(self.total_done, 1)
        dve.wait_ge(self.total_done, BT * t + k + 1)
        dve.reciprocal(self.inverse[:, k, :], self.total[:, k, :]).then_inc(self.inverse_done, 1)

    def divide(self, pool, t, k):
        pool.wait_ge(self.inverse_done, BT * t + k + 1)
        pool.tensor_tensor(self.e[:, k], self.e[:, k], wide(self.inverse[:, k, :], 2, SEQ), ALU.mult)\
            .then_inc(self.ready, 1)


def turn_probabilities(pe, core, soft, ring, t, k):
    pe.wait_ge(soft.ready, BT * t + k + 1)
    for i in range(2):
        job = f"pt{k}{i}"
        pe_wait_free(pe, ring, job, t)
        for q in range(4):
            pair = 4 * i + q
            done = pe.transpose(core.psum[:, ring.bank(job), q * P:(q + 1) * P],
                                soft.e[:, k, 2 * pair:2 * pair + 2, :], core.col("ident"))
        done.then_inc(ring.full_of(job), 1)


def keep_probabilities(act, core, ring, pt, t, k):
    for i in range(2):
        job = f"pt{k}{i}"
        act.wait_ge(ring.full_of(job), ring.filled(job, t))
        act.activation(pt[:, k, 4 * i:4 * i + 4, :], core.psum[:, ring.bank(job), :], ACT.Copy)\
           .then_inc(ring.empty_of(job), 1)


def output_high(act, core, ring, job, dst, src, done, t):
    act.wait_ge(ring.full_of(job), ring.filled(job, t))
    act.activation(dst, src, ACT.Copy).then_inc(done, 1)


def output_low(dve, core, ring, job, dst, src, high, done, count, t):
    dve.wait_ge(done, count)
    dve.tensor_tensor(dst, src, f32(high), ALU.subtract).then_inc(ring.empty_of(job), 1)


def copy_context(dve, core, ring, after, buf, sem, t):
    if not first(t):
        dve.wait_ge(ring.full_of(after), ring.filled(after, t - 1))
    for dst, src in zip(buf, (core.ctx_h, core.ctx_l)):
        dve.tensor_scalar(dst[:, :], f32(src[:, block_tokens(t)]), 1.0, None, ALU.mult).then_inc(sem, 1)


def setup(core):
    nc, dram = core.nc, core.dram
    place = core.placer(0)
    raw_ctx = place("raw_ctx", [P, TILES, CTX])
    mask8 = place("mask8", [2, TILES, SEQ // 4], I32)
    maskf = place("maskf", [2, TILES, SEQ])
    types = place("types", [P, 2, TILES], I32)
    typef = place("typef", [P, 2, TILES])
    pos = place("pos", [SEQ, P], I32)
    posf = place("posf", [SEQ, 3, P])
    onehot = place("onehot", [SEQ, P])
    tables_sb = place("tables", [P, NCOLS - KEPT])

    def table(name, rows=P):
        a, n = COLS[name]
        return tables_sb[0:rows, a - KEPT:a - KEPT + n]

    loaded, tables, landed = core.sem("loaded"), core.sem("tables"), [core.sem(f"w0_landed{c}") for c in range(4)]
    x_landed = core.sem("x_landed")
    turned, kept = core.sem("ctx_turned"), core.sem("ctx_kept")
    w_high, ctx_high, steps, rope_done = core.sem("w0_high"), core.sem("ctx_high"), core.sem("setup_steps"), core.sem("rope_done")
    tanh_done, zeroed, sel_done = core.sem("tanh_done"), core.sem("pad_zeroed"), core.sem("sel_done")
    mask_done, pool_low = core.sem("mask_done"), core.sem("w0_pool_low")
    n_chunks = len(landed)
    wc = (WCOLS[0] - W_ATT["wo"]) // n_chunks
    GROUPS = 4
    per = TILES // GROUPS
    h, l = core.weights[0]
    raw_w = core.raw_w0
    x_tiles = dram["x"].rearrange("(t p) d -> p t d", p=P)

    with nc.Block() as block:
        @block.sync
        def _(sp):
            sp.dma_start(raw_ctx[:, :, :], dram["ctx"].rearrange("(t p) e -> p t e", p=P)).then_inc(loaded, 16)
            sp.dma_start(core.cols[:, :], dram["cols"][:, 0:KEPT]).then_inc(tables, 16)
            sp.dma_start(tables_sb[:, :], dram["cols"][:, KEPT:NCOLS]).then_inc(tables, 16)
            for c in range(n_chunks):
                sp.dma_start(raw_w[:, c * wc:(c + 1) * wc], dram["w0"][:, c * wc:(c + 1) * wc]).then_inc(landed[c], 16)
            sp.dma_start(core.x[:, 0:BT, :], x_tiles[:, 0:BT, :]).then_inc(x_landed, 16)
            sp.dma_start(core.x[:, BT:TILES, :], x_tiles[:, BT:TILES, :]).then_inc(core.x_rest, 16)
            sp.dma_start(raw_w[:, n_chunks * wc:], dram["w0"][:, n_chunks * wc:]).then_inc(core.wo_landed, 16)
            sp.wait_ge(x_landed, 16)

        @block.gpsimd
        def _(pool):
            pool.memset(core.x[:, TILES:TILES + BT, :], 0.0).then_inc(core.begun, 1)
            pool.memset(core.spare[:, :], 0.0).then_inc(zeroed, 1)
            pool.memset(f32(core.ctx_pad), 0.0).then_inc(zeroed, 1)
            pool.memset(core.vm[:, TILES:TILES + BT], 0.0).then_inc(zeroed, 1)
            pool.memset(core.not_vm[:, TILES:TILES + BT], 0.0).then_inc(zeroed, 1)
            pool.wait_ge(tables, 16 * 5)
            pool.tensor_copy(core.ident_b[:, :], core.col("ident")).then_inc(zeroed, 1)
            pool.tensor_copy(core.causal[:, :], table("causal")).then_inc(zeroed, 1)
            pool.tensor_copy(core.batch_sel[:, :], table("batch_sel", 2)).then_inc(zeroed, 1)
            pool.tensor_copy(maskf[:, :, :], mask8[:, :, :].bitcast(U8)).then_inc(mask_done, 1)
            pool.wait_ge(mask_done, 1)
            pool.tensor_scalar(core.mask_row[:, :, :], maskf[:, :, :], -1.0, -MASKED, ALU.add, ALU.mult).then_inc(mask_done, 1)
            pool.wait_ge(w_high, 1)
            pool.tensor_tensor(l[:, 0:wc], raw_w[:, 0:wc], f32(h[:, 0:wc]), ALU.subtract).then_inc(pool_low, 1)

        @block.tensor
        def _(pe):
            pe.wait_ge(loaded, 16)
            pe.wait_ge(tables, 16 * 5)
            for g in range(GROUPS):
                for i in range(per):
                    done = pe.transpose(core.psum[:, g, i * P:(i + 1) * P], raw_ctx[:, g * per + i, :], core.col("ident"))
                done.then_inc(turned, 1)
            pe.wait_ge(rope_done, 1)
            pe.matmul(core.psum[:, 4, 0:32], onehot[:, :], table("cossin", SEQ), start=True, stop=True).then_inc(turned, 1)

        @block.scalar
        def _(act):
            act.dma_start(mask8[:, :, :], dram["ctx_mask"]).then_inc(tables, 16)
            act.dma_start(types[:, :, :], dram["types"]).then_inc(tables, 16)
            act.dma_start(pos[:, :], dram["pos"]).then_inc(tables, 16)
            act.wait_ge(tables, 16 * 5)
            a = COLS["gate0"][0]
            act.activation(core.gates[:, :], core.cols[:, a:a + 4], ACT.Tanh).then_inc(tanh_done, 1)
            for g in range(GROUPS):
                act.wait_ge(turned, g + 1)
                act.activation(core.ctx_h[:, g * per * P:(g + 1) * per * P], core.psum[:, g, :], ACT.Copy).then_inc(ctx_high, 1)
            for c in range(n_chunks):
                act.wait_ge(landed[c], 16)
                act.activation(h[:, c * wc:(c + 1) * wc], raw_w[:, c * wc:(c + 1) * wc], ACT.Copy).then_inc(w_high, 1)

        @block.vector
        def _(dve):
            n = 0

            def chained(ins):
                nonlocal n
                n += 1
                ins.then_inc(steps, 1)
                dve.wait_ge(steps, n)

            dve.wait_ge(tables, 16 * 5)
            chained(dve.tensor_copy(posf[:, 0, :], pos[:, :]))
            chained(dve.tensor_scalar(posf[:, 1, :], posf[:, 0, :], 0.0, float(SEQ), ALU.is_lt, ALU.mult))
            chained(dve.tensor_tensor(posf[:, 2, :], posf[:, 1, :], posf[:, 0, :], ALU.add))
            chained(dve.tensor_scalar(posf[:, 0, :], posf[:, 2, :], 0.0, float(SEQ - 1), ALU.max, ALU.min))
            dve.tensor_scalar(onehot[:, :], posf[:, 0, :], table("tcol", SEQ), None, ALU.is_equal).then_inc(rope_done, 1)
            chained(dve.tensor_copy(typef[:, :, :], types[:, :, :]))
            chained(dve.tensor_scalar(typef[:, :, :], typef[:, :, :], 1.0, None, ALU.is_equal))
            chained(dve.tensor_tensor(core.vm[:, 0:TILES], typef[:, 0, :], typef[:, 1, :], ALU.mult))
            dve.tensor_scalar(core.not_vm[:, 0:TILES], core.vm[:, 0:TILES], -1.0, 1.0, ALU.mult, ALU.add).then_inc(sel_done, 1)
            for g in range(GROUPS):
                part = slice(g * per * P, (g + 1) * per * P)
                dve.wait_ge(ctx_high, g + 1)
                dve.tensor_tensor(core.ctx_l[:, part], core.psum[:, g, :], f32(core.ctx_h[:, part]), ALU.subtract).then_inc(kept, 1)
            dve.wait_ge(turned, GROUPS + 1)
            dve.tensor_copy(core.rope[:, :], core.psum[:, 4, 0:32]).then_inc(kept, 1)
            for c in range(1, n_chunks):
                part = slice(c * wc, (c + 1) * wc)
                dve.wait_ge(w_high, c + 1)
                dve.tensor_tensor(l[:, part], raw_w[:, part], f32(h[:, part]), ALU.subtract).then_inc(kept, 1)


def gated_attention(core, n, gate):
    nc, psum = core.nc, core.psum
    place = core.placer(n)
    xn = place("xn", [P, BT, 1, D])
    y = place("y", [P, DC, BLK])
    xh = place("xh", [P, DC, BLK], F32R)
    xl = place("xl", [P, DC, BLK], F32R)
    ch_b = place("ctx_block_h", [P, BLK], F32R)
    cl_b = place("ctx_block_l", [P, BLK], F32R)
    q = place("q", [P, PAIRS, BLK])
    keys = place("keys", [P, PAIRS, BB, 2, SEQ])
    vals = place("vals", [P, PAIRS, BB, 2, SEQ])
    pt = place("pt", [P, BT, PAIRS, P])
    oh = place("oh", [P, PAIRS, BLK], F32R)
    ol = place("ol", [P, PAIRS, BLK], F32R)
    ring_x = Ring(core, f"x{n}", (0,), [("xt", 1)])
    ring1 = Ring(core, f"a{n}", (4, 5),
                 [(f"{w}{i}", d) for h in (0, 2) for w, d in (("k", 2), ("q", 1)) for i in (h, h + 1)]
                 + [(f"v{k}{i}", 2) for k in range(BT) for i in range(2)])
    ring2 = Ring(core, f"o{n}", (6, 7),
                 [(f"{w}{k}{i}", 1) for k in range(BT) for w in ("pt", "av") for i in range(2)] + [("wo", 1)])
    wk, wv, wq, wo = (core.weight(n, w) for w in ("wk", "wv", "wq", "wo"))
    wq = [w.rearrange("p (c m) -> p c m", c=DC) for w in wq]
    wo_flat, wo = wo, [w.rearrange("p (c m) -> p c m", c=PAIRS) for w in wo]
    norm = Norm(core, n, "layer", "eps5", xn, ring_x, "xt")
    turned = Turned(core, n, norm, ring_x, ["xt"], y, xh, xl, f"g{n}", f"b{n}")
    soft = Softmax(core, n, place, ring2, ["pt01", "pt11"])
    following = NextWeights(core, n + 1)
    copied, out_high, cleared, wo_high, wo_split = (core.sem(f"{s}{n}") for s in ("copied", "out_high", "cleared", "wo_high", "wo_split"))

    with nc.Block() as block:
        @block.sync
        def _(sp):
            sweep(sp, lambda: following.load(sp, 0), lambda u: following.load(sp, u), lambda: None)

        @block.gpsimd
        def _(pool):
            def late(t):
                following.split(pool, t, cleared)
                soft.divide(pool, t, 0)
                soft.divide(pool, t, 1)

            def head():
                norm.invert(pool, 0)
                pool.memset(keys[:, :, :, :, :], 0.0).then_inc(cleared, 1)
                pool.memset(vals[:, :, :, :, :], 0.0).then_inc(cleared, 1)
                norm.invert(pool, 1)
                if n == 0:
                    raw = core.raw_w0[:, WCOLS[0] - W_ATT["wo"]:]
                    pool.wait_ge(core.wo_landed, 16)
                    pool.tensor_copy(wo_flat[0], raw).then_inc(wo_high, 1)
                    pool.wait_ge(wo_high, 1)
                    pool.tensor_tensor(wo_flat[1], raw, f32(wo_flat[0]), ALU.subtract).then_inc(wo_split, 1)
                late(0)

            def step(u):
                norm.invert(pool, u + 1)
                late(u)

            sweep(pool, head, step, lambda: None)

        @block.tensor
        def _(pe):
            def project_keys(t, i):
                job = f"k{i}"
                pe_wait_free(pe, ring1, job, t)
                for s in range(2):
                    m = slice((2 * i + s) * P, (2 * i + s + 1) * P)
                    done = three(pe, psum[:, ring1.bank(job), s * BLK:(s + 1) * BLK], [w[:, m] for w in wk],
                                 [core.ctx_h[:, block_tokens(t)], core.ctx_l[:, block_tokens(t)]], True, True)
                done.then_inc(ring1.full_of(job), 1)

            def project_queries(t, i):
                job = f"q{i}"
                if i == 0:
                    pe.wait_ge(turned.split_done, t + 1)
                pe_wait_free(pe, ring1, job, t)
                for s in range(2):
                    m = slice((2 * i + s) * P, (2 * i + s + 1) * P)
                    for c in range(DC):
                        done = three(pe, psum[:, ring1.bank(job), s * BLK:(s + 1) * BLK], [w[:, c, m] for w in wq],
                                     [xh[:, c, :], xl[:, c, :]], c == 0, c == DC - 1)
                done.then_inc(ring1.full_of(job), 1)

            def project_values(t, k):
                pe.wait_ge(copied, 2 * t + 2)
                for i in range(2):
                    job = f"v{k}{i}"
                    pe_wait_free(pe, ring1, job, t)
                    three(pe, psum[:, ring1.bank(job), :], [b[:, k * P:(k + 1) * P] for b in (ch_b, cl_b)],
                          [w[:, i * 512:(i + 1) * 512] for w in wv], True, True).then_inc(ring1.full_of(job), 1)

            def score(t, k):
                for job in ("k3", "q2", "q3"):
                    pe.wait_ge(ring1.empty_of(job), ring1.drained(job, t))
                if not first(t):
                    pe.wait_ge(core.begun, 1)
                    pe.wait_ge(soft.less_done, BT * t - BT + k + 1)
                for half in range(2):
                    bank = 2 * k + half
                    pe.matmul(psum[:, bank, :], core.batch_sel[:, :],
                              wide(core.mask_row[:, bass.ds(BT * t + k, 1), :].squeeze(1), 1, 8),
                              start=True, stop=False, skip_group_check=True)
                    for pair in range(4):
                        pr = 4 * half + pair
                        for b in range(2):
                            done = pe.matmul(psum[64 * b:64 * b + 64, bank, pair * P:(pair + 1) * P],
                                             q[:, pr, (2 * k + b) * SEQ:(2 * k + b + 1) * SEQ],
                                             keys[:, pr, 2 * k + b, :, :], start=False, stop=True, skip_group_check=True)
                done.then_inc(soft.scored, 1)

            def weigh(t, k):
                for i in range(2):
                    pe.wait_ge(ring1.empty_of(f"v{k}{i}"), ring1.drained(f"v{k}{i}", t))
                for i in range(2):
                    job = f"av{k}{i}"
                    pe.wait_ge(ring2.empty_of(f"pt{k}{i}"), ring2.drained(f"pt{k}{i}", t))
                    pe_wait_free(pe, ring2, job, t)
                    for s in range(4):
                        pair = 4 * i + s
                        for b in range(2):
                            done = pe.matmul(psum[:, ring2.bank(job), s * P + b * SEQ:s * P + (b + 1) * SEQ],
                                             vals[:, pair, 2 * k + b, :, :], pt[:, k, pair, b * SEQ:(b + 1) * SEQ],
                                             start=True, stop=True)
                    done.then_inc(ring2.full_of(job), 1)

            def project_out(t):
                for job in ("av10", "av11"):
                    pe.wait_ge(ring2.empty_of(job), ring2.drained(job, t))
                pe_wait_free(pe, ring2, "wo", t)
                for k in range(BT):
                    for c in range(PAIRS):
                        done = three(pe, psum[:, ring2.bank("wo"), k * D:(k + 1) * D],
                                     [o[:, c, k * P:(k + 1) * P] for o in (oh, ol)], [w[:, c, :] for w in wo],
                                     c == 0, c == PAIRS - 1)
                done.then_inc(ring2.full_of("wo"), 1)

            def turn_rows(t):
                if not first(t):
                    pe.wait_ge(soft.less_done, BT * t - BT + 1)
                turned.transpose(pe, t)

            def head():
                project_keys(0, 0)
                project_keys(0, 1)
                turn_rows(0)
                project_queries(0, 0)
                project_queries(0, 1)
                for p in (project_keys, project_queries):
                    for i in (2, 3):
                        p(0, i)
                pe.wait_ge(cleared, 2)
                score(0, 0)
                project_values(0, 0)
                score(0, 1)
                turn_rows(1)
                project_values(0, 1)

                if n == 0:
                    pe.wait_ge(wo_split, 1)

            def step(u):
                for h in (0, 2):
                    for p in (project_keys, project_queries):
                        for i in (h, h + 1):
                            p(u, i)
                turn_probabilities(pe, core, soft, ring2, u - 1, 0)
                score(u, 0)
                weigh(u - 1, 0)
                score(u, 1)
                turn_probabilities(pe, core, soft, ring2, u - 1, 1)
                project_values(u, 0)
                weigh(u - 1, 1)
                turn_rows(u + 1)
                project_values(u, 1)
                project_out(u - 1)

            def tail():
                for k in range(BT):
                    turn_probabilities(pe, core, soft, ring2, NB - 1, k)
                    weigh(NB - 1, k)
                project_out(NB - 1)

            sweep(pe, head, step, tail)

        def keep_keys(copy, s, t, i):
            job = f"k{i}"
            copy(job, ring1.filled(job, t), keys[64 * s:64 * s + 64, 2 * i:2 * i + 2, :, s, :],
                 psum[64 * s:64 * s + 64, ring1.bank(job), :].rearrange("p (a b j) -> p a b j", a=2, b=BB))

        def keep_values(copy, b, t, k):
            for i in range(2):
                job = f"v{k}{i}"
                src = psum[64 * b:64 * b + 64, ring1.bank(job), :].rearrange("p (a s d) -> p a s d", a=4, s=2)
                for s in range(2):
                    copy(job, ring1.filled(job, t) if s == 0 else None,
                         vals[64 * s:64 * s + 64, 4 * i:4 * i + 4, 2 * k + b, s, :], src[:, :, s, :], s == 1)

        @block.scalar
        def _(act):
            def copy(job, full, dst, src, last=True):
                if full is not None:
                    act.wait_ge(ring1.full_of(job), full)
                done = act.activation(dst, src, ACT.Copy)
                if last:
                    done.then_inc(ring1.empty_of(job), 1)

            def keep_queries(t, i):
                job = f"q{i}"
                act.wait_ge(ring1.full_of(job), ring1.filled(job, t))
                act.activation(q[:, 2 * i:2 * i + 2, :], psum[:, ring1.bank(job), :], ACT.Copy, scale=0.125)\
                   .then_inc(ring1.empty_of(job), 1)

            def keep_qk(t):
                for h in (0, 2):
                    for i in (h, h + 1):
                        keep_keys(copy, 0, t, i)
                    for i in (h, h + 1):
                        keep_queries(t, i)

            def keep_output(t, k, i):
                job = f"av{k}{i}"
                output_high(act, core, ring2, job, oh[:, 4 * i:4 * i + 4, k * P:(k + 1) * P],
                            psum[:, ring2.bank(job), :].rearrange("p (a t) -> p a t", a=4), out_high, t)

            def head():
                turned.scale(act, 0)
                act.wait_ge(cleared, 1)
                keep_qk(0)
                act.wait_ge(cleared, 2)
                keep_values(copy, 0, 0, 0)
                soft.exp(act, 0, 0)
                turned.scale(act, 1)
                keep_values(copy, 0, 0, 1)
                soft.exp(act, 0, 1)

            def step(u):
                keep_qk(u)
                keep_probabilities(act, core, ring2, pt, u - 1, 0)
                keep_output(u - 1, 0, 0)
                soft.exp(act, u, 0)
                keep_output(u - 1, 0, 1)
                keep_probabilities(act, core, ring2, pt, u - 1, 1)
                keep_values(copy, 0, u, 0)
                keep_output(u - 1, 1, 0)
                soft.exp(act, u, 1)
                keep_output(u - 1, 1, 1)
                keep_values(copy, 0, u, 1)
                turned.scale(act, u + 1)

            def tail():
                for k in range(BT):
                    keep_probabilities(act, core, ring2, pt, NB - 1, k)
                    keep_output(NB - 1, k, 0)
                    keep_output(NB - 1, k, 1)

            sweep(act, head, step, tail)

        @block.vector
        def _(dve):
            def copy(job, full, dst, src, last=True):
                if full is not None:
                    dve.wait_ge(ring1.full_of(job), full)
                done = dve.tensor_copy(dst, src)
                if last:
                    done.then_inc(ring1.empty_of(job), 1)

            def outputs(t, k):
                for i in range(2):
                    job = f"av{k}{i}"
                    high = oh[:, 4 * i:4 * i + 4, k * P:(k + 1) * P]
                    output_low(dve, core, ring2, job, ol[:, 4 * i:4 * i + 4, k * P:(k + 1) * P],
                               psum[:, ring2.bank(job), :].rearrange("p (a t) -> p a t", a=4), high, out_high,
                               4 * t + 2 * k + i + 1, t)

            def residual(t):
                dve.wait_ge(ring2.full_of("wo"), ring2.filled("wo", t))
                rows = core.x[:, block_tiles(t), :]
                dve.scalar_tensor_tensor(rows, psum[:, ring2.bank("wo"), :].rearrange("p (k d) -> p k d", k=BT), gate,
                                         rows, ALU.mult, ALU.add).then_inc(ring2.empty_of("wo"), 1)

            def head():
                norm.stats(dve, 0)
                norm.normalise(dve, 0)
                turned.split(dve, 0)
                dve.wait_ge(cleared, 1)
                for i in (0, 1):
                    keep_keys(copy, 1, 0, i)
                copy_context(dve, core, ring1, "v11", (ch_b, cl_b), copied, 0)
                if n == 0:
                    dve.wait_ge(core.x_rest, 16)
                norm.stats(dve, 1)
                for i in (2, 3):
                    keep_keys(copy, 1, 0, i)
                norm.normalise(dve, 1)
                dve.wait_ge(cleared, 2)
                soft.less_top(dve, 0, 0)
                keep_values(copy, 1, 0, 0)
                soft.less_top(dve, 0, 1)
                turned.split(dve, 1)
                keep_values(copy, 1, 0, 1)
                for k in range(BT):
                    soft.sums(dve, 0, k)

            def step(u):
                for i in (0, 1):
                    keep_keys(copy, 1, u, i)
                copy_context(dve, core, ring1, "v11", (ch_b, cl_b), copied, u)
                for i in (2, 3):
                    keep_keys(copy, 1, u, i)
                norm.stats(dve, u + 1)
                norm.normalise(dve, u + 1)
                soft.less_top(dve, u, 0)
                outputs(u - 1, 0)
                soft.sums(dve, u, 0)
                soft.less_top(dve, u, 1)
                keep_values(copy, 1, u, 0)
                outputs(u - 1, 1)
                keep_values(copy, 1, u, 1)
                turned.split(dve, u + 1)
                soft.sums(dve, u, 1)
                residual(u - 1)

            def tail():
                for k in range(BT):
                    outputs(NB - 1, k)
                residual(NB - 1)

            sweep(dve, head, step, tail)


def feed_forward(core, n, gate, last):
    nc, psum = core.nc, core.psum
    place = core.placer(n)
    xn = place("xn", [P, BT, 1, D])
    y = place("y", [P, DC, BLK])
    xh = place("xh", [P, DC, BLK], F32R)
    xl = place("xl", [P, DC, BLK], F32R)
    FT = FF // P
    hid = place("hid", [P, FT, BLK])
    hh = place("hid_h", [P, FT, BLK], F32R)
    hl = place("hid_l", [P, FT, BLK], F32R)
    ring = Ring(core, f"f{n}", tuple(range(6)), [("xt", 1)] + [(f"h{i}", 1) for i in range(4)] + [("w2", 1)])
    w1 = [w.rearrange("p (c m) -> p c m", c=DC) for w in core.weight(n, "w1")]
    w2 = [w.rearrange("p (c m) -> p c m", c=FT) for w in core.weight(n, "w2")]
    norm = Norm(core, n, "layer", "eps5", xn, ring, "xt")
    turned = Turned(core, n, norm, ring, ["xt"], y, xh, xl, f"g{n}", f"b{n}")
    following = NextWeights(core, n + 1)
    hid_high, hid_low, started, stored = (core.sem(f"{s}{n}") for s in ("hid_high", "hid_low", "started", "stored"))
    out = core.out.rearrange("(t p) d -> p t d", p=P)

    with nc.Block() as block:
        @block.sync
        def _(sp):
            def store(t):
                if last:
                    sp.wait_ge(ring.empty_of("w2"), ring.drained("w2", t))
                    sp.dma_start(out[:, block_tiles(t), :], core.x[:, block_tiles(t), :]).then_inc(stored, 16)

            def step(u):
                following.load(sp, u)
                store(u - 1)

            sweep(sp, lambda: following.load(sp, 0), step, lambda: store(NB - 1))
            if last:
                sp.wait_ge(stored, 16 * NB)

        @block.gpsimd
        def _(pool):
            pool.memset(core.ve[:, 0, :], 0.0).then_inc(started, 1)

            def head():
                norm.invert(pool, 0)
                norm.invert(pool, 1)
                following.split(pool, 0, started)

            def step(u):
                norm.invert(pool, u + 1)
                following.split(pool, u, started)

            sweep(pool, head, step, lambda: None)

        @block.tensor
        def _(pe):
            def up(t):
                pe.wait_ge(turned.split_done, t + 1)
                for i in range(4):
                    job = f"h{i}"
                    pe_wait_free(pe, ring, job, t)
                    for s in range(2):
                        m = slice((2 * i + s) * P, (2 * i + s + 1) * P)
                        for c in range(DC):
                            done = three(pe, psum[:, ring.bank(job), s * BLK:(s + 1) * BLK], [w[:, c, m] for w in w1],
                                         [xh[:, c, :], xl[:, c, :]], c == 0, c == DC - 1)
                    done.then_inc(ring.full_of(job), 1)

            def down(t):
                pe_wait_free(pe, ring, "w2", t)
                for k in range(BT):
                    for c in range(FT):
                        if k == 0 and c % 2 == 0:
                            pe.wait_ge(hid_low, 4 * t + c // 2 + 1)
                        done = three(pe, psum[:, ring.bank("w2"), k * D:(k + 1) * D],
                                     [g[:, c, k * P:(k + 1) * P] for g in (hh, hl)], [w[:, c, :] for w in w2],
                                     c == 0, c == FT - 1)
                done.then_inc(ring.full_of("w2"), 1)

            def head():
                turned.transpose(pe, 0)
                up(0)

            def step(u):
                turned.transpose(pe, u)
                down(u - 1)
                up(u)

            sweep(pe, head, step, lambda: down(NB - 1))

        @block.scalar
        def _(act):
            def step(t):
                turned.scale(act, t)
                for i in range(4):
                    job = f"h{i}"
                    act.wait_ge(ring.full_of(job), ring.filled(job, t))
                    if not first(t):
                        act.wait_ge(hid_low, 4 * t - 4 + i + 1)
                    act.activation(hid[:, 2 * i:2 * i + 2, :], psum[:, ring.bank(job), :], ACT.Gelu).then_inc(ring.empty_of(job), 1)

            sweep(act, lambda: step(0), step, lambda: None)

        @block.vector
        def _(dve):
            def split_hidden(t):
                for i in range(4):
                    job, part = f"h{i}", slice(2 * i, 2 * i + 2)
                    dve.wait_ge(ring.empty_of(job), ring.drained(job, t))
                    dve.tensor_copy(hh[:, part, :], hid[:, part, :]).then_inc(hid_high, 1)
                    dve.wait_ge(hid_high, 4 * t + i + 1)
                    dve.tensor_tensor(hl[:, part, :], hid[:, part, :], f32(hh[:, part, :]), ALU.subtract).then_inc(hid_low, 1)

            def residual(t):
                dve.wait_ge(ring.full_of("w2"), ring.filled("w2", t))
                rows = core.x[:, block_tiles(t), :]
                dve.scalar_tensor_tensor(rows, psum[:, ring.bank("w2"), :].rearrange("p (k d) -> p k d", k=BT), gate,
                                         rows, ALU.mult, ALU.add).then_inc(ring.empty_of("w2"), 1)

            def head():
                norm.stats(dve, 0)
                norm.normalise(dve, 0)
                turned.split(dve, 0)
                norm.stats(dve, 1)
                norm.normalise(dve, 1)
                split_hidden(0)

            def step(u):
                turned.split(dve, u)
                norm.stats(dve, u + 1)
                residual(u - 1)
                norm.normalise(dve, u + 1)
                split_hidden(u)

            sweep(dve, head, step, lambda: residual(NB - 1))


def memory_gate(core, n):
    nc, psum = core.nc, core.psum
    place = core.placer(n)
    rows = place("rows", [P, BT, D])
    y = place("y", [P, DC, BLK])
    xh, xl = (place(s, [P, DC, BLK], F32R) for s in ("xh", "xl"))
    ch_b, cl_b = (place(s, [P, BLK], F32R) for s in ("ctx_block_h", "ctx_block_l"))
    mem_t = place("mem_t", [P, DC, BLK])
    mem = place("mem", [P, BT, D])
    e = place("e", [P, BT, SEQ])
    top, total, inverse = (place(s, [P, BT]) for s in ("top", "total", "inverse"))
    prob = place("prob", [P, BT, 2, SEQ])
    pt = place("pt", [P, BT, P])
    ct_h, ct_l = (place(s, [P, DC, BLK], F32R) for s in ("ct_h", "ct_l"))
    tanh_z, gc, fused = (place(s, [P, BT, D]) for s in ("tanh_z", "gc", "fused"))
    ring1 = Ring(core, "m1_", (0, 1, 2, 3), [("xt", 1), ("mt", 1), ("mp", 1), ("sc", 1)])
    ring2 = Ring(core, "m2_", (4, 5, 6, 7), [("pt", 1), ("ct", 1), ("cx", 1), ("gt", 1)])
    wm = core.weight(n, "wm")
    wg = [w.rearrange("p (c m) -> p c m", c=4) for w in core.weight(n, "wg")]
    norm = Norm(core, n, "rms", "eps6", None, ring1, "xt")
    following = NextWeights(core, n + 1)
    sems = ("copied", "rows_ready", "x_high", "x_split", "top_done", "exp_done", "total_done", "inverse_done", "prob_ready",
            "ct_high", "fused_done", "zeroed")
    (copied, rows_ready, x_high, x_split, top_done, exp_done, total_done, inverse_done, prob_ready,
     ct_high, fused_done, zeroed) = (core.sem(f"m_{s}") for s in sems)
    tile = lambda k: slice(k * P, (k + 1) * P)
    banked = lambda ring, job, k=BT: psum[:, ring.bank(job), :].rearrange("p (k d) -> p k d", k=k)

    with nc.Block() as block:
        @block.sync
        def _(sp):
            sweep(sp, lambda: following.load(sp, 0), lambda u: following.load(sp, u), lambda: None)

        @block.gpsimd
        def _(pool):
            pool.memset(prob[:, :, :, :], 0.0).then_inc(zeroed, 1)

            def step(u):
                norm.invert(pool, u - 1)
                following.split(pool, u, zeroed)

            sweep(pool, lambda: following.split(pool, 0, zeroed), step, lambda: norm.invert(pool, NB - 1))

        @block.tensor
        def _(pe):
            def turn_rows(t):
                pe.wait_ge(rows_ready, t + 1)
                pe_wait_free(pe, ring1, "xt", t)
                for c in range(DC):
                    for k in range(BT):
                        done = pe.transpose(psum[:, ring1.bank("xt"), (c * BT + k) * P:(c * BT + k + 1) * P],
                                            rows[:, k, c * P:(c + 1) * P], core.col("ident"))
                done.then_inc(ring1.full_of("xt"), 1)

            def memory_turned(t):
                pe_wait_free(pe, ring1, "mt", t)
                for c in range(DC):
                    done = three(pe, psum[:, ring1.bank("mt"), c * BLK:(c + 1) * BLK], [w[:, tile(c)] for w in wm],
                                 [core.ctx_h[:, block_tokens(t)], core.ctx_l[:, block_tokens(t)]], True, True)
                done.then_inc(ring1.full_of("mt"), 1)

            def memory(t):
                pe.wait_ge(copied, 2 * t + 2)
                pe_wait_free(pe, ring1, "mp", t)
                for k in range(BT):
                    done = three(pe, psum[:, ring1.bank("mp"), k * D:(k + 1) * D], [b[:, tile(k)] for b in (ch_b, cl_b)], wm, True, True)
                done.then_inc(ring1.full_of("mp"), 1)

            def score(t):
                for job in ("xt", "mt"):
                    pe.wait_ge(ring1.empty_of(job), ring1.drained(job, t))
                pe_wait_free(pe, ring1, "sc", t)
                for k in range(BT):
                    for c in range(DC):
                        for b in range(2):
                            at = slice((2 * k + b) * SEQ, (2 * k + b + 1) * SEQ)
                            done = pe.matmul(psum[64 * b:64 * b + 64, ring1.bank("sc"), k * SEQ:(k + 1) * SEQ],
                                             y[:, c, at], mem_t[:, c, at], start=c == 0, stop=c == DC - 1)
                done.then_inc(ring1.full_of("sc"), 1)

            def turn_prob(t):
                pe.wait_ge(prob_ready, 2 * t + 2)
                pe_wait_free(pe, ring2, "pt", t)
                for k in range(BT):
                    done = pe.transpose(psum[:, ring2.bank("pt"), tile(k)], prob[:, k, :, :], core.col("ident"))
                done.then_inc(ring2.full_of("pt"), 1)

            def weigh(t):
                pe.wait_ge(ring2.empty_of("pt"), ring2.drained("pt", t))
                pe.wait_ge(ring1.empty_of("mp"), ring1.drained("mp", t))
                pe_wait_free(pe, ring2, "ct", t)
                for c in range(DC):
                    for k in range(BT):
                        done = pe.matmul(psum[:, ring2.bank("ct"), c * BLK + k * P:c * BLK + (k + 1) * P],
                                         mem[:, k, tile(c)], pt[:, k, :], start=True, stop=True)
                done.then_inc(ring2.full_of("ct"), 1)
                pe_wait_free(pe, ring2, "cx", t)
                for k in range(BT):
                    done = pe.matmul(psum[:, ring2.bank("cx"), k * D:(k + 1) * D], pt[:, k, :], mem[:, k, :], start=True, stop=True)
                done.then_inc(ring2.full_of("cx"), 1)

            def gate(t):
                pe.wait_ge(x_split, t + 1)
                pe_wait_free(pe, ring2, "gt", t)
                pe.wait_ge(ring2.empty_of("ct"), ring2.drained("ct", t))
                for k in range(BT):
                    for c in range(4):
                        parts = (xh, xl) if c < DC else (ct_h, ct_l)
                        three(pe, psum[:, ring2.bank("gt"), k * D:(k + 1) * D], [p[:, c % DC, tile(k)] for p in parts],
                              [w[:, c, :] for w in wg], c == 0, False)
                    done = pe.matmul(psum[:, ring2.bank("gt"), k * D:(k + 1) * D], core.col("ident"), core.col("bgate"),
                                     start=False, stop=True)
                done.then_inc(ring2.full_of("gt"), 1)

            def head():
                pe.wait_ge(zeroed, 1)
                turn_rows(0)
                memory_turned(0)
                memory(0)
                score(0)
                turn_rows(1)

            def step(u):
                turn_prob(u - 1)
                memory_turned(u)
                score(u)
                weigh(u - 1)
                memory(u)
                gate(u - 1)
                turn_rows(u + 1)

            def tail():
                turn_prob(NB - 1)
                weigh(NB - 1)
                gate(NB - 1)

            sweep(pe, head, step, tail)

        @block.scalar
        def _(act):
            def keep(ring, job, dst, src, t, done=None):
                act.wait_ge(ring.full_of(job), ring.filled(job, t))
                act.activation(dst, src, ACT.Copy).then_inc(ring.empty_of(job) if done is None else done, 1)

            def keep_y(t):
                if not first(t):
                    act.wait_ge(x_split, t)
                keep(ring1, "xt", y[:, :, :], banked(ring1, "xt"), t)

            def soft(t):
                act.wait_ge(ring1.empty_of("sc"), ring1.drained("sc", t))
                act.activation(e[:, :, :], e[:, :, :], ACT.Exp, scale=1.0 / 16).then_inc(exp_done, 1)

            def gate(t):
                if not first(t):
                    act.wait_ge(ring2.empty_of("cx"), ring2.drained("cx", t - 1))
                act.wait_ge(ring2.full_of("gt"), ring2.filled("gt", t))
                act.activation(tanh_z[:, :, :], banked(ring2, "gt"), ACT.Tanh, scale=0.5).then_inc(ring2.empty_of("gt"), 1)

            def head():
                keep_y(0)
                keep(ring1, "mt", mem_t[:, :, :], banked(ring1, "mt"), 0)
                keep(ring1, "mp", mem[:, :, :], banked(ring1, "mp"), 0)
                soft(0)
                keep_y(1)

            def step(u):
                keep(ring2, "pt", pt[:, :, :], psum[:, ring2.bank("pt"), 0:BLK].rearrange("p (k t) -> p k t", k=BT), u - 1)
                keep(ring1, "mt", mem_t[:, :, :], banked(ring1, "mt"), u)
                keep(ring2, "ct", ct_h[:, :, :], banked(ring2, "ct"), u - 1, ct_high)
                soft(u)
                keep(ring1, "mp", mem[:, :, :], banked(ring1, "mp"), u)
                gate(u - 1)
                keep_y(u + 1)

            def tail():
                keep(ring2, "pt", pt[:, :, :], psum[:, ring2.bank("pt"), 0:BLK].rearrange("p (k t) -> p k t", k=BT), NB - 1)
                keep(ring2, "ct", ct_h[:, :, :], banked(ring2, "ct"), NB - 1, ct_high)
                gate(NB - 1)

            sweep(act, head, step, tail)

        @block.vector
        def _(dve):
            def bring_rows(t):
                if not first(t):
                    dve.wait_ge(ring1.full_of("xt"), ring1.filled("xt", t - 1))
                dve.tensor_scalar(rows[:, :, :], core.x[:, block_tiles(t), :], 1.0, None, ALU.mult).then_inc(rows_ready, 1)

            def split_rows(t):
                dve.wait_ge(ring1.empty_of("xt"), ring1.drained("xt", t))
                if not first(t):
                    dve.wait_ge(ring2.full_of("gt"), ring2.filled("gt", t - 1))
                dve.tensor_copy(xh[:, :, :], y[:, :, :]).then_inc(x_high, 1)
                dve.wait_ge(x_high, t + 1)
                dve.tensor_tensor(xl[:, :, :], y[:, :, :], f32(xh[:, :, :]), ALU.subtract).then_inc(x_split, 1)

            def split_weighted(t):
                dve.wait_ge(ct_high, t + 1)
                dve.tensor_tensor(ct_l[:, :, :], banked(ring2, "ct"), f32(ct_h[:, :, :]), ALU.subtract).then_inc(ring2.empty_of("ct"), 1)

            def less_top(t):
                scores = psum[:, ring1.bank("sc"), 0:BT * SEQ].rearrange("p (k j) -> p k j", k=BT)
                dve.wait_ge(ring1.full_of("sc"), ring1.filled("sc", t))
                dve.tensor_reduce(top[:, :], scores, AX.X, ALU.max).then_inc(top_done, 1)
                dve.wait_ge(top_done, t + 1)
                dve.tensor_tensor(e[:, :, :], scores, wide(top[:, :], 2, SEQ), ALU.subtract).then_inc(ring1.empty_of("sc"), 1)

            def probabilities(t):
                dve.wait_ge(exp_done, t + 1)
                dve.tensor_reduce(total[:, :], e[:, :, :], AX.X, ALU.add).then_inc(total_done, 1)
                dve.wait_ge(total_done, t + 1)
                dve.reciprocal(inverse[:, :], total[:, :]).then_inc(inverse_done, 1)
                dve.wait_ge(inverse_done, t + 1)
                for b in range(2):
                    half = slice(64 * b, 64 * b + 64)
                    dve.tensor_tensor(prob[half, :, b, :], e[half, :, :], wide(inverse[half, :], 2, SEQ), ALU.mult).then_inc(prob_ready, 1)

            def fuse(t):
                dve.wait_ge(ring2.empty_of("gt"), ring2.drained("gt", t))
                dve.wait_ge(ring2.full_of("cx"), ring2.filled("cx", t))
                dve.scalar_tensor_tensor(gc[:, :, :], tanh_z[:, :, :], 1.0, banked(ring2, "cx"), ALU.add, ALU.mult)\
                   .then_inc(ring2.empty_of("cx"), 1)
                dve.wait_ge(ring2.empty_of("cx"), ring2.drained("cx", t))
                dve.scalar_tensor_tensor(fused[:, :, :], gc[:, :, :], 0.5, core.x[:, block_tiles(t), :], ALU.mult, ALU.add)\
                   .then_inc(fused_done, 1)
                dve.wait_ge(fused_done, 3 * t + 1)
                norm.stats(dve, t, fused)

            def scale_fused(t):
                dve.wait_ge(norm.rstd_done, t + 1)
                for k in range(BT):
                    dve.scalar_tensor_tensor(core.x[:, bass.ds(BT * t + k, 1), :].squeeze(1), fused[:, k, :], core.rstd[:, k:k + 1],
                                             core.col("normw"), ALU.mult, ALU.mult).then_inc(fused_done, 1)

            def head():
                bring_rows(0)
                copy_context(dve, core, ring1, "mp", (ch_b, cl_b), copied, 0)
                bring_rows(1)
                split_rows(0)
                dve.wait_ge(zeroed, 1)
                less_top(0)
                probabilities(0)
                copy_context(dve, core, ring1, "mp", (ch_b, cl_b), copied, 1)

            def step(u):
                split_weighted(u - 1)
                less_top(u)
                probabilities(u)
                bring_rows(u + 1)
                split_rows(u)
                fuse(u - 1)
                copy_context(dve, core, ring1, "mp", (ch_b, cl_b), copied, u + 1)
                scale_fused(u - 1)

            def tail():
                split_weighted(NB - 1)
                fuse(NB - 1)
                scale_fused(NB - 1)

            sweep(dve, head, step, tail)


def add_experts(dve, core, ring, jobs, mixed, t):
    for k, job in enumerate(jobs):
        row = core.x[:, bass.ds(BT * t + k, 1), :].squeeze(1)
        dve.wait_ge(ring.full_of(job), ring.filled(job, t))
        dve.scalar_tensor_tensor(row, psum_half(core, ring, job, 1), core.not_vm[:, bass.ds(BT * t + k, 1)], row,
                                 ALU.mult, ALU.add).then_inc(mixed, 1)
    for k, job in enumerate(jobs):
        row = core.x[:, bass.ds(BT * t + k, 1), :].squeeze(1)
        dve.wait_ge(mixed, BT * t + k + 1)
        dve.scalar_tensor_tensor(row, psum_half(core, ring, job, 0), core.vm[:, bass.ds(BT * t + k, 1)], row,
                                 ALU.mult, ALU.add).then_inc(ring.empty_of(job), 1)


def psum_half(core, ring, job, i):
    return core.psum[:, ring.bank(job), i * D:(i + 1) * D]


def self_attention(core, n):
    nc, psum = core.nc, core.psum
    place = core.placer(n)
    XC = 2 * DC
    HD = D // HEADS
    xn = place("xn", [P, BT, 2, D])
    y = place("y", [P, XC, BLK])
    xh, xl = (place(s, [P, XC, BLK], F32R) for s in ("xh", "xl"))
    by_cos, by_sin, turned_qk = (place(s, [P, BT, 2 * D]) for s in ("by_cos", "by_sin", "turned_qk"))
    q = place("q", [P, DC, BLK])
    keys = place("keys", [P, BB, DC, 8, SEQ])
    vals = place("vals", [P, BB, PAIRS, 2, HD])
    pt = place("pt", [P, BT, PAIRS, P])
    oh, ol = (place(s, [P, DC, BLK], F32R) for s in ("oh", "ol"))
    ring_x = Ring(core, "sx_", (0, 1), [("xv", 1), ("xo", 1)])
    ring1 = Ring(core, "s1_", (4, 5), [("qk0", 1), ("qk1", 1), ("rt0", 2), ("v0", 2), ("rt1", 2), ("v1", 2)])
    ring2 = Ring(core, "s2_", (6, 7),
                 [("pt00", 1), ("pt01", 1), ("av0", 1), ("pt10", 1), ("pt11", 1), ("av1", 1), ("d0", 1), ("d1", 1)])
    qkv = [w.rearrange("p (c m) -> p c m", c=XC) for w in core.weight(n, "qkv")]
    dense = [w.rearrange("p (c m) -> p c m", c=DC) for w in core.weight(n, "dense")]
    norm = Norm(core, n, "experts", "eps6", xn, ring_x, "xo")
    turned = Turned(core, n, norm, ring_x, ["xv", "xo"], y, xh, xl, f"g{n}", None)
    soft = Softmax(core, n, place, ring2, ["pt01", "pt11"])
    following = NextWeights(core, n + 1)
    rotated, out_high, cleared, mixed = (core.sem(f"{s}{n}") for s in ("rotated", "out_high", "cleared", "mixed"))
    tile = lambda k: slice(k * P, (k + 1) * P)

    with nc.Block() as block:
        @block.sync
        def _(sp):
            sweep(sp, lambda: following.load(sp, 0), lambda u: following.load(sp, u), lambda: None)

        @block.gpsimd
        def _(pool):
            def rotate(t):
                for k in range(BT):
                    pool.wait_ge(ring1.empty_of(f"qk{k}"), ring1.drained(f"qk{k}", t))
                    pool.tensor_tensor(turned_qk[:, k, :], by_cos[:, k, :], by_sin[:, k, :], ALU.add).then_inc(rotated, 1)

            def late(t):
                rotate(t)
                norm.invert(pool, t + 1)
                following.split(pool, t, cleared)
                soft.divide(pool, t, 0)
                soft.divide(pool, t, 1)

            def head():
                norm.invert(pool, 0)
                pool.memset(vals[:, :, :, :, :], 0.0).then_inc(cleared, 1)
                late(0)

            sweep(pool, head, late, lambda: None)

        @block.tensor
        def _(pe):
            def project_qk(t, k):
                job = f"qk{k}"
                if k == 0:
                    pe.wait_ge(turned.split_done, 2 * t + 2)
                pe_wait_free(pe, ring1, job, t)
                for c in range(XC):
                    done = three(pe, psum[:, ring1.bank(job), :], [p[:, c, tile(k)] for p in (xh, xl)],
                                 [w[:, c, 0:2 * D] for w in qkv], c == 0, c == XC - 1)
                done.then_inc(ring1.full_of(job), 1)

            def project_values(t, k):
                job = f"v{k}"
                pe_wait_free(pe, ring1, job, t)
                for c in range(XC):
                    done = three(pe, psum[:, ring1.bank(job), 0:D], [p[:, c, tile(k)] for p in (xh, xl)],
                                 [w[:, c, 2 * D:3 * D] for w in qkv], c == 0, c == XC - 1)
                done.then_inc(ring1.full_of(job), 1)

            def turn_qk(t, k):
                job = f"rt{k}"
                pe.wait_ge(rotated, BT * t + k + 1)
                pe_wait_free(pe, ring1, job, t)
                for i in range(4):
                    done = pe.transpose(psum[:, ring1.bank(job), tile(i)], turned_qk[:, k, tile(i)], core.col("ident"))
                done.then_inc(ring1.full_of(job), 1)

            def score(t, k):
                pe.wait_ge(ring1.empty_of(f"rt{k}"), ring1.drained(f"rt{k}", t))
                if not first(t):
                    pe.wait_ge(soft.less_done, BT * t - BT + k + 1)
                for c in range(DC):
                    bank = 2 * k + c
                    pe.matmul(psum[:, bank, :], core.ident_b[:, :], wide(core.causal[:, :], 1, 8), start=True, stop=False,
                              skip_group_check=True)
                    for b in range(2):
                        done = pe.matmul(psum[64 * b:64 * b + 64, bank, :], q[:, c, (2 * k + b) * SEQ:(2 * k + b + 1) * SEQ],
                                         keys[:, 2 * k + b, c, :, :], start=False, stop=True, skip_group_check=True)
                done.then_inc(soft.scored, 1)

            def weigh(t, k):
                job = f"av{k}"
                for i in range(2):
                    pe.wait_ge(ring2.empty_of(f"pt{k}{i}"), ring2.drained(f"pt{k}{i}", t))
                pe.wait_ge(ring1.empty_of(f"v{k}"), ring1.drained(f"v{k}", t))
                pe_wait_free(pe, ring2, job, t)
                pe.wait_ge(core.begun, 1)
                for c in range(DC):
                    for b in range(2):
                        for s in range(4):
                            done = pe.matmul(psum[32 * s:32 * s + 32, ring2.bank(job), c * P + b * SEQ:c * P + (b + 1) * SEQ],
                                             vals[:, 2 * k + b, 4 * c + s, :, :], pt[:, k, 4 * c + s, b * SEQ:(b + 1) * SEQ],
                                             start=True, stop=True)
                done.then_inc(ring2.full_of(job), 1)

            def project_out(t, k):
                job = f"d{k}"
                pe.wait_ge(ring2.empty_of(f"av{k}"), ring2.drained(f"av{k}", t))
                pe_wait_free(pe, ring2, job, t)
                for c in range(DC):
                    done = three(pe, psum[:, ring2.bank(job), :], [o[:, c, tile(k)] for o in (oh, ol)],
                                 [w[:, c, :] for w in dense], c == 0, c == DC - 1)
                done.then_inc(ring2.full_of(job), 1)

            def turn_rows(t):
                if not first(t):
                    pe.wait_ge(soft.less_done, BT * t - BT + 1)
                turned.transpose(pe, t)

            def head():
                turn_rows(0)
                for k in range(BT):
                    project_qk(0, k)
                turn_qk(0, 0)
                project_values(0, 0)
                turn_qk(0, 1)
                score(0, 0)
                project_values(0, 1)
                score(0, 1)
                turn_rows(1)

            def step(u):
                project_qk(u, 0)
                turn_probabilities(pe, core, soft, ring2, u - 1, 0)
                project_qk(u, 1)
                weigh(u - 1, 0)
                turn_probabilities(pe, core, soft, ring2, u - 1, 1)
                turn_qk(u, 0)
                project_values(u, 0)
                weigh(u - 1, 1)
                turn_qk(u, 1)
                score(u, 0)
                project_values(u, 1)
                score(u, 1)
                turn_rows(u + 1)
                for k in range(BT):
                    project_out(u - 1, k)

            def tail():
                for k in range(BT):
                    turn_probabilities(pe, core, soft, ring2, NB - 1, k)
                    weigh(NB - 1, k)
                for k in range(BT):
                    project_out(NB - 1, k)

            sweep(pe, head, step, tail)

        def keep_values(copy, b, t, k):
            job = f"v{k}"
            src = psum[64 * b:64 * b + 64, ring1.bank(job), 0:D].rearrange("p (a s d) -> p a s d", a=PAIRS, s=2)
            for s in range(2):
                copy(job, ring1.filled(job, t) if s == 0 else None, vals[64 * s:64 * s + 64, 2 * k + b, :, s, :],
                     src[:, :, s, :], s == 1)

        @block.scalar
        def _(act):
            def copy(job, full, dst, src, last=True):
                if full is not None:
                    act.wait_ge(ring1.full_of(job), full)
                done = act.activation(dst, src, ACT.Copy)
                if last:
                    done.then_inc(ring1.empty_of(job), 1)

            def keep_qk(t, k):
                job = f"rt{k}"
                act.wait_ge(ring1.full_of(job), ring1.filled(job, t))
                act.activation(q[:, :, tile(k)], psum[:, ring1.bank(job), 0:D].rearrange("p (c t) -> p c t", c=DC), ACT.Copy,
                               scale=0.25).then_inc(ring1.empty_of(job), 1)
                src = psum[:, ring1.bank(job), D:2 * D].rearrange("p (c b j) -> p c b j", c=DC, b=2)
                for h in range(8):
                    done = act.activation(keys[:, 2 * k:2 * k + 2, :, h, :].rearrange("p b c j -> p c b j"), src, ACT.Copy,
                                          scale=core.col("hm8")[:, h:h + 1])
                done.then_inc(ring1.empty_of(job), 1)

            def keep_output(t, k):
                output_high(act, core, ring2, f"av{k}", oh[:, :, tile(k)],
                            psum[:, ring2.bank(f"av{k}"), 0:D].rearrange("p (c t) -> p c t", c=DC), out_high, t)

            def head():
                turned.scale(act, 0)
                act.wait_ge(cleared, 1)
                for k in range(BT):
                    keep_qk(0, k)
                    keep_values(copy, 0, 0, k)
                soft.exp(act, 0, 0)
                turned.scale(act, 1)
                soft.exp(act, 0, 1)

            def step(u):
                keep_probabilities(act, core, ring2, pt, u - 1, 0)
                keep_output(u - 1, 0)
                keep_probabilities(act, core, ring2, pt, u - 1, 1)
                keep_qk(u, 0)
                keep_values(copy, 0, u, 0)
                keep_output(u - 1, 1)
                keep_qk(u, 1)
                keep_values(copy, 0, u, 1)
                soft.exp(act, u, 0)
                turned.scale(act, u + 1)
                soft.exp(act, u, 1)

            def tail():
                for k in range(BT):
                    keep_probabilities(act, core, ring2, pt, NB - 1, k)
                    keep_output(NB - 1, k)

            sweep(act, head, step, tail)

        @block.vector
        def _(dve):
            def copy(job, full, dst, src, last=True):
                if full is not None:
                    dve.wait_ge(ring1.full_of(job), full)
                done = dve.tensor_copy(dst, src)
                if last:
                    done.then_inc(ring1.empty_of(job), 1)

            def rotate(t, k):
                heads, half = 2 * HEADS, HD // 2
                job = f"qk{k}"
                src = psum[:, ring1.bank(job), :].rearrange("p (h d) -> p h d", h=heads)
                sin = by_sin[:, k, :].rearrange("p (h d) -> p h d", h=heads)
                dve.wait_ge(ring1.full_of(job), ring1.filled(job, t))
                if not first(t):
                    dve.wait_ge(rotated, BT * t - BT + k + 1)
                dve.tensor_tensor(by_cos[:, k, :].rearrange("p (h d) -> p h d", h=heads), src,
                                  wide(core.rope[:, 0:HD], 1, heads), ALU.mult)
                dve.tensor_tensor(sin[:, :, 0:half], src[:, :, half:HD], wide(core.rope[:, HD:HD + half], 1, heads), ALU.mult)
                dve.tensor_tensor(sin[:, :, half:HD], src[:, :, 0:half], wide(core.rope[:, HD + half:2 * HD], 1, heads), ALU.mult)\
                   .then_inc(ring1.empty_of(job), 1)

            def outputs(t, k):
                output_low(dve, core, ring2, f"av{k}", ol[:, :, tile(k)],
                           psum[:, ring2.bank(f"av{k}"), 0:D].rearrange("p (c t) -> p c t", c=DC), oh[:, :, tile(k)], out_high,
                           BT * t + k + 1, t)

            def head():
                norm.stats(dve, 0)
                norm.normalise(dve, 0)
                turned.split(dve, 0)
                for k in range(BT):
                    rotate(0, k)
                norm.stats(dve, 1)
                norm.normalise(dve, 1)
                dve.wait_ge(cleared, 1)
                keep_values(copy, 1, 0, 0)
                soft.less_top(dve, 0, 0)
                keep_values(copy, 1, 0, 1)
                soft.less_top(dve, 0, 1)
                turned.split(dve, 1)
                for k in range(BT):
                    soft.sums(dve, 0, k)

            def step(u):
                rotate(u, 0)
                norm.stats(dve, u + 1)
                outputs(u - 1, 0)
                rotate(u, 1)
                keep_values(copy, 1, u, 0)
                norm.normalise(dve, u + 1)
                outputs(u - 1, 1)
                soft.less_top(dve, u, 0)
                keep_values(copy, 1, u, 1)
                soft.less_top(dve, u, 1)
                turned.split(dve, u + 1)
                soft.sums(dve, u, 0)
                add_experts(dve, core, ring2, ("d0", "d1"), mixed, u - 1)
                soft.sums(dve, u, 1)

            def tail():
                for k in range(BT):
                    outputs(NB - 1, k)
                add_experts(dve, core, ring2, ("d0", "d1"), mixed, NB - 1)

            sweep(dve, head, step, tail)


def cross_attention(core, n):
    nc, psum = core.nc, core.psum
    place = core.placer(n)
    HD = P // HEADS
    SHARE = 10
    xn = place("xn", [P, BT, 1, D])
    y = place("y", [P, DC, BLK])
    xh, xl = (place(s, [P, DC, BLK], F32R) for s in ("xh", "xl"))
    ch_b, cl_b = (place(s, [P, BLK], F32R) for s in ("ctx_block_h", "ctx_block_l"))
    q = place("q", [P, BLK])
    keys = place("keys", [P, BB, HEADS, SEQ])
    vals = place("vals", [P, BB, 4, 96])
    pt = place("pt", [P, BT, PAIRS, P])
    oh, ol = (place(s, [P, BLK], F32R) for s in ("oh", "ol"))
    ring_x = Ring(core, "cx_", (0,), [("xt", 1)])
    ring1 = Ring(core, "c1_", (4, 5), [("q", 1), ("v0", 2), ("v1", 2)])
    ring_k = Ring(core, "ck_", (2, 3), [("k0", 1), ("k1", 1)])
    ring2 = Ring(core, "c2_", (6, 7),
                 [("pt00", 1), ("pt01", 1), ("av0", 1), ("pt10", 1), ("pt11", 1), ("av1", 1), ("cd", 1)])
    cq = [w.rearrange("p (c m) -> p c m", c=DC) for w in core.weight(n, "cq")]
    ckv, cd = core.weight(n, "ckv"), core.weight(n, "cd")
    norm = Norm(core, n, "rms", "eps6", xn, ring_x, "xt")
    turned = Turned(core, n, norm, ring_x, ["xt"], y, xh, xl, f"g{n}", None)
    soft = Softmax(core, n, place, ring2, ["pt01", "pt11"])
    following = NextWeights(core, n + 1)
    copied, out_high, cleared = (core.sem(f"{s}{n}") for s in ("copied", "out_high", "cleared"))
    tile = lambda k: slice(k * P, (k + 1) * P)

    with nc.Block() as block:
        @block.sync
        def _(sp):
            sweep(sp, lambda: following.load(sp, 0), lambda u: following.load(sp, u), lambda: None)

        @block.gpsimd
        def _(pool):
            def late(t):
                norm.invert(pool, t + 1)
                following.split(pool, t, cleared)
                soft.divide(pool, t, 0)
                soft.divide(pool, t, 1)

            def head():
                norm.invert(pool, 0)
                pool.memset(vals[:, :, :, :], 0.0).then_inc(cleared, 1)
                late(0)

            sweep(pool, head, late, lambda: None)

        @block.tensor
        def _(pe):
            def project_keys(t):
                if not first(t):
                    pe.wait_ge(core.begun, 1)
                    pe.wait_ge(soft.less_done, BT * t)
                for job in ("k0", "k1"):
                    three(pe, psum[:, ring_k.bank(job), 0:BLK], [w[:, 0:P] for w in ckv],
                          [core.ctx_h[:, block_tokens(t)], core.ctx_l[:, block_tokens(t)]], True, True).then_inc(ring_k.full_of(job), 1)

            def project_queries(t):
                pe_wait_free(pe, ring1, "q", t)
                pe.wait_ge(turned.split_done, t + 1)
                for c in range(DC):
                    done = three(pe, psum[:, ring1.bank("q"), 0:BLK], [w[:, c, :] for w in cq], [xh[:, c, :], xl[:, c, :]],
                                 c == 0, c == DC - 1)
                done.then_inc(ring1.full_of("q"), 1)

            def project_values(t, k):
                job = f"v{k}"
                pe.wait_ge(copied, 2 * t + 2)
                pe_wait_free(pe, ring1, job, t)
                three(pe, psum[:, ring1.bank(job), 0:P], [b[:, tile(k)] for b in (ch_b, cl_b)],
                      [w[:, P:2 * P] for w in ckv], True, True).then_inc(ring1.full_of(job), 1)

            def score(t, k):
                pe.wait_ge(ring1.empty_of("q"), ring1.drained("q", t))
                for job in ("k0", "k1"):
                    pe.wait_ge(ring_k.empty_of(job), ring_k.drained(job, t))
                if not first(t):
                    pe.wait_ge(soft.less_done, BT * t - BT + k + 1)
                for half in range(2):
                    for b in range(2):
                        done = pe.matmul(psum[64 * b:64 * b + 64, 2 * k + half, :], q[:, (2 * k + b) * SEQ:(2 * k + b + 1) * SEQ],
                                         keys[:, 2 * k + b, 8 * half:8 * half + 8, :], start=True, stop=True)
                done.then_inc(soft.scored, 1)

            def weigh(t, k):
                job = f"av{k}"
                for i in range(2):
                    pe.wait_ge(ring2.empty_of(f"pt{k}{i}"), ring2.drained(f"pt{k}{i}", t))
                pe.wait_ge(ring1.empty_of(f"v{k}"), ring1.drained(f"v{k}", t))
                pe_wait_free(pe, ring2, job, t)
                for b in range(2):
                    for e in range(2):
                        for s in range(4):
                            done = pe.matmul(psum[32 * s:32 * s + 32, ring2.bank(job), b * SEQ:(b + 1) * SEQ],
                                             vals[:, 2 * k + b, s, 32 * e:32 * e + 32], pt[:, k, 2 * s + e, b * SEQ:(b + 1) * SEQ],
                                             start=e == 0, stop=e == 1)
                done.then_inc(ring2.full_of(job), 1)

            def project_out(t):
                for k in range(BT):
                    pe.wait_ge(ring2.empty_of(f"av{k}"), ring2.drained(f"av{k}", t))
                pe_wait_free(pe, ring2, "cd", t)
                for k in range(BT):
                    done = three(pe, psum[:, ring2.bank("cd"), k * D:(k + 1) * D], [o[:, tile(k)] for o in (oh, ol)], cd, True, True)
                done.then_inc(ring2.full_of("cd"), 1)

            def turn_rows(t):
                if not first(t):
                    pe.wait_ge(soft.less_done, BT * t - BT + 1)
                turned.transpose(pe, t)

            def head():
                project_keys(0)
                turn_rows(0)
                project_queries(0)
                for k in range(BT):
                    project_values(0, k)
                    score(0, k)
                turn_rows(1)
                project_keys(1)

            def step(u):
                project_queries(u)
                score(u, 0)
                turn_probabilities(pe, core, soft, ring2, u - 1, 0)
                score(u, 1)
                weigh(u - 1, 0)
                project_values(u, 0)
                turn_probabilities(pe, core, soft, ring2, u - 1, 1)
                turn_rows(u + 1)
                project_values(u, 1)
                weigh(u - 1, 1)
                project_keys(u + 1)
                project_out(u - 1)

            def tail():
                for k in range(BT):
                    turn_probabilities(pe, core, soft, ring2, NB - 1, k)
                    weigh(NB - 1, k)
                project_out(NB - 1)

            sweep(pe, head, step, tail)

        def keep_values(copy, b, t, k):
            job = f"v{k}"
            src = psum[64 * b:64 * b + 64, ring1.bank(job), 0:P].rearrange("p (a e s d) -> p a e s d", a=4, e=2, s=2)
            for s in range(2):
                dst = vals[64 * s:64 * s + 64, 2 * k + b, :, :].rearrange("p a (e w) -> p a e w", e=2)
                copy(job, ring1.filled(job, t) if s == 0 else None, dst[:, :, :, s * HD:(s + 1) * HD], src[:, :, :, s, :], s == 1)

        @block.scalar
        def _(act):
            def copy(job, full, dst, src, last=True):
                if full is not None:
                    act.wait_ge(ring1.full_of(job), full)
                done = act.activation(dst, src, ACT.Copy)
                if last:
                    done.then_inc(ring1.empty_of(job), 1)

            def keep_queries(t):
                act.wait_ge(ring1.full_of("q"), ring1.filled("q", t))
                act.activation(q[:, :], psum[:, ring1.bank("q"), 0:BLK], ACT.Copy, scale=float(1 / np.sqrt(HD)))\
                   .then_inc(ring1.empty_of("q"), 1)

            def spread_keys(t):
                act.wait_ge(ring_k.full_of("k0"), ring_k.filled("k0", t))
                src = psum[:, ring_k.bank("k0"), 0:BLK].rearrange("p (b j) -> p b j", b=BB)
                for h in range(SHARE):
                    done = act.activation(keys[:, :, h, :], src, ACT.Copy, scale=core.col("hm16")[:, h:h + 1])
                done.then_inc(ring_k.empty_of("k0"), 1)

            def keep_output(t, k):
                output_high(act, core, ring2, f"av{k}", oh[:, tile(k)], psum[:, ring2.bank(f"av{k}"), 0:P], out_high, t)

            def head():
                turned.scale(act, 0)
                spread_keys(0)
                keep_queries(0)
                act.wait_ge(cleared, 1)
                for k in range(BT):
                    keep_values(copy, 0, 0, k)
                    soft.exp(act, 0, k)
                turned.scale(act, 1)
                spread_keys(1)

            def step(u):
                keep_queries(u)
                keep_probabilities(act, core, ring2, pt, u - 1, 0)
                soft.exp(act, u, 0)
                keep_output(u - 1, 0)
                keep_values(copy, 0, u, 0)
                keep_probabilities(act, core, ring2, pt, u - 1, 1)
                turned.scale(act, u + 1)
                keep_output(u - 1, 1)
                keep_values(copy, 0, u, 1)
                soft.exp(act, u, 1)
                spread_keys(u + 1)

            def tail():
                for k in range(BT):
                    keep_probabilities(act, core, ring2, pt, NB - 1, k)
                    keep_output(NB - 1, k)

            sweep(act, head, step, tail)

        @block.vector
        def _(dve):
            def copy(job, full, dst, src, last=True):
                if full is not None:
                    dve.wait_ge(ring1.full_of(job), full)
                done = dve.tensor_copy(dst, src)
                if last:
                    done.then_inc(ring1.empty_of(job), 1)

            def spread_keys(t):
                dve.wait_ge(ring_k.full_of("k1"), ring_k.filled("k1", t))
                src = psum[:, ring_k.bank("k1"), 0:BLK].rearrange("p (b j) -> p b j", b=BB)
                dve.tensor_tensor(keys[:, :, SHARE:, :], wide(src, 2, HEADS - SHARE), wide(wide(core.col("hm16")[:, SHARE:], 2, SEQ), 1, BB),
                                  ALU.mult).then_inc(ring_k.empty_of("k1"), 1)

            def outputs(t, k):
                output_low(dve, core, ring2, f"av{k}", ol[:, tile(k)], psum[:, ring2.bank(f"av{k}"), 0:P], oh[:, tile(k)], out_high,
                           BT * t + k + 1, t)

            def residual(t):
                rows = core.x[:, block_tiles(t), :]
                dve.wait_ge(ring2.full_of("cd"), ring2.filled("cd", t))
                dve.tensor_tensor(rows, psum[:, ring2.bank("cd"), :].rearrange("p (k d) -> p k d", k=BT), rows, ALU.add)\
                   .then_inc(ring2.empty_of("cd"), 1)

            def head():
                norm.stats(dve, 0)
                norm.normalise(dve, 0)
                spread_keys(0)
                turned.split(dve, 0)
                copy_context(dve, core, ring1, "v1", (ch_b, cl_b), copied, 0)
                norm.stats(dve, 1)
                norm.normalise(dve, 1)
                dve.wait_ge(cleared, 1)
                for k in range(BT):
                    keep_values(copy, 1, 0, k)
                    soft.less_top(dve, 0, k)
                turned.split(dve, 1)
                for k in range(BT):
                    soft.sums(dve, 0, k)
                spread_keys(1)

            def step(u):
                norm.stats(dve, u + 1)
                soft.less_top(dve, u, 0)
                copy_context(dve, core, ring1, "v1", (ch_b, cl_b), copied, u)
                norm.normalise(dve, u + 1)
                keep_values(copy, 1, u, 0)
                outputs(u - 1, 0)
                soft.less_top(dve, u, 1)
                soft.sums(dve, u, 0)
                outputs(u - 1, 1)
                keep_values(copy, 1, u, 1)
                turned.split(dve, u + 1)
                spread_keys(u + 1)
                residual(u - 1)
                soft.sums(dve, u, 1)

            def tail():
                for k in range(BT):
                    outputs(NB - 1, k)
                residual(NB - 1)

            sweep(dve, head, step, tail)


def experts(core, n):
    nc, psum = core.nc, core.psum
    place = core.placer(n)
    XC, NF = 2 * DC, len(F_SIZES)
    xn = place("xn", [P, BT, 2, D])
    y = place("y", [P, XC, BLK])
    xh, xl = (place(s, [P, XC, BLK], F32R) for s in ("xh", "xl"))
    silu = place("silu", [P, 2, BLK])
    hid = place("hid", [P, NF, BLK])
    hh, hl = (place(s, [P, NF, BLK], F32R) for s in ("hid_h", "hid_l"))
    ring_x = Ring(core, "ex_", (0, 1), [("xv", 1), ("xo", 1)])
    ring_g = Ring(core, "eg_", (2, 3, 4, 5), [(f"g{f}", 1) for f in range(NF)])
    ring_d = Ring(core, "ed_", (6, 7), [("d0", 1), ("d1", 1)])
    gu = [w.rearrange("p (c m) -> p c m", c=XC) for w in core.weight(n, "gu")]
    dn = [w.rearrange("p (c m) -> p c m", c=NF) for w in core.weight(n, "dn")]
    norm = Norm(core, n, "experts", "eps6", xn, ring_x, "xo")
    turned = Turned(core, n, norm, ring_x, ["xv", "xo"], y, xh, xl, f"g{n}", None)
    following = NextWeights(core, n + 1)
    silu_done, hid_high, hid_low, mixed, started = (core.sem(f"e_{s}") for s in ("silu", "hid_high", "hid_low", "mixed", "started"))
    tile = lambda k: slice(k * P, (k + 1) * P)

    with nc.Block() as block:
        @block.sync
        def _(sp):
            sweep(sp, lambda: following.load(sp, 0), lambda u: following.load(sp, u), lambda: None)

        @block.gpsimd
        def _(pool):
            pool.memset(core.spare[:, 2:3], 0.0).then_inc(started, 1)

            def late(t):
                norm.invert(pool, t + 1)
                for f, size in enumerate(F_SIZES):
                    pool.wait_ge(hid_high, NF * t + f + 1)
                    pool.tensor_tensor(hl[0:size, f, :], hid[0:size, f, :], f32(hh[0:size, f, :]), ALU.subtract).then_inc(hid_low, 1)
                following.split(pool, t, started)

            def head():
                norm.invert(pool, 0)
                late(0)

            sweep(pool, head, late, lambda: None)

        @block.tensor
        def _(pe):
            def up(t):
                pe.wait_ge(turned.split_done, 2 * t + 2)
                for f, (off, size) in enumerate(zip(F_OFF, F_SIZES)):
                    job = f"g{f}"
                    pe_wait_free(pe, ring_g, job, t)
                    for i in range(2):
                        m = slice(i * MOE_FF + off, i * MOE_FF + off + size)
                        for c in range(XC):
                            done = three(pe, psum[0:size, ring_g.bank(job), i * BLK:(i + 1) * BLK], [w[:, c, m] for w in gu],
                                         [xh[:, c, :], xl[:, c, :]], c == 0, c == XC - 1)
                    done.then_inc(ring_g.full_of(job), 1)

            def down(t):
                for k in range(BT):
                    job = f"d{k}"
                    pe_wait_free(pe, ring_d, job, t)
                    for f, size in enumerate(F_SIZES):
                        if k == 0:
                            pe.wait_ge(hid_low, NF * t + f + 1)
                        done = three(pe, psum[:, ring_d.bank(job), :], [g[0:size, f, tile(k)] for g in (hh, hl)],
                                     [w[0:size, f, :] for w in dn], f == 0, f == NF - 1)
                    done.then_inc(ring_d.full_of(job), 1)

            def head():
                turned.transpose(pe, 0)
                up(0)

            def step(u):
                turned.transpose(pe, u)
                down(u - 1)
                up(u)

            sweep(pe, head, step, lambda: down(NB - 1))

        @block.scalar
        def _(act):
            def step(t):
                turned.scale(act, t)
                for f, size in enumerate(F_SIZES):
                    job = f"g{f}"
                    act.wait_ge(ring_g.full_of(job), ring_g.filled(job, t))
                    if f >= 2:
                        act.wait_ge(ring_g.empty_of(f"g{f - 2}"), ring_g.drained(f"g{f - 2}", t))
                    elif not first(t):
                        act.wait_ge(ring_g.empty_of(f"g{NF - 2 + f}"), ring_g.drained(f"g{NF - 2 + f}", t - 1))
                    act.activation(silu[0:size, f % 2, :], psum[0:size, ring_g.bank(job), 0:BLK], ACT.Silu).then_inc(silu_done, 1)

            sweep(act, lambda: step(0), step, lambda: None)

        @block.vector
        def _(dve):
            def hidden(t):
                for f, size in enumerate(F_SIZES):
                    job = f"g{f}"
                    dve.wait_ge(silu_done, NF * t + f + 1)
                    if not first(t):
                        dve.wait_ge(hid_low, NF * t - NF + f + 1)
                    dve.tensor_tensor(hid[0:size, f, :], psum[0:size, ring_g.bank(job), BLK:2 * BLK], silu[0:size, f % 2, :], ALU.mult)\
                       .then_inc(ring_g.empty_of(job), 1)
                    dve.wait_ge(ring_g.empty_of(job), ring_g.drained(job, t))
                    dve.tensor_copy(hh[0:size, f, :], hid[0:size, f, :]).then_inc(hid_high, 1)

            def head():
                norm.stats(dve, 0)
                norm.normalise(dve, 0)
                turned.split(dve, 0)
                norm.stats(dve, 1)
                norm.normalise(dve, 1)
                hidden(0)

            def step(u):
                turned.split(dve, u)
                norm.stats(dve, u + 1)
                add_experts(dve, core, ring_d, ("d0", "d1"), mixed, u - 1)
                norm.normalise(dve, u + 1)
                hidden(u)

            sweep(dve, head, step, lambda: add_experts(dve, core, ring_d, ("d0", "d1"), mixed, NB - 1))


def build_program(nc, dram, out, phases=tuple(range(8))):
    with ExitStack() as ctx:
        core = Core(nc, ctx, dram, out)
        setup(core)
        steps = [
            lambda: gated_attention(core, 0, core.gates[:, 0:1]),
            lambda: feed_forward(core, 1, core.gates[:, 1:2], False),
            lambda: memory_gate(core, 2),
            lambda: self_attention(core, 3),
            lambda: cross_attention(core, 4),
            lambda: experts(core, 5),
            lambda: gated_attention(core, 6, core.gates[:, 2:3]),
            lambda: feed_forward(core, 7, core.gates[:, 3:4], True),
        ]
        core.end_phase()
        for n in phases:
            steps[n]()
            if n != phases[-1]:
                core.end_phase()


def _chunks(w, k):
    return w.reshape(k, P, -1).transpose(1, 0, 2).reshape(P, -1)


def _pack(a):
    cat = np.concatenate

    def att(p):
        wkv = a[f"{p}_Wkv"]
        return cat([wkv[:, :INNER], wkv[:, INNER:], _chunks(a[f"{p}_Wq"], DC), _chunks(a[f"{p}_Wo"], PAIRS)], 1)

    def ffn(p):
        return cat([_chunks(a[f"{p}_W1"], DC), _chunks(a[f"{p}_W2"], FF // P)], 1)

    m, e = "L1_xattn_", "L2_xattn_"
    qkv = cat([_chunks(a[e + "v_qkv"], DC), _chunks(a[e + "l_qkv"], DC)], 1)
    dense = _chunks(cat([a[e + "v_dense"], a[e + "l_dense"]], 1), DC)
    gu = cat([_chunks(cat([a[e + v + "gate"], a[e + v + "up"]], 1), DC) for v in ("v_", "l_")], 1)
    down = cat([a[e + "v_down"], a[e + "l_down"]], 1)
    dn = np.zeros((P, len(F_SIZES), 2 * D), np.float32)
    for f, (o, s) in enumerate(zip(F_OFF, F_SIZES)):
        dn[:s, f] = down[o:o + s]
    packed = [
        att("L0_xattn"), ffn("L0_xattn"),
        cat([a[m + "W_mem"].T, _chunks(a[m + "W_gate"].T, 4)], 1),
        cat([qkv, dense], 1),
        cat([_chunks(a[e + "cq_w"], DC), a[e + "ckv_w"], a[e + "cdense_w"]], 1),
        cat([gu, dn.reshape(P, -1)], 1),
        att("L3_xattn"), ffn("L3_xattn"),
    ]
    got = {f"w{n}": np.ascontiguousarray(w) for n, w in enumerate(packed)}

    cols = np.zeros((P, NCOLS), np.float32)

    def put(name, v):
        at, n = COLS[name]
        cols[:, at:at + n] = v

    for name, key in (("g0", "L0_xattn_ln_q_g"), ("b0", "L0_xattn_ln_q_b"), ("g1", "L0_xattn_ln_ff_g"), ("b1", "L0_xattn_ln_ff_b"),
                      ("g6", "L3_xattn_ln_q_g"), ("b6", "L3_xattn_ln_q_b"), ("g7", "L3_xattn_ln_ff_g"), ("b7", "L3_xattn_ln_ff_b"),
                      ("g3", e + "ln_in_w"), ("g4", e + "ln_post_cross_w"), ("g5", e + "ln_post_attn_w")):
        put(name, a[key].reshape(DC, P).T)
    for name, key in (("gate0", "L0_xattn_attn_gate"), ("gate1", "L0_xattn_ff_gate"),
                      ("gate6", "L3_xattn_attn_gate"), ("gate7", "L3_xattn_ff_gate")):
        put(name, a[key][None, :])
    part = np.arange(P)
    put("hm8", part[:, None] // 16 == np.arange(8)[None, :])
    put("hm16", part[:, None] // 8 == np.arange(16)[None, :])
    put("tcol", part[:, None])
    put("eps5", 1e-5), put("eps6", 1e-6), put("minus_half", -0.5)
    put("bgate", a[m + "b_gate"][None, :]), put("normw", a[m + "norm_w"][None, :])
    put("ident", np.eye(P))
    inv = (1.0 / 10000.0 ** (np.arange(0, 16, 2, dtype=np.float32) / 16)).astype(np.float32)
    ang = np.outer(np.arange(SEQ, dtype=np.float32), inv).astype(np.float32)
    at, _ = COLS["cossin"]
    cols[:SEQ, at:at + 32] = np.concatenate([np.cos(ang), np.cos(ang), -np.sin(ang), np.sin(ang)], 1)
    put("causal", np.where(np.arange(SEQ)[None, :] <= part[:, None] % SEQ, 0.0, MASKED))
    put("batch_sel", part[:, None] == part[None, :] // SEQ)
    got["cols"] = cols

    keep = a["mask_BxS2_bk0"].view(np.int32).reshape(TILES, 2, SEQ // 4)
    got["ctx_mask"] = np.ascontiguousarray(keep.transpose(1, 0, 2))
    types = a["mask_BxS_ik0"]
    after = np.concatenate([types[:, 1:], np.zeros((BATCH, 1), types.dtype)], 1)
    got["types"] = np.ascontiguousarray(np.stack([types.reshape(TILES, P).T, after.reshape(TILES, P).T], 1))
    got["pos"] = np.ascontiguousarray(np.broadcast_to(np.tile(a["pos_1xS"], (1, 2)), (SEQ, P)))
    got["x"] = a["x"].reshape(TOK, D)
    got["ctx"] = a["ctx_1024"].reshape(TOK, CTX)
    return got


def kernel(**inputs):
    import concourse.bacc as bacc
    from concourse.bass_utils import run_bass_kernel_spmd

    packed = _pack({k: np.asarray(v) for k, v in inputs.items()})
    nc = bacc.Bacc("TRN2", target_bir_lowering=False, num_devices=1)
    dram = {k: nc.dram_tensor(f"in_{k}", v.shape, mybir.dt.from_np(v.dtype), kind="ExternalInput").ap() for k, v in packed.items()}
    out = nc.dram_tensor("out", (TOK, D), F32, kind="ExternalOutput").ap()
    build_program(nc, dram, out)
    r = run_bass_kernel_spmd(nc, [{f"in_{k}": v for k, v in packed.items()}], core_ids=[0])
    return r.results[0]["out"].reshape(BATCH, SEQ, D)
```
